# Optimizing a Trainium2 kernel written in Bass

```python
import numpy as np
import jax
import jax.numpy as jnp

def _softmax(x, axis=-1):
    return jax.nn.softmax(x, axis=axis)

def _gelu(x):
    return jax.nn.gelu(x, approximate=True)

def _silu(x):
    return jax.nn.silu(x)

def _sigmoid(x):
    return jax.nn.sigmoid(x)

def _layernorm(x, axis=-1, eps=1e-05):
    m = jnp.mean(x, axis=axis, keepdims=True)
    v = jnp.var(x, axis=axis, keepdims=True)
    return (x - m) / jnp.sqrt(v + eps)

def _scatter_add(tgt, idx, src, axis=0):
    return tgt.at[idx].add(src)

def _segment_sum(src, seg, n):
    return jax.ops.segment_sum(src, seg, n)
kernel_name = 'mk_xattn_ffn_d2_seqx_r4_11686c'

def setup_inputs(seed: int=0):
    np.random.seed(seed)
    _w = jnp.asarray

    def _rec_inputs():
        import jax
        import jax.numpy as jnp
        _rk = jax.random.key(seed)
        x = -0.0002928 + 1 * jax.random.normal(jax.random.fold_in(_rk, 1), (16, 128, 256), jnp.float32)
        _lenS = 128 - jax.random.randint(jax.random.fold_in(_rk, 7), (16,), 0, max(1, 128 // 4) + 1, jnp.int32)
        _lenS2 = 128 - jax.random.randint(jax.random.fold_in(_rk, 8), (16,), 0, max(1, 128 // 4) + 1, jnp.int32)
        _ctx_1024P = jax.random.normal(jax.random.fold_in(_rk, 11), (16, 16, 256), jnp.float32)
        _ctx_1024c = jax.random.dirichlet(jax.random.fold_in(_rk, 511), 0.3 * jnp.ones((16,), jnp.float32), (16, 128))
        _ctx_1024t = jnp.einsum('bsk,bkd->bsd', _ctx_1024c, _ctx_1024P)
        _ctx_1024t = _ctx_1024t * jax.lax.rsqrt(jnp.mean(jnp.square(_ctx_1024t)) + 1e-12) * 0.953939
        ctx_1024 = -1.39393e-06 + 0.999914 * (_ctx_1024t + 0.3 * jax.random.normal(jax.random.fold_in(_rk, 611), (16, 128, 256), jnp.float32))
        _validS = jnp.arange(128)[None, :] < _lenS[:, None]
        _validS2 = jnp.arange(128)[None, :] < _lenS2[:, None]
        _causal = jnp.tril(jnp.ones((128, 128), dtype=bool))
        mask_BxS2_ff1 = jnp.where(jnp.ones((16, 128), dtype=bool), 1.0, 0.0).astype(jnp.float32)
        return (x, ctx_1024, mask_BxS2_ff1)
    x, ctx_1024, mask_BxS2_ff1 = _rec_inputs()

    def _L0_xattn_setup():
        import jax, jax.numpy as jnp
        import numpy as np
        import math
        EMBED_DIM = 256
        NUM_HEADS = 16
        HEAD_DIM = EMBED_DIM // NUM_HEADS
        ROPE_BASE = 10000.0

        def _rope_cache(S, D, dtype):
            inv_freq = 1.0 / ROPE_BASE ** (jnp.arange(0, D, 2, dtype=jnp.float32) / D)
            t = jnp.arange(S, dtype=jnp.float32)
            freqs = t[:, None] * inv_freq[None, :]
            return (jnp.cos(freqs).astype(dtype), jnp.sin(freqs).astype(dtype))

        def _apply_rope(x, cos, sin):
            x_even = x[..., 0::2]
            x_odd = x[..., 1::2]
            rot_even = x_even * cos - x_odd * sin
            rot_odd = x_odd * cos + x_even * sin
            return jnp.stack([rot_even, rot_odd], axis=-1).reshape(x.shape)
        key = jax.random.key(seed)
        ks = jax.random.split(key, 11)
        B, S, E = (2, 512, EMBED_DIM)
        s = 1.0 / math.sqrt(E)
        return {'query': jax.random.normal(ks[0], (B, S, E), jnp.float32), 'key': jax.random.normal(ks[1], (B, S, E), jnp.float32), 'value': jax.random.normal(ks[2], (B, S, E), jnp.float32), 'Wq': jax.random.normal(ks[3], (E, E), jnp.float32) * s, 'bq': jnp.zeros((E,), jnp.float32), 'Wk': jax.random.normal(ks[4], (E, E), jnp.float32) * s, 'bk': jnp.zeros((E,), jnp.float32), 'Wv': jax.random.normal(ks[5], (E, E), jnp.float32) * s, 'bv': jnp.zeros((E,), jnp.float32), 'Wo': jax.random.normal(ks[6], (E, E), jnp.float32) * s, 'bo': jnp.zeros((E,), jnp.float32)}
    _L0_xattn_all = _L0_xattn_setup()
    _L0_xattn_in = {k: v for k, v in _L0_xattn_all.items() if k in ('Wq', 'bq', 'Wk', 'bk', 'Wv', 'bv', 'Wo', 'bo')}
    del _L0_xattn_all

    def _L0_ffn_setup():
        import jax, jax.numpy as jnp
        import numpy as np
        B, S, D = (2, 512, 256)
        H = 512
        E = 8
        K = 2
        HS = 512 * 1
        SCALE = 1.0 / float(np.sqrt(D))
        key = jax.random.key(seed)
        ks = jax.random.split(key, 9)
        init = 0.02
        return {'x': jax.random.normal(ks[0], (B, S, D), dtype=jnp.float32), 'Wr': jax.random.normal(ks[1], (D, E), dtype=jnp.float32) * init, 'rb': jnp.zeros((E,), dtype=jnp.float32), 'W1': jax.random.normal(ks[2], (E, D, H), dtype=jnp.float32) * init, 'W2': jax.random.normal(ks[3], (E, H, D), dtype=jnp.float32) * init, 'W3': jax.random.normal(ks[4], (E, D, H), dtype=jnp.float32) * init, 'Ws1': jax.random.normal(ks[5], (D, HS), dtype=jnp.float32) * init, 'Ws2': jax.random.normal(ks[6], (HS, D), dtype=jnp.float32) * init, 'Ws3': jax.random.normal(ks[7], (D, HS), dtype=jnp.float32) * init}
    _L0_ffn_all = _L0_ffn_setup()
    _L0_ffn_in = {k: v for k, v in _L0_ffn_all.items() if k in ('Wr', 'rb', 'W1', 'W2', 'W3', 'Ws1', 'Ws2', 'Ws3')}
    del _L0_ffn_all

    def _L1_xattn_setup():
        import jax, jax.numpy as jnp
        import numpy as np
        EMBED_DIM = 256
        NUM_HEADS = 16
        HEAD_DIM = EMBED_DIM // NUM_HEADS
        BSZ, TGT, SRC = (4, 512, 512)

        def _split_heads(x, bsz, seqlen):
            return x.reshape(bsz, seqlen, NUM_HEADS, HEAD_DIM).transpose(0, 2, 1, 3)
        key = jax.random.key(seed)
        ks = jax.random.split(key, 8)
        s = EMBED_DIM ** (-0.5)
        return {'query': jax.random.normal(ks[0], (BSZ, TGT, EMBED_DIM), jnp.float32), 'key': jax.random.normal(ks[1], (BSZ, SRC, EMBED_DIM), jnp.float32), 'key_padding_mask': jnp.ones((BSZ, SRC), jnp.float32), 'Wq': jax.random.normal(ks[2], (EMBED_DIM, EMBED_DIM), jnp.float32) * s, 'bq': jnp.zeros((EMBED_DIM,), jnp.float32), 'Wk': jax.random.normal(ks[3], (EMBED_DIM, EMBED_DIM), jnp.float32) * s, 'bk': jnp.zeros((EMBED_DIM,), jnp.float32), 'Wv': jax.random.normal(ks[4], (EMBED_DIM, EMBED_DIM), jnp.float32) * s, 'bv': jnp.zeros((EMBED_DIM,), jnp.float32), 'Wo': jax.random.normal(ks[5], (EMBED_DIM, EMBED_DIM), jnp.float32) * s, 'bo': jnp.zeros((EMBED_DIM,), jnp.float32)}
    _L1_xattn_all = _L1_xattn_setup()
    _L1_xattn_in = {k: v for k, v in _L1_xattn_all.items() if k in ('Wq', 'bq', 'Wk', 'bk', 'Wv', 'bv', 'Wo', 'bo')}
    del _L1_xattn_all

    def _L1_ffn_setup():
        import jax, jax.numpy as jnp
        import numpy as np
        B, S, H = (1, 512, 256)
        E, K = (16, 4)
        G, TG = (4, 2)
        I_MOE = 128
        N_SH = 2
        SCALE = 2.5

        def _mlp(x, gw, uw, dw):
            return jax.nn.silu(x @ gw.T) * (x @ uw.T) @ dw.T

        def _route(x2d, router_weight, e_bias):
            T = x2d.shape[0]
            scores = jax.nn.sigmoid(x2d @ router_weight.T)
            sc = scores + e_bias[None, :]
            group_scores = jnp.sum(jax.lax.top_k(sc.reshape(T, G, E // G), 2)[0], axis=-1)
            _, gidx = jax.lax.top_k(group_scores, TG)
            gmask = jnp.zeros((T, G), sc.dtype).at[jnp.arange(T)[:, None], gidx].set(1.0)
            smask = jnp.repeat(gmask, E // G, axis=1)
            masked = jnp.where(smask > 0, sc, 0.0)
            _, tidx = jax.lax.top_k(masked, K)
            tw = jnp.take_along_axis(scores, tidx, axis=1)
            tw = tw / (jnp.sum(tw, axis=-1, keepdims=True) + 1e-20)
            tw = tw * SCALE
            return (tidx, tw)

        def _moe_forward(hidden_states, router_weight, e_bias, gate_w, up_w, down_w, sh_gate_w, sh_up_w, sh_down_w):
            orig_shape = hidden_states.shape
            x = hidden_states.reshape(-1, H)
            T = x.shape[0]
            tidx, tw = _route(x, router_weight, e_bias)
            g = jnp.einsum('th,eih->tei', x, gate_w)
            u = jnp.einsum('th,eih->tei', x, up_w)
            h = jax.nn.silu(g) * u
            yo = jnp.einsum('tei,ehi->teh', h, down_w)
            combine = jnp.zeros((T, E), tw.dtype).at[jnp.arange(T)[:, None], tidx].add(tw)
            routed = jnp.einsum('te,teh->th', combine, yo)
            shared = _mlp(hidden_states.reshape(-1, H), sh_gate_w, sh_up_w, sh_down_w)
            return (routed + shared).reshape(orig_shape)
        key = jax.random.key(seed)
        ks = jax.random.split(key, 9)
        s = 0.02
        return {'hidden_states': jax.random.normal(ks[0], (B, S, H), jnp.float32), 'router_weight': jax.random.normal(ks[1], (E, H), jnp.float32) * s, 'e_bias': jnp.zeros((E,), jnp.float32), 'gate_w': jax.random.normal(ks[2], (E, I_MOE, H), jnp.float32) * s, 'up_w': jax.random.normal(ks[3], (E, I_MOE, H), jnp.float32) * s, 'down_w': jax.random.normal(ks[4], (E, H, I_MOE), jnp.float32) * s, 'sh_gate_w': jax.random.normal(ks[5], (N_SH * I_MOE, H), jnp.float32) * s, 'sh_up_w': jax.random.normal(ks[6], (N_SH * I_MOE, H), jnp.float32) * s, 'sh_down_w': jax.random.normal(ks[7], (H, N_SH * I_MOE), jnp.float32) * s}
    _L1_ffn_all = _L1_ffn_setup()
    _L1_ffn_in = {k: v for k, v in _L1_ffn_all.items() if k in ('router_weight', 'e_bias', 'gate_w', 'up_w', 'down_w', 'sh_gate_w', 'sh_up_w', 'sh_down_w')}
    del _L1_ffn_all
    return {'x': x, 'ctx_1024': ctx_1024, 'mask_BxS2_ff1': mask_BxS2_ff1, 'L0_xattn_Wq': _L0_xattn_in['Wq'], 'L0_xattn_bq': _L0_xattn_in['bq'], 'L0_xattn_Wk': _L0_xattn_in['Wk'], 'L0_xattn_bk': _L0_xattn_in['bk'], 'L0_xattn_Wv': _L0_xattn_in['Wv'], 'L0_xattn_bv': _L0_xattn_in['bv'], 'L0_xattn_Wo': _L0_xattn_in['Wo'], 'L0_xattn_bo': _L0_xattn_in['bo'], 'L0_ffn_Wr': _L0_ffn_in['Wr'], 'L0_ffn_rb': _L0_ffn_in['rb'], 'L0_ffn_W1': _L0_ffn_in['W1'], 'L0_ffn_W2': _L0_ffn_in['W2'], 'L0_ffn_W3': _L0_ffn_in['W3'], 'L0_ffn_Ws1': _L0_ffn_in['Ws1'], 'L0_ffn_Ws2': _L0_ffn_in['Ws2'], 'L0_ffn_Ws3': _L0_ffn_in['Ws3'], 'L1_xattn_Wq': _L1_xattn_in['Wq'], 'L1_xattn_bq': _L1_xattn_in['bq'], 'L1_xattn_Wk': _L1_xattn_in['Wk'], 'L1_xattn_bk': _L1_xattn_in['bk'], 'L1_xattn_Wv': _L1_xattn_in['Wv'], 'L1_xattn_bv': _L1_xattn_in['bv'], 'L1_xattn_Wo': _L1_xattn_in['Wo'], 'L1_xattn_bo': _L1_xattn_in['bo'], 'L1_ffn_router_weight': _L1_ffn_in['router_weight'], 'L1_ffn_e_bias': _L1_ffn_in['e_bias'], 'L1_ffn_gate_w': _L1_ffn_in['gate_w'], 'L1_ffn_up_w': _L1_ffn_in['up_w'], 'L1_ffn_down_w': _L1_ffn_in['down_w'], 'L1_ffn_sh_gate_w': _L1_ffn_in['sh_gate_w'], 'L1_ffn_sh_up_w': _L1_ffn_in['sh_up_w'], 'L1_ffn_sh_down_w': _L1_ffn_in['sh_down_w']}

def reference(x, ctx_1024, mask_BxS2_ff1, L0_xattn_Wq, L0_xattn_bq, L0_xattn_Wk, L0_xattn_bk, L0_xattn_Wv, L0_xattn_bv, L0_xattn_Wo, L0_xattn_bo, L0_ffn_Wr, L0_ffn_rb, L0_ffn_W1, L0_ffn_W2, L0_ffn_W3, L0_ffn_Ws1, L0_ffn_Ws2, L0_ffn_Ws3, L1_xattn_Wq, L1_xattn_bq, L1_xattn_Wk, L1_xattn_bk, L1_xattn_Wv, L1_xattn_bv, L1_xattn_Wo, L1_xattn_bo, L1_ffn_router_weight, L1_ffn_e_bias, L1_ffn_gate_w, L1_ffn_up_w, L1_ffn_down_w, L1_ffn_sh_gate_w, L1_ffn_sh_up_w, L1_ffn_sh_down_w):
    import jax
    import jax.numpy as jnp

    def _L0_xattn_ref(query, key, value, Wq, bq, Wk, bk, Wv, bv, Wo, bo):
        import jax, jax.numpy as jnp
        import numpy as np
        import math
        EMBED_DIM = 256
        NUM_HEADS = 16
        HEAD_DIM = EMBED_DIM // NUM_HEADS
        ROPE_BASE = 10000.0

        def _rope_cache(S, D, dtype):
            inv_freq = 1.0 / ROPE_BASE ** (jnp.arange(0, D, 2, dtype=jnp.float32) / D)
            t = jnp.arange(S, dtype=jnp.float32)
            freqs = t[:, None] * inv_freq[None, :]
            return (jnp.cos(freqs).astype(dtype), jnp.sin(freqs).astype(dtype))

        def _apply_rope(x, cos, sin):
            x_even = x[..., 0::2]
            x_odd = x[..., 1::2]
            rot_even = x_even * cos - x_odd * sin
            rot_odd = x_odd * cos + x_even * sin
            return jnp.stack([rot_even, rot_odd], axis=-1).reshape(x.shape)
        B, S, E = query.shape
        H, D = (NUM_HEADS, HEAD_DIM)
        q = (query @ Wq.T + bq).reshape(B, S, H, D).transpose(0, 2, 1, 3)
        k = (key @ Wk.T + bk).reshape(B, S, H, D).transpose(0, 2, 1, 3)
        v = (value @ Wv.T + bv).reshape(B, S, H, D).transpose(0, 2, 1, 3)
        cos, sin = _rope_cache(S, D, q.dtype)
        q = _apply_rope(q, cos, sin)
        k = _apply_rope(k, cos, sin)
        scores = jnp.einsum('bhsd,bhtd->bhst', q, k) / math.sqrt(D)
        attn = jax.nn.softmax(scores, axis=-1)
        out = jnp.einsum('bhst,bhtd->bhsd', attn, v)
        out = out.transpose(0, 2, 1, 3).reshape(B, S, E)
        return out @ Wo.T + bo

    def _L0_ffn_ref(x, Wr, rb, W1, W2, W3, Ws1, Ws2, Ws3):
        import jax, jax.numpy as jnp
        import numpy as np
        B, S, D = (2, 512, 256)
        H = 512
        E = 8
        K = 2
        HS = 512 * 1
        SCALE = 1.0 / float(np.sqrt(D))
        logits = jnp.einsum('bsd,de->bse', x, Wr) * SCALE
        _, idx = jax.lax.top_k(logits + rb, K)
        gathered = jnp.take_along_axis(logits, idx, axis=-1)
        w = jax.nn.softmax(gathered, axis=-1)
        w_full = jnp.sum(jax.nn.one_hot(idx, E, dtype=x.dtype) * w[..., None], axis=-2)
        h = jnp.einsum('bsd,edh->bseh', x, W1) * jax.nn.silu(jnp.einsum('bsd,edh->bseh', x, W3))
        expert_out = jnp.einsum('bseh,ehd->bsed', h, W2)
        out = jnp.einsum('bsed,bse->bsd', expert_out, w_full)
        hs = jnp.einsum('bsd,dh->bsh', x, Ws1) * jax.nn.silu(jnp.einsum('bsd,dh->bsh', x, Ws3))
        out = out + jnp.einsum('bsh,hd->bsd', hs, Ws2)
        return out

    def _L1_xattn_ref(query, key, key_padding_mask, Wq, bq, Wk, bk, Wv, bv, Wo, bo):
        import jax, jax.numpy as jnp
        import numpy as np
        EMBED_DIM = 256
        NUM_HEADS = 16
        HEAD_DIM = EMBED_DIM // NUM_HEADS
        BSZ, TGT, SRC = (4, 512, 512)

        def _split_heads(x, bsz, seqlen):
            return x.reshape(bsz, seqlen, NUM_HEADS, HEAD_DIM).transpose(0, 2, 1, 3)
        bsz, src_len, embed_dim = key.shape
        tgt_len = query.shape[1]
        scaling = HEAD_DIM ** (-0.5)
        q = (query @ Wq.T + bq) * scaling
        k = key @ Wk.T + bk
        v = key @ Wv.T + bv
        qh = _split_heads(q, bsz, tgt_len)
        kh = _split_heads(k, bsz, src_len)
        vh = _split_heads(v, bsz, src_len)
        scores = jnp.einsum('bhtd,bhsd->bhts', qh, kh)
        inv = 1.0 - key_padding_mask.astype(scores.dtype)
        neg = jnp.finfo(scores.dtype).min
        add_mask = jnp.where(inv.astype(bool), neg, inv)
        scores = scores + add_mask[:, None, None, :]
        probs = jax.nn.softmax(scores, axis=-1)
        out = jnp.einsum('bhts,bhsd->bhtd', probs, vh)
        out = out.transpose(0, 2, 1, 3).reshape(bsz, tgt_len, embed_dim)
        return out @ Wo.T + bo

    def _L1_ffn_ref(hidden_states, router_weight, e_bias, gate_w, up_w, down_w, sh_gate_w, sh_up_w, sh_down_w):
        import jax, jax.numpy as jnp
        import numpy as np
        B, S, H = (1, 512, 256)
        E, K = (16, 4)
        G, TG = (4, 2)
        I_MOE = 128
        N_SH = 2
        SCALE = 2.5

        def _mlp(x, gw, uw, dw):
            return jax.nn.silu(x @ gw.T) * (x @ uw.T) @ dw.T

        def _route(x2d, router_weight, e_bias):
            T = x2d.shape[0]
            scores = jax.nn.sigmoid(x2d @ router_weight.T)
            sc = scores + e_bias[None, :]
            group_scores = jnp.sum(jax.lax.top_k(sc.reshape(T, G, E // G), 2)[0], axis=-1)
            _, gidx = jax.lax.top_k(group_scores, TG)
            gmask = jnp.zeros((T, G), sc.dtype).at[jnp.arange(T)[:, None], gidx].set(1.0)
            smask = jnp.repeat(gmask, E // G, axis=1)
            masked = jnp.where(smask > 0, sc, 0.0)
            _, tidx = jax.lax.top_k(masked, K)
            tw = jnp.take_along_axis(scores, tidx, axis=1)
            tw = tw / (jnp.sum(tw, axis=-1, keepdims=True) + 1e-20)
            tw = tw * SCALE
            return (tidx, tw)

        def _moe_forward(hidden_states, router_weight, e_bias, gate_w, up_w, down_w, sh_gate_w, sh_up_w, sh_down_w):
            orig_shape = hidden_states.shape
            x = hidden_states.reshape(-1, H)
            T = x.shape[0]
            tidx, tw = _route(x, router_weight, e_bias)
            g = jnp.einsum('th,eih->tei', x, gate_w)
            u = jnp.einsum('th,eih->tei', x, up_w)
            h = jax.nn.silu(g) * u
            yo = jnp.einsum('tei,ehi->teh', h, down_w)
            combine = jnp.zeros((T, E), tw.dtype).at[jnp.arange(T)[:, None], tidx].add(tw)
            routed = jnp.einsum('te,teh->th', combine, yo)
            shared = _mlp(hidden_states.reshape(-1, H), sh_gate_w, sh_up_w, sh_down_w)
            return (routed + shared).reshape(orig_shape)
        return _moe_forward(hidden_states, router_weight, e_bias, gate_w, up_w, down_w, sh_gate_w, sh_up_w, sh_down_w)
    x = x + _L0_xattn_ref(_layernorm(x, axis=-1), ctx_1024, ctx_1024, L0_xattn_Wq, L0_xattn_bq, L0_xattn_Wk, L0_xattn_bk, L0_xattn_Wv, L0_xattn_bv, L0_xattn_Wo, L0_xattn_bo)
    x = x + _L0_ffn_ref(_layernorm(x, axis=-1), L0_ffn_Wr, L0_ffn_rb, L0_ffn_W1, L0_ffn_W2, L0_ffn_W3, L0_ffn_Ws1, L0_ffn_Ws2, L0_ffn_Ws3)
    x = x + _L1_xattn_ref(_layernorm(x, axis=-1), ctx_1024, mask_BxS2_ff1, L1_xattn_Wq, L1_xattn_bq, L1_xattn_Wk, L1_xattn_bk, L1_xattn_Wv, L1_xattn_bv, L1_xattn_Wo, L1_xattn_bo)
    x = x + _L1_ffn_ref(_layernorm(x, axis=-1), L1_ffn_router_weight, L1_ffn_e_bias, L1_ffn_gate_w, L1_ffn_up_w, L1_ffn_down_w, L1_ffn_sh_gate_w, L1_ffn_sh_up_w, L1_ffn_sh_down_w)
    return x

_drawn_inputs = setup_inputs


def setup_inputs(seed=0):
    import zlib

    import numpy as np

    out = dict(_drawn_inputs(seed))
    spreads = {'L0_xattn_bq': (0.0, 0.485),
     'L0_xattn_bk': (0.0, 0.8),
     'L0_xattn_bv': (0.0, 0.1),
     'L0_xattn_bo': (0.0, 0.1),
     'L0_ffn_rb': (0.0, 0.524),
     'L1_xattn_bq': (0.0, 0.462),
     'L1_xattn_bk': (0.0, 0.8),
     'L1_xattn_bv': (0.0, 0.1),
     'L1_xattn_bo': (0.0, 0.1),
     'L1_ffn_e_bias': (0.0, 0.79)}
    factors = {'L0_ffn_Wr': 8.0,
     'L0_ffn_W1': 4.181,
     'L0_ffn_W2': 4.187,
     'L0_ffn_W3': 4.23,
     'L0_ffn_Ws1': 2.975,
     'L0_ffn_Ws2': 2.971,
     'L0_ffn_Ws3': 3.0,
     'L1_ffn_router_weight': 6.163,
     'L1_ffn_gate_w': 4.87,
     'L1_ffn_up_w': 4.839,
     'L1_ffn_down_w': 4.837,
     'L1_ffn_sh_gate_w': 4.371,
     'L1_ffn_sh_up_w': 4.289,
     'L1_ffn_sh_down_w': 4.293}
    for name, (base, spread) in spreads.items():
        noise = np.random.default_rng([zlib.crc32(name.encode()), seed]).standard_normal(out[name].shape)
        drawn = base * np.exp(spread * noise) if base else spread * noise
        out[name] = jnp.asarray(drawn.astype(out[name].dtype))
    for name, factor in factors.items():
        out[name] = (out[name] * factor).astype(out[name].dtype)
    return out
```

```python
from contextlib import ExitStack

import numpy as np

import concourse.bass as bass
from concourse import mybir

B, S, D = 16, 128, 256
HEADS, HD = 16, 16
P = 128
KT = D // P
BLK = 4
NBLK = B // BLK
TOK = B * S
N = BLK * S
GRP = 4
NG = HEADS // GRP
VW = 50
E0, E1 = 8, 16
TOP0, TOP1 = 2, 4
UNITS = 18
EPS = 1e-5
LOGIT_SCALE = 1.0 / 16.0
ROUTE_SCALE = 2.5
BIG = 3.3895313892515355e38


def program(nc, x, ctxT, maskrow, cosT, sinT, ident_in, aw, ab, arow, rw, rrow, fw, out):
    F32, F32R = mybir.dt.float32, mybir.dt.float32r
    F16, BF16 = mybir.dt.float16, mybir.dt.bfloat16
    ALU, ACT = mybir.AluOpType, mybir.ActivationFunctionType
    AX = mybir.AxisListType
    ds = bass.ds

    ctx = ExitStack()
    with ctx:
        def sb(stack, name, shape, dt):
            return stack.enter_context(nc.sbuf_tensor(name, shape, dt))

        def sem(name):
            return ctx.enter_context(nc.semaphore(name))

        xres = sb(ctx, "xres", [P, B, D], F32)
        xT_hi = sb(ctx, "xT_hi", [P, KT, TOK], F32R)
        xT_lo = sb(ctx, "xT_lo", [P, KT, TOK], F32R)
        ident = sb(ctx, "ident", [P, P], F32)
        xn = sb(ctx, "xn", [P, 2, BLK, D], F32)
        stats = sb(ctx, "stats", [P, BLK, 6], F32)
        meanvar = sb(ctx, "meanvar", [P, 2, BLK, 2], F32)
        std = sb(ctx, "std", [P, 2, BLK], F32)
        rstd = sb(ctx, "rstd", [P, 2, BLK], F32)
        eps_col = sb(ctx, "eps_col", [P, 1], F32)
        zero_col = sb(ctx, "zero_col", [P, 1], F32)
        cosS = sb(ctx, "cosS", [P, S], F32)
        sinS = sb(ctx, "sinS", [P, S], F32)
        ones_row = sb(ctx, "ones_row", [1, P], BF16)
        mask_f = xn[0:1].rearrange("p a b d -> p (a b d)")
        mask_b = sb(ctx, "mask_b", [1, B * S], BF16)
        bias_col = [sb(ctx, f"bias_col{l}", [P, 8], F32) for l in range(2)]
        bv_row = [sb(ctx, f"bv_row{l}", [P, D], F32) for l in range(2)]
        bo_row = [sb(ctx, f"bo_row{l}", [P, D], F32) for l in range(2)]
        NE, TOPS = [E0, E1], [TOP0, TOP1]
        route_w = [sb(ctx, f"route_w{l}", [P, KT, NE[l]], F32) for l in range(2)]
        route_wr = [sb(ctx, f"route_wr{l}", [P, KT, 2, NE[l]], F32R) for l in range(2)]
        route_b = [sb(ctx, f"route_b{l}", [P, NE[l]], F32) for l in range(2)]
        EW = E1 + 8
        logit = sb(ctx, "logit", [P, B, E1], F32)
        score = sb(ctx, "score", [P, B, EW], F32)
        taken = sb(ctx, "taken", [P, B, EW], F32)
        top8 = sb(ctx, "top8", [P, B, 8], F32)
        rt = [sb(ctx, f"rt{i}", [P, B, E1], F32) for i in range(2)]
        r1 = [sb(ctx, f"r1_{i}", [P, B, 4], F32) for i in range(4)]
        gate = sb(ctx, "gate", [P, UNITS, B], F32)

        at = ExitStack()
        ctx_raw = sb(at, "ctx_raw", [P, KT, N], F32)
        ctx_hi = sb(at, "ctx_hi", [P, KT, N], F32R)
        ctx_lo = sb(at, "ctx_lo", [P, KT, N], F32R)
        aw_raw = sb(at, "aw_raw", [P, 2, KT * D], F32)
        aw_hi = sb(at, "aw_hi", [P, 6, KT, D], F32R)
        aw_lo = sb(at, "aw_lo", [P, 6, KT, D], F32R)
        rope_b = sb(at, "rope_b", [P, 2, N], F32)
        qk = sb(at, "qk", [P, 2, N], F32)
        qstack = sb(at, "qstack", [P, KT, 2, N], F32R)
        k_parts = sb(at, "k_parts", [P, 2, KT, N], F32R)
        kexp = [sb(at, f"kexp{i}", [P, 2, NG, GRP, S], F32R) for i in range(2)]
        v32 = sb(at, "v32", [P, 2, 2, D], F32)
        v_res = sb(at, "v_res", [P, 2, 2, D], F32)
        v_parts = sb(at, "v_parts", [P, BLK, HEADS, VW], BF16)
        prob = sb(at, "prob", [P, 2, NG, N], F32)
        probT_hi = sb(at, "probT_hi", [P, 2, N], F16)
        probT_lo = sb(at, "probT_lo", [P, 2, N], F16)
        smax = sb(at, "smax", [P, 2, HEADS], F32)
        rden = sb(at, "rden", [P, 2, HEADS], F32)
        o_sb = v_res[:].rearrange("p a b d -> p (a b) d")
        oT_hi, oT_lo = qstack[:, 0], qstack[:, 1]
        at.close()
        ft = ExitStack()
        w_raw = sb(ft, "w_raw", [P, 2, 1536], F32)
        w_hi = [sb(ft, f"w_hi{i}", [P, 1536], F32R) for i in range(2)]
        w_lo = [sb(ft, f"w_lo{i}", [P, 1536], F32R) for i in range(2)]
        act_sb = sb(ft, "act_sb", [P, 2, N], F32)
        hid = sb(ft, "hid", [P, 2, N], F32)
        hid_hi = sb(ft, "hid_hi", [P, 2, 2, N], F32R)
        hid_lo = sb(ft, "hid_lo", [P, 2, 2, N], F32R)
        ft.close()

        bank = [ctx.enter_context(nc.psum_tensor(f"bank{i}", [P, 512], F32)) for i in range(8)]

        s_in = sem("s_in")
        s_x = sem("s_x")
        s_store = sem("s_store")
        s_set = sem("s_set")
        s_vset = sem("s_vset")
        s_wsplit = [sem(f"s_route_split{l}") for l in range(2)]

        def stage_sems(names, l):
            return {n: sem(f"{n}_{l}") for n in names}

        LN = [stage_sems(["ln_stat", "ln_var", "ln_std", "ln_rstd", "ln_xn", "ln_T", "ln_hi", "ln_lo"], i) for i in range(4)]
        AT = [stage_sems(["aw_in0", "aw_in1", "kdma0", "kdma1", "aw_hi", "aw_lo", "ctx_in", "ctx_hi", "ctx_lo", "proj", "rope", "qk", "qhi", "qlo",
                          "vps", "v32", "vhi", "vres", "vmid", "vlo", "kzero", "score", "max", "sub", "exp",
                          "pT", "phi", "plo", "pv", "rden", "o", "oT", "ohi", "olo", "wo", "xadd", "xbo"], l)
              for l in range(2)]
        FF = [stage_sems(["w_in0", "w_in1", "w_hi", "w_lo", "up", "act", "hid", "hhi", "hlo", "y", "acc",
                          "rlog", "rcopy", "rsum", "rfun_in", "rfun", "route"], l) for l in range(2)]

        NW = [6, 4]
        JT = [2, 1]
        V_W, O_W = [4, 2], [5, 3]
        UNIT_W = [[(0, 1), (0, 1), (2, 3), (2, 3)], [(0,), (0,), (1,), (1,)]]
        HALF = UNITS // 2
        STEPS = 2 * NBLK

        def step_no(it, ls):
            return it * STEPS + ls

        def tile_no(it, ls, j, J):
            return it * (STEPS * J) + (ls * J + j)

        block = ctx.enter_context(nc.Block())

        @block.sync
        def _(sp):
            sp.dma_start(xres[:], x.rearrange("b s d -> s b d")).then_inc(s_x, 16)
            sp.dma_start(ident[:], ident_in).then_inc(s_in, 16)
            sp.dma_start(cosS[:], cosT).then_inc(s_in, 16)
            sp.dma_start(sinS[:], sinT).then_inc(s_in, 16)
            sp.dma_start(mask_f, maskrow).then_inc(s_in, 16)
            for l in range(2):
                sp.dma_start(bias_col[l][:], ab[l]).then_inc(s_in, 16)
                sp.dma_start(bv_row[l][:], arow[l][0:1, :].to_broadcast([P, D])).then_inc(s_in, 16)
                sp.dma_start(bo_row[l][:], arow[l][1:2, :].to_broadcast([P, D])).then_inc(s_in, 16)
                sp.dma_start(route_w[l][:], rw[l]).then_inc(s_in, 16)
                sp.dma_start(route_b[l][:], rrow[l].to_broadcast([P, NE[l]])).then_inc(s_in, 16)
            for l in range(2):
                a, f, J = AT[l], FF[l], JT[l]
                if l > 0:
                    sp.wait_ge(FF[l - 1]["acc"], UNITS * NBLK * BLK)
                for w in range(NW[l]):
                    if w >= 2:
                        sp.wait_ge(a["aw_lo"], w - 1)
                    sp.dma_start(aw_raw[:, w % 2, :], aw[l][:, w, :]).then_inc(a[f"aw_in{w % 2}"], 16)
                with sp.Fori(0, NBLK) as n:
                    sp.dma_start(ctx_raw[:], ctxT[:, :, ds(n * N, N)]).then_inc(a["ctx_in"], 16)
                    sp.wait_ge(a["kzero"], 2)
                    sp.wait_ge(a["qlo"], n * 6 + 6)
                    for b in range(BLK):
                        if b >= 2:
                            sp.wait_ge(a["score"], n * (BLK * NG) + (b - 1) * NG)
                        for half in range(2):
                            for g2 in range(2):
                                for j in range(GRP):
                                    src = k_parts[64 * g2 + HD * j:64 * g2 + HD * (j + 1), :, :, b * S:(b + 1) * S]
                                    dst = kexp[b % 2][64 * half + HD * j:64 * half + HD * (j + 1), :, g2::2, j, :]
                                    sp.dma_start(dst.bitcast(F32), src.bitcast(F32)).then_inc(a[f"kdma{b % 2}"], 16)
                sp.wait_ge(a["xadd"], 2 * NBLK)
                for par in range(2):
                    sp.dma_start(w_raw[:, par, 0:768 * J], fw[l][par, :, :]).then_inc(f[f"w_in{par}"], 16)
                with sp.Fori(1, HALF) as it:
                    for par in range(2):
                        sp.wait_ge(f["w_lo"], it * 2 + par - 1)
                        src = fw[l][ds(it * 2 + par, 1), :, :].rearrange("u p c -> p (u c)")
                        sp.dma_start(w_raw[:, par, 0:768 * J], src).then_inc(f[f"w_in{par}"], 16)
            sp.wait_ge(FF[1]["acc"], UNITS * NBLK * BLK)
            sp.dma_start(out.rearrange("b s d -> s b d"), xres[:]).then_inc(s_store, 16)
            sp.wait_ge(s_store, 16)

        @block.gpsimd
        def _(pool):
            def add_bias(m, bo, a):
                for n in range(NBLK):
                    pool.wait_ge(m["ln_xn"], 4 * n + 4)
                    rows = xres[:, BLK * n:BLK * (n + 1), :]
                    nc.gpsimd.tensor_tensor(rows, rows, bo[:].unsqueeze(1).to_broadcast([P, BLK, D]),
                                            ALU.add).then_inc(a["xbo"], 1)

            def split_unit(f, it, par, W):
                pool.wait_ge(f[f"w_in{par}"], it * 16 + 16)
                raw = w_raw[:, par, 0:W]
                nc.gpsimd.tensor_tensor(w_hi[par][:, 0:W], raw, zero_col[:].to_broadcast([P, W]),
                                        ALU.subtract).then_inc(f["w_hi"], 1)
                pool.wait_ge(f["w_hi"], it * 2 + par + 1)
                nc.gpsimd.tensor_tensor(w_lo[par][:, 0:W], w_raw[:, par, 0:W],
                                        w_hi[par][:, 0:W].bitcast(F32), ALU.subtract).then_inc(f["w_lo"], 1)

            nc.gpsimd.memset(ones_row[:], 1.0).then_inc(s_set, 1)
            nc.gpsimd.memset(eps_col[:], EPS).then_inc(s_set, 1)
            nc.gpsimd.memset(zero_col[:], 0.0).then_inc(s_set, 1)
            pool.wait_ge(s_set, 3)
            pool.wait_ge(s_in, 16 * 14)
            for l in range(2):
                nc.gpsimd.tensor_copy(route_wr[l][:, :, 0, :], route_w[l][:]).then_inc(s_wsplit[l], 1)
                pool.wait_ge(s_wsplit[l], 1)
                nc.gpsimd.tensor_tensor(route_wr[l][:, :, 1, :], route_w[l][:],
                                        route_wr[l][:, :, 0, :].bitcast(F32), ALU.subtract).then_inc(s_wsplit[l], 1)
            for l in range(2):
                a, f = AT[l], FF[l]
                if l > 0:
                    pool.wait_ge(FF[l - 1]["acc"], UNITS * NBLK * BLK)
                for i in range(2):
                    nc.gpsimd.memset(kexp[i][:].bitcast(F32), 0.0).then_inc(a["kzero"], 1)
                nc.gpsimd.memset(v_parts[:, :, :, HD:HD + 2], 1.0).then_inc(a["vmid"], 1)
                add_bias(LN[2 * l], bo_row[l], a)
                with pool.Fori(0, NBLK) as n:
                    for h in range(2):
                        parts = v_parts[:, 2 * h:2 * h + 2].rearrange("p b h w -> p (b h) w")
                        full = v32[:, h].rearrange("p b (h d) -> p (b h) d", h=HEADS)
                        rest = v_res[:, h].rearrange("p b (h d) -> p (b h) d", h=HEADS)
                        pool.wait_ge(a["vhi"], n * 2 + (h + 1))
                        nc.gpsimd.tensor_tensor(rest, full, parts[:, :, 0:16], ALU.subtract).then_inc(a["vres"], 1)
                        pool.wait_ge(a["vres"], n * 2 + (h + 1))
                        nc.gpsimd.tensor_tensor(parts[:, :, 18:34], rest, zero_col[:].unsqueeze(2).to_broadcast([P, 2 * HEADS, HD]),
                                                ALU.subtract).then_inc(a["vmid"], 1)
                        pool.wait_ge(a["vmid"], n * 2 + (h + 2))
                        nc.gpsimd.tensor_tensor(parts[:, :, 34:50], rest, parts[:, :, 18:34],
                                                ALU.subtract).then_inc(a["vlo"], 1)
                pool.wait_ge(a["xadd"], 2 * NBLK)
                for par in range(2):
                    split_unit(f, 0, par, 768 * JT[l])
                with pool.Fori(1, HALF) as it:
                    for par in range(2):
                        pool.wait_ge(f["y"], (it * 2 + par - 1) * (2 * NBLK))
                        split_unit(f, it, par, 768 * JT[l])

        @block.scalar
        def _(act):
            def ln_act(m):
                for n in range(NBLK + 1):
                    if n < NBLK:
                        act.wait_ge(m["ln_var"], 4 * n + 4)
                        nc.scalar.activation(std[:, n % 2, :], meanvar[:, n % 2, :, 1], ACT.Sqrt,
                                             bias=eps_col[:]).then_inc(m["ln_std"], 1)
                    for k in range(KT if n else 0):
                        act.wait_ge(m["ln_T"], 2 * n + k - 1)
                        nc.scalar.activation(xT_hi[:, k, N * (n - 1):N * n], bank[2 * ((n - 1) % 2) + k][:],
                                             ACT.Copy).then_inc(m["ln_hi"], 1)

            def experts(f, J, it, first):
                for ls in range(STEPS):
                    for j in range(J):
                        t = tile_no(it, ls, j, J)
                        act.wait_ge(f["up"], t + 1)
                        nc.scalar.activation(act_sb[:, (ls * J + j) % 2, :], bank[2 * ((ls * J + j) % 2) + 1][:],
                                             ACT.Silu).then_inc(f["act"], 1)
                        act.wait_ge(f["hid"], t + 1)
                        if not (first and ls < 2):
                            act.wait_ge(f["y"], (step_no(it, ls) - 1) * 2)
                        nc.scalar.activation(hid_hi[:, ls % 2, j, :], hid[:, (ls * J + j) % 2, :],
                                             ACT.Copy).then_inc(f["hhi"], 1)

            act.wait_ge(s_set, 2)
            for l in range(2):
                a, f, J = AT[l], FF[l], JT[l]
                for w in range(NW[l]):
                    act.wait_ge(a[f"aw_in{w % 2}"], 16 * (w // 2 + 1))
                    nc.scalar.activation(aw_hi[:, w].rearrange("p k d -> p (k d)"), aw_raw[:, w % 2, :],
                                         ACT.Copy).then_inc(a["aw_hi"], 1)
                ln_act(LN[2 * l])
                with act.Fori(0, NBLK) as n:
                    act.wait_ge(a["ctx_in"], n * 16 + 16)
                    nc.scalar.activation(ctx_hi[:], ctx_raw[:], ACT.Copy).then_inc(a["ctx_hi"], 1)
                    for i in range(4):
                        if l == 1:
                            act.wait_ge(a["proj"], n * 4 + (i + 1))
                            if i >= 2:
                                act.wait_ge(a["qlo"], n * 6 + 2 * (i - 1))
                            nc.scalar.activation(qk[:, i % 2, :], bank[2 * (i % 2)][:], ACT.Identity,
                                                 bias=bias_col[l][:, i:i + 1]).then_inc(a["qk"], 1)
                        act.wait_ge(a["qk"], n * 4 + (i + 1))
                        if i < 2:
                            for g2 in range(2):
                                rows = slice(64 * g2, 64 * g2 + 64)
                                nc.scalar.activation(qstack[rows, i, g2, :], qk[rows, i, :],
                                                     ACT.Copy).then_inc(a["qhi"], 1)
                        else:
                            nc.scalar.activation(k_parts[:, 0, i - 2, :], qk[:, i - 2, :],
                                                 ACT.Copy).then_inc(a["qhi"], 1)
                    for h in range(2):
                        act.wait_ge(a["v32"], n * 2 + (h + 1))
                        nc.scalar.activation(
                            v_parts[:, 2 * h:2 * h + 2].rearrange("p b h w -> p (b h) w")[:, :, 0:16],
                            v32[:, h].rearrange("p b (h d) -> p (b h) d", h=HEADS), ACT.Copy).then_inc(a["vhi"], 1)

                    def exps(b, g):
                        act.wait_ge(a["sub"], n * 16 + (4 * b + g + 1))
                        nc.scalar.activation(prob[:, b % 2, g, :], prob[:, b % 2, g, :], ACT.Exp,
                                             scale=0.25).then_inc(a["exp"], 1)

                    for g in range(NG):
                        exps(0, g)
                    for b in range(BLK):
                        for g in range(NG):
                            if b + 1 < BLK:
                                exps(b + 1, g)
                            act.wait_ge(a["pT"], n * 16 + (4 * b + g + 1))
                            if 4 * b + g >= 2:
                                act.wait_ge(a["pv"], n * 16 + (4 * b + g - 1))
                            nc.scalar.activation(probT_hi[:, g % 2, :], bank[4 + g % 2][:],
                                                 ACT.Copy).then_inc(a["phi"], 1)
                    for k in range(KT):
                        act.wait_ge(a["oT"], n * 2 + (k + 1))
                        nc.scalar.activation(oT_hi[:, k, :], bank[4 + k][:], ACT.Copy).then_inc(a["ohi"], 1)
                ln_act(LN[2 * l + 1])
                act.wait_ge(f["rlog"], 1)
                E = NE[l]
                prods = bank[7][:, 0:B * 2 * E].rearrange("p (b c e) -> p b c e", b=B, c=2)
                nc.scalar.activation(logit[:, :, 0:E], prods[:, :, 0, :], ACT.Copy,
                                     scale=LOGIT_SCALE if l == 0 else 1.0).then_inc(f["rcopy"], 1)
                act.wait_ge(f["rfun_in"], 1)
                nc.scalar.activation(rt[1][:, :, 0:E], rt[1][:, :, 0:E],
                                     ACT.Exp if l == 0 else ACT.Sigmoid).then_inc(f["rfun"], 1)
                experts(f, J, 0, True)
                with act.Fori(1, HALF) as it:
                    experts(f, J, it, False)

        @block.vector
        def _(dve):
            def ln_dve(m, ready):
                def low(n):
                    for k in range(KT):
                        dve.wait_ge(m["ln_hi"], 2 * n + k + 1)
                        cols = slice(N * n, N * (n + 1))
                        nc.vector.tensor_tensor(xT_lo[:, k, cols], bank[2 * (n % 2) + k][:],
                                                xT_hi[:, k, cols].bitcast(F32), ALU.subtract).then_inc(m["ln_lo"], 1)

                for n in range(NBLK):
                    ready(n)
                    for t in range(BLK):
                        nc.vector.bn_stats(stats[:, t, :], xres[:, BLK * n + t, :]).then_inc(m["ln_stat"], 1)
                    for t in range(BLK):
                        dve.wait_ge(m["ln_stat"], 4 * n + t + 1)
                        nc.vector.bn_aggr(meanvar[:, n % 2, t, :], stats[:, t, :]).then_inc(m["ln_var"], 1)
                    if n >= 1:
                        low(n - 1)
                    dve.wait_ge(m["ln_std"], n + 1)
                    nc.vector.reciprocal(rstd[:, n % 2, :], std[:, n % 2, :]).then_inc(m["ln_rstd"], 1)
                    dve.wait_ge(m["ln_rstd"], n + 1)
                    for t in range(BLK):
                        nc.vector.tensor_scalar(xn[:, n % 2, t, :], xres[:, BLK * n + t, :],
                                                meanvar[:, n % 2, t, 0:1], rstd[:, n % 2, t:t + 1],
                                                ALU.subtract, ALU.mult).then_inc(m["ln_xn"], 1)
                low(NBLK - 1)

            def route(l, f):
                E, K = NE[l], TOPS[l]
                W = E + 8 - K
                done = [0]

                def link(ins):
                    done[0] += 1
                    ins.then_inc(f["route"], 1)
                    dve.wait_ge(f["route"], done[0])

                V = nc.vector
                lg, a0, a1 = logit[:, :, 0:E], rt[0][:, :, 0:E], rt[1][:, :, 0:E]
                sc, tk = score[:, :, 0:E], taken[:, :, 0:E]
                prods = bank[7][:, 0:B * 2 * E].rearrange("p (b c e) -> p b c e", b=B, c=2)
                bias = route_b[l][:].unsqueeze(1).to_broadcast([P, B, E])
                V.memset(gate[:, UNITS - 2:UNITS, :], 1.0).then_inc(f["rsum"], 1)
                link(V.memset(score[:, :, E:W], -3e38))
                dve.wait_ge(f["rcopy"], 1)
                if l == 0:
                    link(V.scalar_tensor_tensor(out=lg, in0=prods[:, :, 1, :], scalar=LOGIT_SCALE, in1=lg,
                                                op0=ALU.mult, op1=ALU.add))
                    link(V.tensor_tensor(sc, lg, bias, ALU.add))
                else:
                    V.tensor_tensor(a1, prods[:, :, 1, :], lg, ALU.add).then_inc(f["rfun_in"], 1)
                    dve.wait_ge(f["rfun"], 1)
                    link(V.tensor_tensor(lg, a1, bias, ALU.add))
                    quad = logit[:].rearrange("p b (g e) -> p b g e", g=4)
                    best, pair = r1[0][:], r1[1][:]
                    link(V.tensor_tensor(best, quad[:, :, :, 0], quad[:, :, :, 1], ALU.add))
                    for i, j in ((0, 2), (0, 3), (1, 2), (1, 3), (2, 3)):
                        link(V.tensor_tensor(pair, quad[:, :, :, i], quad[:, :, :, j], ALU.add))
                        link(V.tensor_tensor(best, best, pair, ALU.max))
                    beats = rt[0][:].rearrange("p b (g o) -> p b g o", g=4)
                    link(V.tensor_tensor(beats, best.unsqueeze(2).to_broadcast([P, B, 4, 4]),
                                         best.unsqueeze(3).to_broadcast([P, B, 4, 4]), ALU.is_gt))
                    for g in range(1, 4):
                        link(V.tensor_tensor(beats[:, :, g, 0:g], best[:, :, 0:g],
                                             best[:, :, g:g + 1].to_broadcast([P, B, g]), ALU.is_ge))
                    rank, keep = r1[2][:], r1[3][:]
                    link(V.tensor_reduce(rank, beats, AX.X, ALU.add))
                    link(V.tensor_scalar(keep, rank, 2.0, None, ALU.is_lt))
                    link(V.tensor_tensor(score[:, :, 0:E].rearrange("p b (g e) -> p b g e", g=4), quad,
                                         keep.unsqueeze(3).to_broadcast([P, B, 4, 4]), ALU.mult))
                    link(V.tensor_scalar(sc, sc, 0.0, None, ALU.add))
                for t in range(B):
                    ins = V.max(top8[:, t, :], score[:, t, 0:W])
                    ins.then_inc(f["route"], 1)
                    done[0] += 1
                dve.wait_ge(f["route"], done[0])
                link(V.memset(top8[:, :, K:8], -3e38))
                for t in range(B):
                    V.match_replace(taken[:, t, 0:W], top8[:, t, :], score[:, t, 0:W], 3e38).then_inc(f["route"], 1)
                    done[0] += 1
                dve.wait_ge(f["route"], done[0])
                link(V.tensor_tensor(a0, tk, sc, ALU.not_equal))
                total, inv = r1[0][:, :, 0:1], r1[1][:, :, 0:1]
                if l == 0:
                    link(V.tensor_scalar(a1, a0, -1.0, 1e30, ALU.add, ALU.mult))
                    link(V.tensor_tensor(a1, a1, lg, ALU.add))
                    link(V.reduce_max(r1[2][:, :, 0:1], a1, AX.X))
                    V.tensor_tensor(a1, a1, r1[2][:, :, 0:1].to_broadcast([P, B, E]),
                                    ALU.subtract).then_inc(f["rfun_in"], 1)
                    dve.wait_ge(f["rfun"], 1)
                link(V.tensor_tensor(a1, a1, a0, ALU.mult))
                link(V.tensor_reduce(total, a1, AX.X, ALU.add))
                if l == 1:
                    link(V.tensor_scalar(total, total, 1e-20, None, ALU.add))
                link(V.reciprocal(inv, total))
                link(V.tensor_tensor(a1, a1, inv.to_broadcast([P, B, E]), ALU.mult))
                weights = a1.rearrange("p b e -> p e b")
                if l == 0:
                    units = gate[:, 0:2 * E, :].rearrange("p (e u) b -> p e u b", u=2)
                    for u in range(2):
                        link(V.tensor_copy(units[:, :, u, :], weights))
                else:
                    link(V.tensor_scalar(gate[:, 0:E, :], weights, ROUTE_SCALE, None, ALU.mult))
                return done[0]

            def acc(f, it, ls, subs, first):
                par, n = divmod(ls, NBLK)
                for sub in subs:
                    dve.wait_ge(f["y"], step_no(it, ls) * 2 + (sub // 2 + 1))
                    if not (first and ls < NBLK):
                        dve.wait_ge(f["acc"], (step_no(it, ls) - NBLK) * 4 + (sub + 1))
                    rows = xres[:, BLK * n + sub, :]
                    nc.vector.scalar_tensor_tensor(
                        out=rows, in0=bank[4 + 2 * (ls % 2) + sub // 2][:, D * (sub % 2):D * (sub % 2 + 1)],
                        scalar=gate[:, ds(it * 2 + par, 1), BLK * n + sub] if not isinstance(it, int)
                        else gate[:, it * 2 + par, BLK * n + sub:BLK * n + sub + 1],
                        in1=rows, op0=ALU.mult, op1=ALU.add).then_inc(f["acc"], 1)

            def experts(f, J, it, first):
                for ls in range(STEPS):
                    for j in range(J):
                        t, r = tile_no(it, ls, j, J), (ls * J + j) % 2
                        dve.wait_ge(f["act"], t + 1)
                        nc.vector.tensor_tensor(hid[:, r, :], bank[2 * r][:], act_sb[:, r, :],
                                                ALU.mult).then_inc(f["hid"], 1)
                        subs = range(2 * j, 2 * j + 2) if J == 2 else range(BLK)
                        if ls >= 2:
                            acc(f, it, ls - 2, subs, first)
                        elif not first:
                            acc(f, it - 1, ls - 2 + STEPS, subs, False)
                        dve.wait_ge(f["hhi"], t + 1)
                        nc.vector.tensor_tensor(hid_lo[:, ls % 2, j, :], hid[:, r, :],
                                                hid_hi[:, ls % 2, j, :].bitcast(F32),
                                                ALU.subtract).then_inc(f["hlo"], 1)

            dve.wait_ge(s_in, 16 * 14)
            nc.vector.tensor_scalar(mask_b[:], mask_f, 1.0, -BIG, ALU.not_equal, ALU.mult).then_inc(s_vset, 1)
            dve.wait_ge(s_x, 16)
            for l in range(2):
                a, f, J = AT[l], FF[l], JT[l]
                for w in range(NW[l]):
                    dve.wait_ge(a["aw_hi"], w + 1)
                    nc.vector.tensor_tensor(aw_lo[:, w].rearrange("p k d -> p (k d)"), aw_raw[:, w % 2, :],
                                            aw_hi[:, w].rearrange("p k d -> p (k d)").bitcast(F32),
                                            ALU.subtract).then_inc(a["aw_lo"], 1)
                if l == 1:
                    dve.wait_ge(FF[0]["acc"], UNITS * NBLK * BLK)
                ln_dve(LN[2 * l], lambda n: None)
                with dve.Fori(0, NBLK) as n:
                    dve.wait_ge(a["ctx_hi"], n + 1)
                    nc.vector.tensor_tensor(ctx_lo[:], ctx_raw[:], ctx_hi[:].bitcast(F32),
                                            ALU.subtract).then_inc(a["ctx_lo"], 1)

                    def low(i):
                        if i < 2:
                            for g2 in range(2):
                                rows, other = slice(64 * g2, 64 * g2 + 64), slice(64 - 64 * g2, 128 - 64 * g2)
                                dve.wait_ge(a["qhi"], n * 6 + (2 * i + g2 + 1))
                                nc.vector.tensor_tensor(qstack[other, i, g2, :], qk[rows, i, :],
                                                        qstack[rows, i, g2, :].bitcast(F32),
                                                        ALU.subtract).then_inc(a["qlo"], 1)
                        else:
                            dve.wait_ge(a["qhi"], n * 6 + (i + 3))
                            nc.vector.tensor_tensor(k_parts[:, 1, i - 2, :], qk[:, i - 2, :],
                                                    k_parts[:, 0, i - 2, :].bitcast(F32),
                                                    ALU.subtract).then_inc(a["qlo"], 1)

                    for i in range(4):
                        if l == 0:
                            r = i % 2
                            dve.wait_ge(a["proj"], n * 4 + (i + 1))
                            if i >= 2:
                                dve.wait_ge(a["qlo"], n * 6 + 2 * (i - 1))
                            for c, (dst, tab) in enumerate(((qk, cosS), (rope_b, sinS))):
                                nc.vector.scalar_tensor_tensor(
                                    out=dst[:, r].rearrange("p (b s) -> p b s", b=BLK),
                                    in0=bank[2 * r + c][:].rearrange("p (b s) -> p b s", b=BLK),
                                    scalar=bias_col[l][:, 4 * c + i:4 * c + i + 1],
                                    in1=tab[:].unsqueeze(1).to_broadcast([P, BLK, S]),
                                    op0=ALU.add, op1=ALU.mult).then_inc(a["rope"], 1)
                            dve.wait_ge(a["rope"], n * 8 + 2 * (i + 1))
                            nc.vector.tensor_tensor(qk[:, r, :], qk[:, r, :], rope_b[:, r, :],
                                                    ALU.add).then_inc(a["qk"], 1)
                        low(i)
                    for h in range(2):
                        dve.wait_ge(a["vps"], n * 2 + (h + 1))
                        nc.vector.tensor_tensor(v32[:, h], bank[4 + h][:].rearrange("p (b d) -> p b d", b=2),
                                                bv_row[l][:].unsqueeze(1).to_broadcast([P, 2, D]),
                                                ALU.add).then_inc(a["v32"], 1)

                    def shifted(b, g):
                        i = 4 * b + g + 1
                        dve.wait_ge(a["score"], n * 16 + i)
                        grp = bank[g][:].rearrange("p (h t) -> p h t", h=GRP)
                        mx = smax[:, b % 2, GRP * g:GRP * (g + 1)]
                        nc.vector.reduce_max(mx, grp, AX.X).then_inc(a["max"], 1)
                        dve.wait_ge(a["max"], n * 16 + i)
                        nc.vector.tensor_tensor(prob[:, b % 2, g, :].rearrange("p (h t) -> p h t", h=GRP), grp,
                                                mx.unsqueeze(2).to_broadcast([P, GRP, S]),
                                                ALU.subtract).then_inc(a["sub"], 1)

                    def output(b):
                        dve.wait_ge(a["pv"], n * 16 + (4 * b + 4))
                        heads = bank[6 + b % 2][:, 0:17 * HEADS].rearrange("p (h w) -> p h w", h=HEADS)
                        nc.vector.reciprocal(rden[:, b % 2, :], heads[:, :, 16]).then_inc(a["rden"], 1)
                        dve.wait_ge(a["rden"], n * 4 + (b + 1))
                        nc.vector.tensor_tensor(o_sb[:, b, :].rearrange("p (h d) -> p h d", h=HEADS),
                                                heads[:, :, 0:HD],
                                                rden[:, b % 2, :].unsqueeze(2).to_broadcast([P, HEADS, HD]),
                                                ALU.mult).then_inc(a["o"], 1)

                    for g in range(NG):
                        shifted(0, g)
                    for b in range(BLK):
                        for g in range(NG):
                            if b + 1 < BLK:
                                shifted(b + 1, g)
                            dve.wait_ge(a["phi"], n * 16 + (4 * b + g + 1))
                            nc.vector.tensor_tensor(probT_lo[:, g % 2, :], bank[4 + g % 2][:], probT_hi[:, g % 2, :],
                                                    ALU.subtract).then_inc(a["plo"], 1)
                            if g == 1 and b >= 1:
                                output(b - 1)
                    output(BLK - 1)
                    for k in range(KT):
                        dve.wait_ge(a["ohi"], n * 2 + (k + 1))
                        nc.vector.tensor_tensor(oT_lo[:, k, :], bank[4 + k][:], oT_hi[:, k, :].bitcast(F32),
                                                ALU.subtract).then_inc(a["olo"], 1)
                    dve.wait_ge(a["xbo"], n + 1)
                    for h in range(2):
                        dve.wait_ge(a["wo"], n * 2 + (h + 1))
                        rows = xres[:, ds(n * BLK + 2 * h, 2), :]
                        nc.vector.tensor_tensor(rows, bank[h][:].rearrange("p (b d) -> p b d", b=2), rows,
                                                ALU.add).then_inc(a["xadd"], 1)
                ln_dve(LN[2 * l + 1], lambda n: dve.wait_ge(a["xadd"], 2 * n + 2))
                dve.wait_ge(f["rlog"], 1)
                route(l, f)
                experts(f, J, 0, True)
                with dve.Fori(1, HALF) as it:
                    experts(f, J, it, False)
                for ls in range(STEPS - 2, STEPS):
                    acc(f, HALF - 1, ls, range(BLK), False)

        @block.tensor
        def _(pe):
            def ln_pe(m):
                for n in range(NBLK):
                    pe.wait_ge(m["ln_xn"], 4 * n + 4)
                    if n >= 2:
                        pe.wait_ge(m["ln_lo"], 2 * n - 2)
                    for k in range(KT):
                        for t in range(BLK):
                            last = nc.tensor.transpose(bank[2 * (n % 2) + k][:, P * t:P * (t + 1)],
                                                       xn[:, n % 2, t, P * k:P * (k + 1)], ident[:])
                        last.then_inc(m["ln_T"], 1)

            def products(dst, left, right, finish=True):
                pairs = [(lh, rh) for k in range(KT)
                         for lh, rh in ((left[0](k), right[0](k)), (left[1](k), right[0](k)),
                                        (left[0](k), right[1](k)))]
                for i, (lh, rh) in enumerate(pairs):
                    last = nc.tensor.matmul(dst, lh, rh, start=(i == 0), stop=(i == len(pairs) - 1))
                return last

            def up(l, f, J, it, ls, first):
                par, n = divmod(ls, NBLK)
                if n == 0:
                    pe.wait_ge(f["w_lo"], it * 2 + (par + 1))
                for j in range(J):
                    r = (ls * J + j) % 2
                    if not (first and ls * J + j < 2):
                        pe.wait_ge(f["hid"], tile_no(it, ls, j, J) - 1)
                    for c in range(2):
                        def w(part):
                            return lambda k: part[par][:, (c * KT + k) * P * J + P * j:(c * KT + k) * P * J + P * (j + 1)]
                        cols = slice(N * n, N * (n + 1))
                        last = products(bank[2 * r + c][:], (w(w_hi), w(w_lo)),
                                        (lambda k: xT_hi[:, k, cols], lambda k: xT_lo[:, k, cols]))
                    last.then_inc(f["up"], 1)

            def down(f, J, it, ls, first):
                par = ls // NBLK
                pe.wait_ge(f["hlo"], tile_no(it, ls, J, J))
                if not (first and ls < 2):
                    pe.wait_ge(f["acc"], (step_no(it, ls) - 1) * 4)
                for sub in range(BLK):
                    rows = slice(P * sub, P * (sub + 1))
                    pairs = []
                    for j in range(J):
                        cols = slice(4 * P * J + D * j, 4 * P * J + D * (j + 1))
                        hh, hl = hid_hi[:, ls % 2, j, rows], hid_lo[:, ls % 2, j, rows]
                        wh, wl = w_hi[par][:, cols], w_lo[par][:, cols]
                        pairs += [(hh, wh), (hl, wh), (hh, wl)]
                    dst = bank[4 + 2 * (ls % 2) + sub // 2][:, D * (sub % 2):D * (sub % 2 + 1)]
                    for i, (h, w) in enumerate(pairs):
                        last = nc.tensor.matmul(dst, h, w, start=(i == 0), stop=(i == len(pairs) - 1))
                    if sub % 2:
                        last.then_inc(f["y"], 1)

            def experts(l, f, J, it, first, final):
                for ls in range(STEPS):
                    if ls + 1 < STEPS:
                        up(l, f, J, it, ls + 1, first)
                    elif not final:
                        up(l, f, J, it + 1, 0, False)
                    down(f, J, it, ls, first)

            pe.wait_ge(s_in, 16 * 14)
            for l in range(2):
                a, f, J = AT[l], FF[l], JT[l]
                ln_pe(LN[2 * l])
                pe.wait_ge(LN[2 * l]["ln_lo"], 2 * NBLK)
                pe.wait_ge(a["aw_lo"], NW[l])
                if l == 1:
                    pe.wait_ge(s_vset, 1)
                    pe.wait_ge(s_set, 2)
                with pe.Fori(0, NBLK) as n:
                    for i in range(4):
                        m = i % 2
                        if i == 2:
                            pe.wait_ge(a["ctx_lo"], n + 1)
                        if i >= 2:
                            pe.wait_ge(a["qk"], n * 4 + (i - 1))
                        for c, w in enumerate(UNIT_W[l][i]):
                            def wt(part):
                                return lambda k: part[:, w, k, P * m:P * (m + 1)]
                            if i < 2:
                                right = (lambda k: xT_hi[:, k, ds(n * N, N)], lambda k: xT_lo[:, k, ds(n * N, N)])
                            else:
                                right = (lambda k: ctx_hi[:, k, :], lambda k: ctx_lo[:, k, :])
                            last = products(bank[2 * (i % 2) + c][:], (wt(aw_hi), wt(aw_lo)), right)
                        last.then_inc(a["proj"], 1)
                    for b in range(BLK):
                        rows = slice(P * b, P * (b + 1))
                        last = products(bank[4 + b // 2][:, D * (b % 2):D * (b % 2 + 1)],
                                        (lambda k: ctx_hi[:, k, rows], lambda k: ctx_lo[:, k, rows]),
                                        (lambda k: aw_hi[:, V_W[l], k, :], lambda k: aw_lo[:, V_W[l], k, :]))
                        if b % 2:
                            last.then_inc(a["vps"], 1)

                    def scores(b, g):
                        if b == 0:
                            pe.wait_ge(a["qk"], n * 4 + 4)
                        else:
                            pe.wait_ge(a["sub"], n * 16 + (4 * (b - 1) + g + 1))
                        if g == 0:
                            pe.wait_ge(a[f"kdma{b % 2}"], n * 512 + (b // 2 + 1) * 256)
                        q = qstack[:, g // 2, g % 2, S * b:S * (b + 1)]
                        for part in range(2):
                            last = nc.tensor.matmul(bank[g][:], q, kexp[b % 2][:, part, g].rearrange("p h t -> p (h t)"),
                                                    start=(part == 0), stop=(part == 1 and l == 0))
                        if l == 1:
                            row = mask_b[:, ds((n * BLK + b) * S, S)].unsqueeze(1).to_broadcast([1, GRP, S])
                            last = nc.tensor.matmul(bank[g][:].rearrange("p (h t) -> p h t", h=GRP), ones_row[:], row,
                                                    start=False, stop=True)
                        last.then_inc(a["score"], 1)

                    def turned(b, g):
                        i = 4 * b + g
                        pe.wait_ge(a["exp"], n * 16 + (i + 1))
                        if i < 2:
                            pe.wait_ge(a["v32"], n * 2 + (i + 1))
                        else:
                            pe.wait_ge(a["plo"], n * 16 + (i - 1))
                        for h in range(GRP):
                            last = nc.tensor.transpose(bank[4 + g % 2][:, S * h:S * (h + 1)],
                                                       prob[:, b % 2, g, S * h:S * (h + 1)], ident[:])
                        last.then_inc(a["pT"], 1)

                    def weighed(b, g):
                        i = 4 * b + g
                        pe.wait_ge(a["plo"], n * 16 + (i + 1))
                        if i == 0:
                            pe.wait_ge(a["vlo"], n * 2 + 2)
                        if b >= 2 and g == 0:
                            pe.wait_ge(a["o"], n * 4 + (b - 1))
                        for h in range(GRP):
                            head = GRP * g + h
                            dst = 17 * head
                            cols = slice(S * h, S * (h + 1))
                            parts = ((0, 17), (18, 16), (34, 16))
                            terms = [(p, c, w) for p in (probT_hi, probT_lo) for c, w in parts]
                            for t, (p, c, w) in enumerate(terms):
                                last = nc.tensor.matmul(bank[6 + b % 2][:, dst:dst + w], p[:, g % 2, cols],
                                                        v_parts[:, b, head, c:c + w], start=(t == 0),
                                                        stop=(t == len(terms) - 1))
                        last.then_inc(a["pv"], 1)

                    for g in range(NG):
                        scores(0, g)
                    for b in range(BLK):
                        for g in range(NG):
                            if b + 1 < BLK:
                                scores(b + 1, g)
                            turned(b, g)
                            if g > 0:
                                weighed(b, g - 1)
                            elif b > 0:
                                weighed(b - 1, NG - 1)
                    weighed(BLK - 1, NG - 1)
                    pe.wait_ge(a["o"], n * 4 + 4)
                    pe.wait_ge(a["plo"], n * 16 + 16)
                    for k in range(KT):
                        for b in range(BLK):
                            last = nc.tensor.transpose(bank[4 + k][:, P * b:P * (b + 1)],
                                                       o_sb[:, b, P * k:P * (k + 1)], ident[:])
                        last.then_inc(a["oT"], 1)
                    pe.wait_ge(a["olo"], n * 2 + 2)
                    for b in range(BLK):
                        rows = slice(P * b, P * (b + 1))
                        last = products(bank[b // 2][:, D * (b % 2):D * (b % 2 + 1)],
                                        (lambda k: oT_hi[:, k, rows], lambda k: oT_lo[:, k, rows]),
                                        (lambda k: aw_hi[:, O_W[l], k, :], lambda k: aw_lo[:, O_W[l], k, :]))
                        if b % 2:
                            last.then_inc(a["wo"], 1)
                    pe.wait_ge(a["xadd"], n * 2 + 2)
                ln_pe(LN[2 * l + 1])
                pe.wait_ge(LN[2 * l + 1]["ln_lo"], 2 * NBLK)
                pe.wait_ge(s_wsplit[l], 2)
                E = NE[l]
                for t in range(B):
                    rows = slice(P * t, P * (t + 1))
                    pairs = [(p[:, k, rows], k) for k in range(KT) for p in (xT_hi, xT_lo)]
                    for i, (p, k) in enumerate(pairs):
                        last = nc.tensor.matmul(bank[7][:, 2 * E * t:2 * E * (t + 1)], p,
                                                route_wr[l][:, k].rearrange("p c e -> p (c e)"),
                                                start=(i == 0), stop=(i == len(pairs) - 1))
                last.then_inc(f["rlog"], 1)
                up(l, f, J, 0, 0, True)
                pe.wait_ge(f["rfun"], 1)
                experts(l, f, J, 0, True, False)
                with pe.Fori(1, HALF - 1) as it:
                    experts(l, f, J, it, False, False)
                experts(l, f, J, HALF - 1, False, True)



def kernel(**inputs):
    import concourse.bacc as bacc
    from concourse import mybir as _mybir
    from concourse.bass_utils import run_bass_kernel_spmd

    a = {k: np.asarray(v) for k, v in inputs.items()}

    def tiles(w):
        return w.reshape(w.shape[0] // P, P, w.shape[1]).transpose(1, 0, 2)

    def flat(w):
        t = tiles(w)
        return t.reshape(P, -1)

    partner = np.arange(D) ^ 1
    arrays = {"x": a["x"]}
    arrays["ctxT"] = tiles(a["ctx_1024"].reshape(TOK, D).T)
    arrays["maskrow"] = a["mask_BxS2_ff1"].reshape(1, TOK)
    freq = 1.0 / 10000.0 ** (np.arange(0, HD, 2, dtype=np.float32) / HD)
    angle = (np.arange(S, dtype=np.float32)[:, None] * freq[None, :].astype(np.float32)).astype(np.float32)
    row = np.arange(P) % HD
    sign = np.where(row % 2 == 0, -1.0, 1.0).astype(np.float32)
    arrays["cosT"] = np.cos(angle).T[row // 2]
    arrays["sinT"] = np.sin(angle).T[row // 2] * sign[:, None]
    arrays["ident"] = np.eye(P, dtype=np.float32)
    for l in range(2):
        w = {n: a[f"L{l}_xattn_W{n}"].T for n in "qkvo"}
        b = {n: a[f"L{l}_xattn_b{n}"] for n in "qkvo"}
        ws = [w["q"], w["q"][:, partner], w["k"], w["k"][:, partner], w["v"], w["o"]] if l == 0 else \
            [w[n] for n in "qkvo"]
        arrays[f"aw{l}"] = np.stack([flat(v) for v in ws], axis=1)
        cols = [b["q"], b["k"], b["q"][partner], b["k"][partner]]
        arrays[f"ab{l}"] = np.concatenate([c.reshape(KT, P).T for c in cols], axis=1)
        arrays[f"arow{l}"] = np.stack([b["v"], b["o"]])
    arrays["rw0"] = tiles(a["L0_ffn_Wr"])
    arrays["rw1"] = tiles(a["L1_ffn_router_weight"].T)
    arrays["rrow0"] = a["L0_ffn_rb"].reshape(1, E0)
    arrays["rrow1"] = a["L1_ffn_e_bias"].reshape(1, E1)

    def unit(linear, gated, out):
        return np.concatenate([flat(linear), flat(gated), flat(out)], axis=1)

    W1 = list(a["L0_ffn_W1"]) + [a["L0_ffn_Ws1"]]
    W2 = list(a["L0_ffn_W2"]) + [a["L0_ffn_Ws2"]]
    W3 = list(a["L0_ffn_W3"]) + [a["L0_ffn_Ws3"]]
    arrays["fw0"] = np.stack([unit(W1[u // 2][:, h], W3[u // 2][:, h], W2[u // 2][h, :])
                              for u in range(UNITS) for h in (slice(256 * (u % 2), 256 * (u % 2) + 256),)])
    parts = [(a["L1_ffn_up_w"][e], a["L1_ffn_gate_w"][e], a["L1_ffn_down_w"][e]) for e in range(E1)]
    for h in (slice(0, P), slice(P, 2 * P)):
        parts.append((a["L1_ffn_sh_up_w"][h], a["L1_ffn_sh_gate_w"][h], a["L1_ffn_sh_down_w"][:, h]))
    arrays["fw1"] = np.stack([unit(u.T, g.T, d.T) for u, g, d in parts])

    nc = bacc.Bacc("TRN2", target_bir_lowering=False, num_devices=1)
    arrays = {f"in_{k}": np.ascontiguousarray(v) for k, v in arrays.items()}
    ap = {k[3:]: nc.dram_tensor(k, v.shape, _mybir.dt.from_np(v.dtype), kind="ExternalInput").ap()
          for k, v in arrays.items()}
    out = nc.dram_tensor("out_x", (B, S, D), _mybir.dt.float32, kind="ExternalOutput").ap()
    program(nc, ap["x"], ap["ctxT"], ap["maskrow"], ap["cosT"], ap["sinT"], ap["ident"],
            [ap["aw0"], ap["aw1"]], [ap["ab0"], ap["ab1"]], [ap["arow0"], ap["arow1"]],
            [ap["rw0"], ap["rw1"]], [ap["rrow0"], ap["rrow1"]], [ap["fw0"], ap["fw1"]], out)
    r = run_bass_kernel_spmd(nc, [arrays], core_ids=[0])
    return r.results[0]["out_x"]
```

```python
from contextlib import ExitStack

import numpy as np

import concourse.bass as bass
from concourse import mybir

B, S, D = 16, 128, 256
HEADS, HD = 16, 16
P = 128
KT = D // P
BLK = 4
NBLK = B // BLK
TOK = B * S
N = BLK * S
GRP = 4
NG = HEADS // GRP
VW = 50
RING, RINGT = 6, 3
E0, E1 = 8, 16
TOP0, TOP1 = 2, 4
UNITS = 18
EPS = 1e-5
LOGIT_SCALE = 1.0 / 16.0
ROUTE_SCALE = 2.5
BIG = 3.3895313892515355e38


def program(nc, x, ctxT, maskrow, tab_in, ident_in, aw, ab, arow, rw, rrow, fw, out):
    F32, F32R = mybir.dt.float32, mybir.dt.float32r
    F16, BF16 = mybir.dt.float16, mybir.dt.bfloat16
    ALU, ACT = mybir.AluOpType, mybir.ActivationFunctionType
    AX = mybir.AxisListType
    ds = bass.ds

    ctx = ExitStack()
    with ctx:
        def sb(stack, name, shape, dt):
            return stack.enter_context(nc.sbuf_tensor(name, shape, dt))

        def sem(name):
            return ctx.enter_context(nc.semaphore(name))

        xres = sb(ctx, "xres", [P, B, D], F32)
        xT_hi = sb(ctx, "xT_hi", [P, KT, TOK], F32R)
        xT_lo = sb(ctx, "xT_lo", [P, KT, TOK], F32R)
        ident = sb(ctx, "ident", [P, P], F32)
        stats = sb(ctx, "stats", [P, BLK, 6], F32)
        meanvar = sb(ctx, "meanvar", [P, 2, BLK, 2], F32)
        std = sb(ctx, "std", [P, 2, BLK], F32)
        rstd = sb(ctx, "rstd", [P, 2, BLK], F32)
        eps_col = sb(ctx, "eps_col", [P, 1], F32)
        zero_col = sb(ctx, "zero_col", [P, 1], F32)
        rope_tab = sb(ctx, "rope_tab", [P, 2, 2, S], F32)
        first_row = sb(ctx, "first_row", [P, P], BF16)
        mask_b = sb(ctx, "mask_b", [P, B * S], BF16)
        bias_col = [sb(ctx, f"bias_col{l}", [P, 8], F32) for l in range(2)]
        bv_row = [sb(ctx, f"bv_row{l}", [P, D], F32) for l in range(2)]
        bo_row = [sb(ctx, f"bo_row{l}", [P, D], F32) for l in range(2)]
        NE, TOPS = [E0, E1], [TOP0, TOP1]
        route_w = [sb(ctx, f"route_w{l}", [P, KT, NE[l]], F32) for l in range(2)]
        route_wr = [sb(ctx, f"route_wr{l}", [P, KT, 2, NE[l]], F32R) for l in range(2)]
        route_b = [sb(ctx, f"route_b{l}", [P, NE[l]], F32) for l in range(2)]
        EW = E1 + 8
        logit = sb(ctx, "logit", [P, B, E1], F32)
        score = sb(ctx, "score", [P, B, EW], F32)
        taken = sb(ctx, "taken", [P, B, EW], F32)
        top8 = sb(ctx, "top8", [P, B, 8], F32)
        rt = [sb(ctx, f"rt{i}", [P, B, E1], F32) for i in range(2)]
        r1 = [sb(ctx, f"r1_{i}", [P, B, 4], F32) for i in range(4)]
        gate = sb(ctx, "gate", [P, UNITS, B], F32)

        at = ExitStack()
        ctx_raw = sb(at, "ctx_raw", [P, KT, N], F32)
        ctx_hi = sb(at, "ctx_hi", [P, KT, N], F32R)
        ctx_lo = sb(at, "ctx_lo", [P, KT, N], F32R)
        aw_hi = sb(at, "aw_hi", [P, 6, KT, D], F32R)
        aw_lo = sb(at, "aw_lo", [P, 6, KT, D], F32R)
        rope_b = sb(at, "rope_b", [P, 2, N], F32)
        qk = sb(at, "qk", [P, 2, N], F32)
        q_parts = sb(at, "q_parts", [P, 2, KT, N], F32R)
        k_parts = sb(at, "k_parts", [P, 2, KT, N], F32R)
        kexp = [sb(at, f"kexp{i}", [P, 2, NG, GRP, S], F32R) for i in range(2)]
        v32 = sb(at, "v32", [P, 2, 2, D], F32)
        v_parts = sb(at, "v_parts", [P, BLK, HEADS, VW], BF16)
        probT_hi = sb(at, "probT_hi", [P, RINGT, N], F16)
        probT_lo = sb(at, "probT_lo", [P, RINGT, N], F16)
        nmax = sb(at, "nmax", [P, 2, HEADS], F32)
        rden = sb(at, "rden", [P, 2, HEADS // 2], F32)
        o_raw = sb(at, "o_raw", [P, 2, HEADS // 2, VW], F32)
        o_sb = sb(at, "o_sb", [P, BLK, HEADS, HD], F32)
        oT_hi = sb(at, "oT_hi", [P, KT, N], F32R)
        oT_lo = sb(at, "oT_lo", [P, KT, N], F32R)
        st = ExitStack()
        prob = sb(st, "prob", [P, RING, N], F32)
        st.close()
        xn = sb(at, "xn", [P, 2, BLK, D], F32)
        aw_raw = sb(at, "aw_raw", [P, 2, KT * D], F32)
        mask_f = xn[0:1].rearrange("p a b d -> p (a b d)")
        at.close()
        ft = ExitStack()
        w_raw = sb(ft, "w_raw", [P, 2, 1536], F32)
        w_hi = [sb(ft, f"w_hi{i}", [P, 1536], F32R) for i in range(2)]
        w_lo = [sb(ft, f"w_lo{i}", [P, 1536], F32R) for i in range(2)]
        act_sb = sb(ft, "act_sb", [P, 2, N], F32)
        hid = sb(ft, "hid", [P, 2, N], F32)
        hid_hi = sb(ft, "hid_hi", [P, 2, 2, N], F32R)
        hid_lo = sb(ft, "hid_lo", [P, 2, 2, N], F32R)
        ft.close()

        bank = [ctx.enter_context(nc.psum_tensor(f"bank{i}", [P, 512], F32)) for i in range(8)]

        s_in = sem("s_in")
        s_x = sem("s_x")
        s_store = sem("s_store")
        s_set = sem("s_set")
        s_vset = sem("s_vset")
        s_wsplit = [sem(f"s_route_split{l}") for l in range(2)]

        def stage_sems(names, l):
            return {n: sem(f"{n}_{l}") for n in names}

        LN = [stage_sems(["ln_stat", "ln_var", "ln_std", "ln_rstd", "ln_xn", "ln_T", "ln_hi", "ln_lo"], i) for i in range(4)]
        AT = [stage_sems(["aw_in0", "aw_in1", "kdma0", "kdma1", "aw_hi", "aw_lo", "ctx_in", "ctx_hi", "ctx_lo",
                          "proj", "rope", "qk", "qkhi", "qklo", "vps", "v32", "vhi", "vones", "vres", "vmid", "vlo",
                          "kzero", "score", "max", "sub", "exp", "pT", "phi", "plo", "pv", "ocopy", "oadd", "rden",
                          "o", "oT", "ohi", "olo", "wo", "xadd", "xbo"], l)
              for l in range(2)]
        FF = [stage_sems(["w_in0", "w_in1", "w_hi", "w_lo", "up", "act", "hid", "hhi", "hlo", "y", "acc",
                          "rlog", "rcopy", "rsum", "rfun_in", "rfun", "route"], l) for l in range(2)]

        NW = [6, 4]
        JT = [2, 1]
        V_W, O_W = [4, 2], [5, 3]
        UNIT_W = [[(2, 3), (2, 3), (0, 1), (0, 1)], [(1,), (1,), (0,), (0,)]]
        GROUPS = BLK * NG
        HALF = UNITS // 2
        STEPS = 2 * NBLK

        def step_no(it, ls):
            return it * STEPS + ls

        def tile_no(it, ls, j, J):
            return it * (STEPS * J) + (ls * J + j)

        block = ctx.enter_context(nc.Block())

        @block.sync
        def _(sp):
            sp.dma_start(xres[:], x.rearrange("b s d -> s b d")).then_inc(s_x, 16)
            sp.dma_start(ident[:], ident_in).then_inc(s_in, 16)
            sp.dma_start(rope_tab[:], tab_in).then_inc(s_in, 16)
            sp.dma_start(mask_f, maskrow).then_inc(s_in, 16)
            for l in range(2):
                sp.dma_start(bias_col[l][:], ab[l]).then_inc(s_in, 16)
                sp.dma_start(bv_row[l][:], arow[l][0:1, :].to_broadcast([P, D])).then_inc(s_in, 16)
                sp.dma_start(bo_row[l][:], arow[l][1:2, :].to_broadcast([P, D])).then_inc(s_in, 16)
                sp.dma_start(route_w[l][:], rw[l]).then_inc(s_in, 16)
                sp.dma_start(route_b[l][:], rrow[l].to_broadcast([P, NE[l]])).then_inc(s_in, 16)
            for l in range(2):
                a, f, J = AT[l], FF[l], JT[l]
                if l > 0:
                    sp.wait_ge(FF[l - 1]["acc"], UNITS * NBLK * BLK)
                for w in range(NW[l]):
                    if w >= 2:
                        sp.wait_ge(a["aw_lo"], w - 1)
                    sp.dma_start(aw_raw[:, w % 2, :], aw[l][:, w, :]).then_inc(a[f"aw_in{w % 2}"], 16)

                def keys(n):
                    sp.wait_ge(a["qklo"], n * 4 + 2)
                    for b in range(BLK):
                        if b >= 2:
                            sp.wait_ge(a["score"], n * GROUPS + (b - 1) * NG)
                        for g2 in range(2):
                            for j in range(GRP):
                                rows = slice(64 * g2 + HD * j, 64 * g2 + HD * (j + 1))
                                src = k_parts[rows, :, :, b * S:(b + 1) * S]
                                dst = kexp[b % 2][rows, :, g2::2, j, :]
                                sp.dma_start(dst.bitcast(F32), src.bitcast(F32)).then_inc(a[f"kdma{b % 2}"], 16)

                sp.dma_start(ctx_raw[:], ctxT[:, :, 0:N]).then_inc(a["ctx_in"], 16)
                sp.wait_ge(a["kzero"], 2)
                with sp.Fori(0, NBLK - 1) as n:
                    sp.wait_ge(a["ctx_lo"], n + 1)
                    sp.dma_start(ctx_raw[:], ctxT[:, :, ds(n * N + N, N)]).then_inc(a["ctx_in"], 16)
                    keys(n)
                keys(NBLK - 1)
                sp.wait_ge(a["xadd"], 2 * NBLK)
                for par in range(2):
                    sp.dma_start(w_raw[:, par, 0:768 * J], fw[l][par, :, :]).then_inc(f[f"w_in{par}"], 16)
                with sp.Fori(1, HALF) as it:
                    for par in range(2):
                        sp.wait_ge(f["w_lo"], it * 2 + par - 1)
                        src = fw[l][ds(it * 2 + par, 1), :, :].rearrange("u p c -> p (u c)")
                        sp.dma_start(w_raw[:, par, 0:768 * J], src).then_inc(f[f"w_in{par}"], 16)
            sp.wait_ge(FF[1]["acc"], UNITS * NBLK * BLK)
            sp.dma_start(out.rearrange("b s d -> s b d"), xres[:]).then_inc(s_store, 16)
            sp.wait_ge(s_store, 16)

        @block.gpsimd
        def _(pool):
            def add_bias(m, bo, a):
                for n in range(NBLK):
                    pool.wait_ge(m["ln_xn"], 4 * n + 4)
                    rows = xres[:, BLK * n:BLK * (n + 1), :]
                    nc.gpsimd.tensor_tensor(rows, rows, bo[:].unsqueeze(1).to_broadcast([P, BLK, D]),
                                            ALU.add).then_inc(a["xbo"], 1)

            def split_unit(f, it, par, W):
                pool.wait_ge(f[f"w_in{par}"], it * 16 + 16)
                raw = w_raw[:, par, 0:W]
                nc.gpsimd.tensor_tensor(w_hi[par][:, 0:W], raw, zero_col[:].to_broadcast([P, W]),
                                        ALU.subtract).then_inc(f["w_hi"], 1)
                pool.wait_ge(f["w_hi"], it * 2 + par + 1)
                nc.gpsimd.tensor_tensor(w_lo[par][:, 0:W], w_raw[:, par, 0:W],
                                        w_hi[par][:, 0:W].bitcast(F32), ALU.subtract).then_inc(f["w_lo"], 1)

            nc.gpsimd.memset(first_row[:], 0.0).then_inc(s_set, 1)
            nc.gpsimd.memset(mask_b[:], 0.0).then_inc(s_set, 1)
            nc.gpsimd.memset(eps_col[:], EPS).then_inc(s_set, 1)
            nc.gpsimd.memset(zero_col[:], 0.0).then_inc(s_set, 1)
            pool.wait_ge(s_set, 4)
            nc.gpsimd.memset(first_row[0:1, :], 1.0).then_inc(s_set, 1)
            pool.wait_ge(s_in, 16 * 13)
            for l in range(2):
                nc.gpsimd.tensor_copy(route_wr[l][:, :, 0, :], route_w[l][:]).then_inc(s_wsplit[l], 1)
                pool.wait_ge(s_wsplit[l], 1)
                nc.gpsimd.tensor_tensor(route_wr[l][:, :, 1, :], route_w[l][:],
                                        route_wr[l][:, :, 0, :].bitcast(F32), ALU.subtract).then_inc(s_wsplit[l], 1)
            for l in range(2):
                a, f = AT[l], FF[l]
                if l > 0:
                    pool.wait_ge(FF[l - 1]["acc"], UNITS * NBLK * BLK)
                for i in range(2):
                    nc.gpsimd.memset(kexp[i][:].bitcast(F32), 0.0).then_inc(a["kzero"], 1)
                nc.gpsimd.memset(v_parts[:, :, :, HD:HD + 2], 1.0).then_inc(a["vones"], 1)
                add_bias(LN[2 * l], bo_row[l], a)

                def context_low(m):
                    pool.wait_ge(a["ctx_hi"], m + 1)
                    nc.gpsimd.tensor_tensor(ctx_lo[:], ctx_raw[:], ctx_hi[:].bitcast(F32),
                                            ALU.subtract).then_inc(a["ctx_lo"], 1)

                def value_parts(m):
                    for h in range(2):
                        parts = v_parts[:, 2 * h:2 * h + 2].rearrange("p b h w -> p (b h) w")
                        rest = v32[:, h].rearrange("p b (h d) -> p (b h) d", h=HEADS)
                        pool.wait_ge(a["vhi"], m * 2 + (h + 1))
                        nc.gpsimd.tensor_tensor(rest, rest, parts[:, :, 0:16], ALU.subtract).then_inc(a["vres"], 1)
                        pool.wait_ge(a["vres"], m * 2 + (h + 1))
                        nc.gpsimd.tensor_tensor(parts[:, :, 18:34], rest,
                                                zero_col[:].unsqueeze(2).to_broadcast([P, 2 * HEADS, HD]),
                                                ALU.subtract).then_inc(a["vmid"], 1)
                        pool.wait_ge(a["vmid"], m * 2 + (h + 1))
                        nc.gpsimd.tensor_tensor(parts[:, :, 34:50], rest, parts[:, :, 18:34],
                                                ALU.subtract).then_inc(a["vlo"], 1)

                def outputs(n):
                    for c in range(2 * BLK):
                        raw, dst = o_raw[:, c % 2], o_sb[:, c // 2, 8 * (c % 2):8 * (c % 2) + 8, :]
                        pool.wait_ge(a["ocopy"], n * 8 + (c + 1))
                        nc.gpsimd.tensor_tensor(dst, raw[:, :, 0:16], raw[:, :, 18:34], ALU.add).then_inc(a["oadd"], 1)
                        pool.wait_ge(a["oadd"], n * 16 + (2 * c + 1))
                        nc.gpsimd.tensor_tensor(dst, dst, raw[:, :, 34:50], ALU.add).then_inc(a["oadd"], 1)
                        pool.wait_ge(a["oadd"], n * 16 + (2 * c + 2))
                        pool.wait_ge(a["rden"], n * 8 + (c + 1))
                        nc.gpsimd.tensor_tensor(dst, dst, rden[:, c % 2].unsqueeze(2).to_broadcast([P, 8, HD]),
                                                ALU.mult).then_inc(a["o"], 1)

                context_low(0)
                value_parts(0)
                with pool.Fori(0, NBLK - 1) as n:
                    context_low(n + 1)
                    outputs(n)
                    value_parts(n + 1)
                outputs(NBLK - 1)
                pool.wait_ge(a["xadd"], 2 * NBLK)
                for par in range(2):
                    split_unit(f, 0, par, 768 * JT[l])
                with pool.Fori(1, HALF) as it:
                    for par in range(2):
                        pool.wait_ge(f["y"], (it * 2 + par - 1) * (2 * NBLK))
                        split_unit(f, it, par, 768 * JT[l])

        @block.scalar
        def _(act):
            def ln_act(m):
                for n in range(NBLK + 1):
                    if n < NBLK:
                        act.wait_ge(m["ln_var"], 4 * n + 4)
                        nc.scalar.activation(std[:, n % 2, :], meanvar[:, n % 2, :, 1], ACT.Sqrt,
                                             bias=eps_col[:]).then_inc(m["ln_std"], 1)
                    for k in range(KT if n else 0):
                        act.wait_ge(m["ln_T"], 2 * n + k - 1)
                        nc.scalar.activation(xT_hi[:, k, N * (n - 1):N * n], bank[2 * ((n - 1) % 2) + k][:],
                                             ACT.Copy).then_inc(m["ln_hi"], 1)

            def experts(f, J, it, first):
                for ls in range(STEPS):
                    for j in range(J):
                        t = tile_no(it, ls, j, J)
                        act.wait_ge(f["up"], t + 1)
                        nc.scalar.activation(act_sb[:, (ls * J + j) % 2, :], bank[2 * ((ls * J + j) % 2) + 1][:],
                                             ACT.Silu).then_inc(f["act"], 1)
                        act.wait_ge(f["hid"], t + 1)
                        if not (first and ls < 2):
                            act.wait_ge(f["y"], (step_no(it, ls) - 1) * 2)
                        nc.scalar.activation(hid_hi[:, ls % 2, j, :], hid[:, (ls * J + j) % 2, :],
                                             ACT.Copy).then_inc(f["hhi"], 1)

            act.wait_ge(s_set, 5)
            act.wait_ge(s_vset, 2)
            for l in range(2):
                a, f, J = AT[l], FF[l], JT[l]
                for w in range(NW[l]):
                    act.wait_ge(a[f"aw_in{w % 2}"], 16 * (w // 2 + 1))
                    nc.scalar.activation(aw_hi[:, w].rearrange("p k d -> p (k d)"), aw_raw[:, w % 2, :],
                                         ACT.Copy).then_inc(a["aw_hi"], 1)
                ln_act(LN[2 * l])

                def context_high(m):
                    act.wait_ge(a["ctx_in"], m * 16 + 16)
                    nc.scalar.activation(ctx_hi[:], ctx_raw[:], ACT.Copy).then_inc(a["ctx_hi"], 1)

                def unit_high(m, i):
                    if l == 1:
                        act.wait_ge(a["proj"], m * 4 + (i + 1))
                        if i >= 2:
                            act.wait_ge(a["qklo"], m * 4 + (i - 1))
                        nc.scalar.activation(qk[:, i % 2, :], bank[2 * (i % 2)][:], ACT.Identity,
                                             bias=bias_col[l][:, i:i + 1],
                                             scale=0.25 if i >= 2 else 1.0).then_inc(a["qk"], 1)
                    act.wait_ge(a["qk"], m * 4 + (i + 1))
                    dst = k_parts if i < 2 else q_parts
                    nc.scalar.activation(dst[:, 0, i % 2, :], qk[:, i % 2, :], ACT.Copy).then_inc(a["qkhi"], 1)

                def values_high(m):
                    for h in range(2):
                        act.wait_ge(a["v32"], m * 2 + (h + 1))
                        nc.scalar.activation(
                            v_parts[:, 2 * h:2 * h + 2].rearrange("p b h w -> p (b h) w")[:, :, 0:16],
                            v32[:, h].rearrange("p b (h d) -> p (b h) d", h=HEADS), ACT.Copy).then_inc(a["vhi"], 1)

                def exps(n, i):
                    b, g = divmod(i, NG)
                    dst = prob[:, i % RING, :]
                    if g % 2 == 0:
                        act.wait_ge(a["sub"], n * 8 + (i // 2 + 1))
                        nc.scalar.activation(dst, dst, ACT.Exp).then_inc(a["exp"], 1)
                    else:
                        act.wait_ge(a["max"], n * GROUPS + (i + 1))
                        for h in range(GRP):
                            last = nc.scalar.activation(dst[:, S * h:S * (h + 1)], bank[g][:, S * h:S * (h + 1)], ACT.Exp,
                                                        bias=nmax[:, b % 2, GRP * g + h:GRP * g + h + 1])
                        last.then_inc(a["exp"], 1)

                def output_copy(n, c):
                    act.wait_ge(a["pv"], n * GROUPS + (2 * c + 2))
                    if c >= 2:
                        act.wait_ge(a["o"], n * 8 + (c - 1))
                    nc.scalar.activation(o_raw[:, c % 2].rearrange("p h w -> p (h w)"),
                                         bank[6 + c % 2][:, 0:8 * VW], ACT.Copy).then_inc(a["ocopy"], 1)

                def attend(n, build):
                    for i in range(GROUPS):
                        if i == 4 and build:
                            context_high(n + 1)
                        act.wait_ge(a["pT"], n * GROUPS + (i + 1))
                        if i >= RINGT:
                            act.wait_ge(a["pv"], n * GROUPS + (i - RINGT + 1))
                        nc.scalar.activation(probT_hi[:, i % RINGT, :], bank[4 + i % 2][:],
                                             ACT.Copy).then_inc(a["phi"], 1)
                        if i + NG < GROUPS:
                            exps(n, i + NG)
                        elif build:
                            unit_high(n + 1, i % NG)
                        if i >= 4 and i % 2 == 0:
                            output_copy(n, i // 2 - 2)
                    output_copy(n, 6)
                    output_copy(n, 7)
                    if build:
                        values_high(n + 1)
                    for k in range(KT):
                        act.wait_ge(a["oT"], n * 2 + (k + 1))
                        nc.scalar.activation(oT_hi[:, k, :], bank[4 + k][:], ACT.Copy).then_inc(a["ohi"], 1)
                    if build:
                        for g in range(NG):
                            exps(n + 1, g)

                context_high(0)
                for i in range(4):
                    unit_high(0, i)
                values_high(0)
                for g in range(NG):
                    exps(0, g)
                with act.Fori(0, NBLK - 1) as n:
                    attend(n, True)
                attend(NBLK - 1, False)
                ln_act(LN[2 * l + 1])
                act.wait_ge(f["rlog"], 1)
                E = NE[l]
                prods = bank[7][:, 0:B * 2 * E].rearrange("p (b c e) -> p b c e", b=B, c=2)
                nc.scalar.activation(logit[:, :, 0:E], prods[:, :, 0, :], ACT.Copy,
                                     scale=LOGIT_SCALE if l == 0 else 1.0).then_inc(f["rcopy"], 1)
                act.wait_ge(f["rfun_in"], 1)
                nc.scalar.activation(rt[1][:, :, 0:E], rt[1][:, :, 0:E],
                                     ACT.Exp if l == 0 else ACT.Sigmoid).then_inc(f["rfun"], 1)
                experts(f, J, 0, True)
                with act.Fori(1, HALF) as it:
                    experts(f, J, it, False)

        @block.vector
        def _(dve):
            def ln_dve(m, ready):
                def low(n):
                    for k in range(KT):
                        dve.wait_ge(m["ln_hi"], 2 * n + k + 1)
                        cols = slice(N * n, N * (n + 1))
                        nc.vector.tensor_tensor(xT_lo[:, k, cols], bank[2 * (n % 2) + k][:],
                                                xT_hi[:, k, cols].bitcast(F32), ALU.subtract).then_inc(m["ln_lo"], 1)

                for n in range(NBLK):
                    ready(n)
                    for t in range(BLK):
                        nc.vector.bn_stats(stats[:, t, :], xres[:, BLK * n + t, :]).then_inc(m["ln_stat"], 1)
                    for t in range(BLK):
                        dve.wait_ge(m["ln_stat"], 4 * n + t + 1)
                        nc.vector.bn_aggr(meanvar[:, n % 2, t, :], stats[:, t, :]).then_inc(m["ln_var"], 1)
                    if n >= 1:
                        low(n - 1)
                    dve.wait_ge(m["ln_std"], n + 1)
                    nc.vector.reciprocal(rstd[:, n % 2, :], std[:, n % 2, :]).then_inc(m["ln_rstd"], 1)
                    dve.wait_ge(m["ln_rstd"], n + 1)
                    for t in range(BLK):
                        nc.vector.tensor_scalar(xn[:, n % 2, t, :], xres[:, BLK * n + t, :],
                                                meanvar[:, n % 2, t, 0:1], rstd[:, n % 2, t:t + 1],
                                                ALU.subtract, ALU.mult).then_inc(m["ln_xn"], 1)
                low(NBLK - 1)

            def route(l, f):
                E, K = NE[l], TOPS[l]
                W = E + 8 - K
                done = [0]

                def link(ins):
                    done[0] += 1
                    ins.then_inc(f["route"], 1)
                    dve.wait_ge(f["route"], done[0])

                V = nc.vector
                lg, a0, a1 = logit[:, :, 0:E], rt[0][:, :, 0:E], rt[1][:, :, 0:E]
                sc, tk = score[:, :, 0:E], taken[:, :, 0:E]
                prods = bank[7][:, 0:B * 2 * E].rearrange("p (b c e) -> p b c e", b=B, c=2)
                bias = route_b[l][:].unsqueeze(1).to_broadcast([P, B, E])
                V.memset(gate[:, UNITS - 2:UNITS, :], 1.0).then_inc(f["rsum"], 1)
                link(V.memset(score[:, :, E:W], -3e38))
                dve.wait_ge(f["rcopy"], 1)
                if l == 0:
                    link(V.scalar_tensor_tensor(out=lg, in0=prods[:, :, 1, :], scalar=LOGIT_SCALE, in1=lg,
                                                op0=ALU.mult, op1=ALU.add))
                    link(V.tensor_tensor(sc, lg, bias, ALU.add))
                else:
                    V.tensor_tensor(a1, prods[:, :, 1, :], lg, ALU.add).then_inc(f["rfun_in"], 1)
                    dve.wait_ge(f["rfun"], 1)
                    link(V.tensor_tensor(lg, a1, bias, ALU.add))
                    quad = logit[:].rearrange("p b (g e) -> p b g e", g=4)
                    best, pair = r1[0][:], r1[1][:]
                    link(V.tensor_tensor(best, quad[:, :, :, 0], quad[:, :, :, 1], ALU.add))
                    for i, j in ((0, 2), (0, 3), (1, 2), (1, 3), (2, 3)):
                        link(V.tensor_tensor(pair, quad[:, :, :, i], quad[:, :, :, j], ALU.add))
                        link(V.tensor_tensor(best, best, pair, ALU.max))
                    beats = rt[0][:].rearrange("p b (g o) -> p b g o", g=4)
                    link(V.tensor_tensor(beats, best.unsqueeze(2).to_broadcast([P, B, 4, 4]),
                                         best.unsqueeze(3).to_broadcast([P, B, 4, 4]), ALU.is_gt))
                    for g in range(1, 4):
                        link(V.tensor_tensor(beats[:, :, g, 0:g], best[:, :, 0:g],
                                             best[:, :, g:g + 1].to_broadcast([P, B, g]), ALU.is_ge))
                    rank, keep = r1[2][:], r1[3][:]
                    link(V.tensor_reduce(rank, beats, AX.X, ALU.add))
                    link(V.tensor_scalar(keep, rank, 2.0, None, ALU.is_lt))
                    link(V.tensor_tensor(score[:, :, 0:E].rearrange("p b (g e) -> p b g e", g=4), quad,
                                         keep.unsqueeze(3).to_broadcast([P, B, 4, 4]), ALU.mult))
                    link(V.tensor_scalar(sc, sc, 0.0, None, ALU.add))
                for t in range(B):
                    ins = V.max(top8[:, t, :], score[:, t, 0:W])
                    ins.then_inc(f["route"], 1)
                    done[0] += 1
                dve.wait_ge(f["route"], done[0])
                link(V.memset(top8[:, :, K:8], -3e38))
                for t in range(B):
                    V.match_replace(taken[:, t, 0:W], top8[:, t, :], score[:, t, 0:W], 3e38).then_inc(f["route"], 1)
                    done[0] += 1
                dve.wait_ge(f["route"], done[0])
                link(V.tensor_tensor(a0, tk, sc, ALU.not_equal))
                total, inv = r1[0][:, :, 0:1], r1[1][:, :, 0:1]
                if l == 0:
                    link(V.tensor_scalar(a1, a0, -1.0, 1e30, ALU.add, ALU.mult))
                    link(V.tensor_tensor(a1, a1, lg, ALU.add))
                    link(V.reduce_max(r1[2][:, :, 0:1], a1, AX.X))
                    V.tensor_tensor(a1, a1, r1[2][:, :, 0:1].to_broadcast([P, B, E]),
                                    ALU.subtract).then_inc(f["rfun_in"], 1)
                    dve.wait_ge(f["rfun"], 1)
                link(V.tensor_tensor(a1, a1, a0, ALU.mult))
                link(V.tensor_reduce(total, a1, AX.X, ALU.add))
                if l == 1:
                    link(V.tensor_scalar(total, total, 1e-20, None, ALU.add))
                link(V.reciprocal(inv, total))
                link(V.tensor_tensor(a1, a1, inv.to_broadcast([P, B, E]), ALU.mult))
                weights = a1.rearrange("p b e -> p e b")
                if l == 0:
                    units = gate[:, 0:2 * E, :].rearrange("p (e u) b -> p e u b", u=2)
                    for u in range(2):
                        link(V.tensor_copy(units[:, :, u, :], weights))
                else:
                    link(V.tensor_scalar(gate[:, 0:E, :], weights, ROUTE_SCALE, None, ALU.mult))
                return done[0]

            def acc(f, it, ls, subs, first):
                par, n = divmod(ls, NBLK)
                for sub in subs:
                    dve.wait_ge(f["y"], step_no(it, ls) * 2 + (sub // 2 + 1))
                    if not (first and ls < NBLK):
                        dve.wait_ge(f["acc"], (step_no(it, ls) - NBLK) * 4 + (sub + 1))
                    rows = xres[:, BLK * n + sub, :]
                    nc.vector.scalar_tensor_tensor(
                        out=rows, in0=bank[4 + 2 * (ls % 2) + sub // 2][:, D * (sub % 2):D * (sub % 2 + 1)],
                        scalar=gate[:, ds(it * 2 + par, 1), BLK * n + sub] if not isinstance(it, int)
                        else gate[:, it * 2 + par, BLK * n + sub:BLK * n + sub + 1],
                        in1=rows, op0=ALU.mult, op1=ALU.add).then_inc(f["acc"], 1)

            def experts(f, J, it, first):
                for ls in range(STEPS):
                    for j in range(J):
                        t, r = tile_no(it, ls, j, J), (ls * J + j) % 2
                        dve.wait_ge(f["act"], t + 1)
                        nc.vector.tensor_tensor(hid[:, r, :], bank[2 * r][:], act_sb[:, r, :],
                                                ALU.mult).then_inc(f["hid"], 1)
                        subs = range(2 * j, 2 * j + 2) if J == 2 else range(BLK)
                        if ls >= 2:
                            acc(f, it, ls - 2, subs, first)
                        elif not first:
                            acc(f, it - 1, ls - 2 + STEPS, subs, False)
                        dve.wait_ge(f["hhi"], t + 1)
                        nc.vector.tensor_tensor(hid_lo[:, ls % 2, j, :], hid[:, r, :],
                                                hid_hi[:, ls % 2, j, :].bitcast(F32),
                                                ALU.subtract).then_inc(f["hlo"], 1)

            dve.wait_ge(s_in, 16 * 13)
            dve.wait_ge(s_set, 4)
            nc.vector.tensor_scalar(mask_b[0:1, :], mask_f, 1.0, -BIG, ALU.not_equal, ALU.mult).then_inc(s_vset, 1)
            nc.vector.tensor_scalar(bias_col[1][:, 2:4], bias_col[1][:, 2:4], 0.25, None, ALU.mult).then_inc(s_vset, 1)
            dve.wait_ge(s_x, 16)
            for l in range(2):
                a, f, J = AT[l], FF[l], JT[l]
                for w in range(NW[l]):
                    dve.wait_ge(a["aw_hi"], w + 1)
                    nc.vector.tensor_tensor(aw_lo[:, w].rearrange("p k d -> p (k d)"), aw_raw[:, w % 2, :],
                                            aw_hi[:, w].rearrange("p k d -> p (k d)").bitcast(F32),
                                            ALU.subtract).then_inc(a["aw_lo"], 1)
                if l == 1:
                    dve.wait_ge(FF[0]["acc"], UNITS * NBLK * BLK)
                ln_dve(LN[2 * l], lambda n: None)

                def unit_build(m, i):
                    r = i % 2
                    if l == 0:
                        dve.wait_ge(a["proj"], m * 4 + (i + 1))
                        if i >= 2:
                            dve.wait_ge(a["qklo"], m * 4 + (i - 1))
                        for c, dst in enumerate((qk, rope_b)):
                            nc.vector.scalar_tensor_tensor(
                                out=dst[:, r].rearrange("p (b s) -> p b s", b=BLK),
                                in0=bank[2 * r + c][:].rearrange("p (b s) -> p b s", b=BLK),
                                scalar=bias_col[l][:, 4 * c + i:4 * c + i + 1],
                                in1=rope_tab[:, i // 2, c].unsqueeze(1).to_broadcast([P, BLK, S]),
                                op0=ALU.add, op1=ALU.mult).then_inc(a["rope"], 1)
                        dve.wait_ge(a["rope"], m * 8 + 2 * (i + 1))
                        nc.vector.tensor_tensor(qk[:, r, :], qk[:, r, :], rope_b[:, r, :],
                                                ALU.add).then_inc(a["qk"], 1)

                def unit_low(m, i):
                    r, dst = i % 2, k_parts if i < 2 else q_parts
                    dve.wait_ge(a["qkhi"], m * 4 + (i + 1))
                    nc.vector.tensor_tensor(dst[:, 1, r, :], qk[:, r, :], dst[:, 0, r, :].bitcast(F32),
                                            ALU.subtract).then_inc(a["qklo"], 1)

                def values(m):
                    for h in range(2):
                        dve.wait_ge(a["vps"], m * 2 + (h + 1))
                        nc.vector.tensor_tensor(v32[:, h], bank[h][:].rearrange("p (b d) -> p b d", b=2),
                                                bv_row[l][:].unsqueeze(1).to_broadcast([P, 2, D]),
                                                ALU.add).then_inc(a["v32"], 1)

                def shifted(n, i):
                    b, g = divmod(i, NG)
                    dve.wait_ge(a["score"], n * GROUPS + (i + 1))
                    grp = bank[g][:].rearrange("p (h t) -> p h t", h=GRP)
                    mx = nmax[:, b % 2, GRP * g:GRP * (g + 1)]
                    nc.vector.tensor_reduce(mx, grp, AX.X, ALU.max, negate=True).then_inc(a["max"], 1)
                    if g % 2 == 0:
                        dve.wait_ge(a["max"], n * GROUPS + (i + 1))
                        nc.vector.tensor_tensor(prob[:, i % RING, :].rearrange("p (h t) -> p h t", h=GRP), grp,
                                                mx.unsqueeze(2).to_broadcast([P, GRP, S]),
                                                ALU.add).then_inc(a["sub"], 1)

                def denominators(n, c):
                    dve.wait_ge(a["ocopy"], n * 8 + (c + 1))
                    nc.vector.reciprocal(rden[:, c % 2, :], o_raw[:, c % 2, :, HD]).then_inc(a["rden"], 1)

                def attend(n, build):
                    for i in range(GROUPS):
                        if i + NG < GROUPS:
                            shifted(n, i + NG)
                        elif build:
                            unit_build(n + 1, i % NG)
                        dve.wait_ge(a["phi"], n * GROUPS + (i + 1))
                        nc.vector.tensor_tensor(probT_lo[:, i % RINGT, :], bank[4 + i % 2][:],
                                                probT_hi[:, i % RINGT, :], ALU.subtract).then_inc(a["plo"], 1)
                        if i + NG >= GROUPS and build:
                            unit_low(n + 1, i % NG)
                        if i >= 5 and i % 2 == 1:
                            denominators(n, (i - 5) // 2)
                    denominators(n, 6)
                    denominators(n, 7)
                    if build:
                        values(n + 1)
                    for k in range(KT):
                        dve.wait_ge(a["ohi"], n * 2 + (k + 1))
                        nc.vector.tensor_tensor(oT_lo[:, k, :], bank[4 + k][:], oT_hi[:, k, :].bitcast(F32),
                                                ALU.subtract).then_inc(a["olo"], 1)
                    if build:
                        for g in range(NG):
                            shifted(n + 1, g)
                    dve.wait_ge(a["xbo"], n + 1)
                    for h in range(2):
                        dve.wait_ge(a["wo"], n * 2 + (h + 1))
                        rows = xres[:, ds(n * BLK + 2 * h, 2), :] if not isinstance(n, int) else \
                            xres[:, n * BLK + 2 * h:n * BLK + 2 * h + 2, :]
                        nc.vector.tensor_tensor(rows, bank[6 + h][:].rearrange("p (b d) -> p b d", b=2), rows,
                                                ALU.add).then_inc(a["xadd"], 1)

                for i in range(4):
                    unit_build(0, i)
                    unit_low(0, i)
                values(0)
                for g in range(NG):
                    shifted(0, g)
                with dve.Fori(0, NBLK - 1) as n:
                    attend(n, True)
                attend(NBLK - 1, False)
                ln_dve(LN[2 * l + 1], lambda n: dve.wait_ge(a["xadd"], 2 * n + 2))
                dve.wait_ge(f["rlog"], 1)
                route(l, f)
                experts(f, J, 0, True)
                with dve.Fori(1, HALF) as it:
                    experts(f, J, it, False)
                for ls in range(STEPS - 2, STEPS):
                    acc(f, HALF - 1, ls, range(BLK), False)

        @block.tensor
        def _(pe):
            def ln_pe(m):
                for n in range(NBLK):
                    pe.wait_ge(m["ln_xn"], 4 * n + 4)
                    if n >= 2:
                        pe.wait_ge(m["ln_lo"], 2 * n - 2)
                    for k in range(KT):
                        for t in range(BLK):
                            last = nc.tensor.transpose(bank[2 * (n % 2) + k][:, P * t:P * (t + 1)],
                                                       xn[:, n % 2, t, P * k:P * (k + 1)], ident[:])
                        last.then_inc(m["ln_T"], 1)

            def products(dst, left, right, finish=True):
                pairs = [(lh, rh) for k in range(KT)
                         for lh, rh in ((left[0](k), right[0](k)), (left[1](k), right[0](k)),
                                        (left[0](k), right[1](k)))]
                for i, (lh, rh) in enumerate(pairs):
                    last = nc.tensor.matmul(dst, lh, rh, start=(i == 0), stop=(i == len(pairs) - 1))
                return last

            def up(l, f, J, it, ls, first):
                par, n = divmod(ls, NBLK)
                if n == 0:
                    pe.wait_ge(f["w_lo"], it * 2 + (par + 1))
                for j in range(J):
                    r = (ls * J + j) % 2
                    if not (first and ls * J + j < 2):
                        pe.wait_ge(f["hid"], tile_no(it, ls, j, J) - 1)
                    for c in range(2):
                        def w(part):
                            return lambda k: part[par][:, (c * KT + k) * P * J + P * j:(c * KT + k) * P * J + P * (j + 1)]
                        cols = slice(N * n, N * (n + 1))
                        last = products(bank[2 * r + c][:], (w(w_hi), w(w_lo)),
                                        (lambda k: xT_hi[:, k, cols], lambda k: xT_lo[:, k, cols]))
                    last.then_inc(f["up"], 1)

            def down(f, J, it, ls, first):
                par = ls // NBLK
                pe.wait_ge(f["hlo"], tile_no(it, ls, J, J))
                if not (first and ls < 2):
                    pe.wait_ge(f["acc"], (step_no(it, ls) - 1) * 4)
                for sub in range(BLK):
                    rows = slice(P * sub, P * (sub + 1))
                    pairs = []
                    for j in range(J):
                        cols = slice(4 * P * J + D * j, 4 * P * J + D * (j + 1))
                        hh, hl = hid_hi[:, ls % 2, j, rows], hid_lo[:, ls % 2, j, rows]
                        wh, wl = w_hi[par][:, cols], w_lo[par][:, cols]
                        pairs += [(hh, wh), (hl, wh), (hh, wl)]
                    dst = bank[4 + 2 * (ls % 2) + sub // 2][:, D * (sub % 2):D * (sub % 2 + 1)]
                    for i, (h, w) in enumerate(pairs):
                        last = nc.tensor.matmul(dst, h, w, start=(i == 0), stop=(i == len(pairs) - 1))
                    if sub % 2:
                        last.then_inc(f["y"], 1)

            def experts(l, f, J, it, first, final):
                for ls in range(STEPS):
                    if ls + 1 < STEPS:
                        up(l, f, J, it, ls + 1, first)
                    elif not final:
                        up(l, f, J, it + 1, 0, False)
                    down(f, J, it, ls, first)

            pe.wait_ge(s_in, 16 * 13)
            for l in range(2):
                a, f, J = AT[l], FF[l], JT[l]
                ln_pe(LN[2 * l])
                pe.wait_ge(LN[2 * l]["ln_lo"], 2 * NBLK)
                pe.wait_ge(a["aw_lo"], NW[l])
                pe.wait_ge(s_vset, 2)
                pe.wait_ge(s_set, 5)

                def block_cols(n):
                    return slice(n * N, n * N + N) if isinstance(n, int) else ds(n * N, N)

                def unit(m, i, first):
                    if i == 0:
                        pe.wait_ge(a["ctx_lo"], m + 1)
                    if i >= 2:
                        pe.wait_ge(a["qk"], m * 4 + (i - 1))
                    elif not first:
                        pe.wait_ge(a["exp"], (m - 1) * GROUPS + (14 + 2 * i))
                    for c, w in enumerate(UNIT_W[l][i]):
                        def wt(part):
                            return lambda k: part[:, w, k, P * (i % 2):P * (i % 2 + 1)]
                        if i < 2:
                            right = (lambda k: ctx_hi[:, k, :], lambda k: ctx_lo[:, k, :])
                        else:
                            right = (lambda k: xT_hi[:, k, block_cols(m)], lambda k: xT_lo[:, k, block_cols(m)])
                        last = products(bank[2 * (i % 2) + c][:], (wt(aw_hi), wt(aw_lo)), right)
                    last.then_inc(a["proj"], 1)

                def values(m):
                    pe.wait_ge(a["qk"], m * 4 + 3)
                    for b in range(BLK):
                        rows = slice(P * b, P * (b + 1))
                        last = products(bank[b // 2][:, D * (b % 2):D * (b % 2 + 1)],
                                        (lambda k: ctx_hi[:, k, rows], lambda k: ctx_lo[:, k, rows]),
                                        (lambda k: aw_hi[:, V_W[l], k, :], lambda k: aw_lo[:, V_W[l], k, :]))
                        if b % 2:
                            last.then_inc(a["vps"], 1)

                def scores(n, i):
                    b, g = divmod(i, NG)
                    if i == 0:
                        pe.wait_ge(a["qklo"], n * 4 + 4)
                        pe.wait_ge(a["v32"], n * 2 + 2)
                    if b >= 1 and g % 2 == 0:
                        pe.wait_ge(a["sub"], n * 8 + (i - NG) // 2 + 1)
                    elif b >= 1:
                        pe.wait_ge(a["exp"], n * GROUPS + (i - NG + 1))
                    if g == 0:
                        pe.wait_ge(a[f"kdma{b % 2}"], n * 256 + (b // 2 + 1) * 128)
                    q = [q_parts[:, part, g // 2, S * b:S * (b + 1)] for part in range(2)]
                    k = [kexp[b % 2][:, part, g].rearrange("p h t -> p (h t)") for part in range(2)]
                    nc.tensor.matmul(bank[g][:], q[0], k[0], start=True, stop=False)
                    nc.tensor.matmul(bank[g][:], q[1], k[0], start=False, stop=False)
                    last = nc.tensor.matmul(bank[g][:], q[0], k[1], start=False, stop=(l == 0))
                    if l == 1:
                        cols = ds((n * BLK + b) * S, S) if not isinstance(n, int) else \
                            slice((n * BLK + b) * S, (n * BLK + b + 1) * S)
                        row = mask_b[:, cols].unsqueeze(1).to_broadcast([P, GRP, S])
                        last = nc.tensor.matmul(bank[g][:].rearrange("p (h t) -> p h t", h=GRP), first_row[:], row,
                                                start=False, stop=True)
                    last.then_inc(a["score"], 1)

                def turned(n, i):
                    pe.wait_ge(a["exp"], n * GROUPS + (i + 1))
                    if i >= 2:
                        pe.wait_ge(a["plo"], n * GROUPS + (i - 1))
                    for h in range(GRP):
                        last = nc.tensor.transpose(bank[4 + i % 2][:, S * h:S * (h + 1)],
                                                   prob[:, i % RING, S * h:S * (h + 1)], ident[:])
                    last.then_inc(a["pT"], 1)

                def weighed(n, i):
                    b, g = divmod(i, NG)
                    pe.wait_ge(a["plo"], n * GROUPS + (i + 1))
                    if i == 0:
                        pe.wait_ge(a["vlo"], n * 2 + 2)
                    if b >= 1 and g % 2 == 0:
                        pe.wait_ge(a["ocopy"], n * 8 + (2 * b - 2 + g // 2 + 1))
                    for h in range(GRP):
                        at_col = VW * (GRP * (g % 2) + h)
                        for part, p in enumerate((probT_hi, probT_lo)):
                            last = nc.tensor.matmul(bank[6 + g // 2][:, at_col:at_col + VW],
                                                    p[:, i % RINGT, S * h:S * (h + 1)],
                                                    v_parts[:, b, GRP * g + h, :], start=(part == 0), stop=(part == 1))
                    last.then_inc(a["pv"], 1)

                def attend(n, build):
                    for i in range(GROUPS):
                        if i + NG < GROUPS:
                            scores(n, i + NG)
                        elif build:
                            unit(n + 1, i % NG, False)
                        turned(n, i)
                        if i >= 2:
                            weighed(n, i - 2)
                    weighed(n, GROUPS - 2)
                    weighed(n, GROUPS - 1)
                    if build:
                        values(n + 1)
                    pe.wait_ge(a["plo"], n * GROUPS + GROUPS)
                    pe.wait_ge(a["o"], n * 8 + 8)
                    for k in range(KT):
                        for b in range(BLK):
                            src = o_sb[:, b, 8 * k:8 * (k + 1), :].rearrange("p h d -> p (h d)")
                            last = nc.tensor.transpose(bank[4 + k][:, P * b:P * (b + 1)], src, ident[:])
                        last.then_inc(a["oT"], 1)
                    if build:
                        for g in range(NG):
                            scores(n + 1, g)
                    pe.wait_ge(a["olo"], n * 2 + 2)
                    for b in range(BLK):
                        rows = slice(P * b, P * (b + 1))
                        last = products(bank[6 + b // 2][:, D * (b % 2):D * (b % 2 + 1)],
                                        (lambda k: oT_hi[:, k, rows], lambda k: oT_lo[:, k, rows]),
                                        (lambda k: aw_hi[:, O_W[l], k, :], lambda k: aw_lo[:, O_W[l], k, :]))
                        if b % 2:
                            last.then_inc(a["wo"], 1)

                for i in range(4):
                    unit(0, i, True)
                values(0)
                for g in range(NG):
                    scores(0, g)
                with pe.Fori(0, NBLK - 1) as n:
                    attend(n, True)
                attend(NBLK - 1, False)
                ln_pe(LN[2 * l + 1])
                pe.wait_ge(LN[2 * l + 1]["ln_lo"], 2 * NBLK)
                pe.wait_ge(s_wsplit[l], 2)
                E = NE[l]
                for t in range(B):
                    rows = slice(P * t, P * (t + 1))
                    pairs = [(p[:, k, rows], k) for k in range(KT) for p in (xT_hi, xT_lo)]
                    for i, (p, k) in enumerate(pairs):
                        last = nc.tensor.matmul(bank[7][:, 2 * E * t:2 * E * (t + 1)], p,
                                                route_wr[l][:, k].rearrange("p c e -> p (c e)"),
                                                start=(i == 0), stop=(i == len(pairs) - 1))
                last.then_inc(f["rlog"], 1)
                up(l, f, J, 0, 0, True)
                pe.wait_ge(f["rfun"], 1)
                experts(l, f, J, 0, True, False)
                with pe.Fori(1, HALF - 1) as it:
                    experts(l, f, J, it, False, False)
                experts(l, f, J, HALF - 1, False, True)



def kernel(**inputs):
    import concourse.bacc as bacc
    from concourse import mybir as _mybir
    from concourse.bass_utils import run_bass_kernel_spmd

    a = {k: np.asarray(v) for k, v in inputs.items()}

    def tiles(w):
        return w.reshape(w.shape[0] // P, P, w.shape[1]).transpose(1, 0, 2)

    def flat(w):
        t = tiles(w)
        return t.reshape(P, -1)

    partner = np.arange(D) ^ 1
    arrays = {"x": a["x"]}
    arrays["ctxT"] = tiles(a["ctx_1024"].reshape(TOK, D).T)
    arrays["maskrow"] = a["mask_BxS2_ff1"].reshape(1, TOK)
    freq = 1.0 / 10000.0 ** (np.arange(0, HD, 2, dtype=np.float32) / HD)
    angle = (np.arange(S, dtype=np.float32)[:, None] * freq[None, :].astype(np.float32)).astype(np.float32)
    row = np.arange(P) % HD
    sign = np.where(row % 2 == 0, -1.0, 1.0).astype(np.float32)
    cos, sin = np.cos(angle).T[row // 2], np.sin(angle).T[row // 2] * sign[:, None]
    arrays["tab"] = np.stack([cos, sin, cos * np.float32(0.25), sin * np.float32(0.25)],
                             axis=1).reshape(P, 2, 2, S)
    arrays["ident"] = np.eye(P, dtype=np.float32)
    for l in range(2):
        w = {n: a[f"L{l}_xattn_W{n}"].T for n in "qkvo"}
        b = {n: a[f"L{l}_xattn_b{n}"] for n in "qkvo"}
        ws = [w["q"], w["q"][:, partner], w["k"], w["k"][:, partner], w["v"], w["o"]] if l == 0 else \
            [w[n] for n in "qkvo"]
        arrays[f"aw{l}"] = np.stack([flat(v) for v in ws], axis=1)
        cols = [b["k"], b["q"], b["k"][partner], b["q"][partner]]
        arrays[f"ab{l}"] = np.concatenate([c.reshape(KT, P).T for c in cols], axis=1)
        arrays[f"arow{l}"] = np.stack([b["v"], b["o"]])
    arrays["rw0"] = tiles(a["L0_ffn_Wr"])
    arrays["rw1"] = tiles(a["L1_ffn_router_weight"].T)
    arrays["rrow0"] = a["L0_ffn_rb"].reshape(1, E0)
    arrays["rrow1"] = a["L1_ffn_e_bias"].reshape(1, E1)

    def unit(linear, gated, out):
        return np.concatenate([flat(linear), flat(gated), flat(out)], axis=1)

    W1 = list(a["L0_ffn_W1"]) + [a["L0_ffn_Ws1"]]
    W2 = list(a["L0_ffn_W2"]) + [a["L0_ffn_Ws2"]]
    W3 = list(a["L0_ffn_W3"]) + [a["L0_ffn_Ws3"]]
    arrays["fw0"] = np.stack([unit(W1[u // 2][:, h], W3[u // 2][:, h], W2[u // 2][h, :])
                              for u in range(UNITS) for h in (slice(256 * (u % 2), 256 * (u % 2) + 256),)])
    parts = [(a["L1_ffn_up_w"][e], a["L1_ffn_gate_w"][e], a["L1_ffn_down_w"][e]) for e in range(E1)]
    for h in (slice(0, P), slice(P, 2 * P)):
        parts.append((a["L1_ffn_sh_up_w"][h], a["L1_ffn_sh_gate_w"][h], a["L1_ffn_sh_down_w"][:, h]))
    arrays["fw1"] = np.stack([unit(u.T, g.T, d.T) for u, g, d in parts])

    nc = bacc.Bacc("TRN2", target_bir_lowering=False, num_devices=1)
    arrays = {f"in_{k}": np.ascontiguousarray(v) for k, v in arrays.items()}
    ap = {k[3:]: nc.dram_tensor(k, v.shape, _mybir.dt.from_np(v.dtype), kind="ExternalInput").ap()
          for k, v in arrays.items()}
    out = nc.dram_tensor("out_x", (B, S, D), _mybir.dt.float32, kind="ExternalOutput").ap()
    program(nc, ap["x"], ap["ctxT"], ap["maskrow"], ap["tab"], ap["ident"],
            [ap["aw0"], ap["aw1"]], [ap["ab0"], ap["ab1"]], [ap["arow0"], ap["arow1"]],
            [ap["rw0"], ap["rw1"]], [ap["rrow0"], ap["rrow1"]], [ap["fw0"], ap["fw1"]], out)
    r = run_bass_kernel_spmd(nc, [arrays], core_ids=[0])
    return r.results[0]["out_x"]
```

```python
from contextlib import ExitStack

import numpy as np

import concourse.bass as bass
from concourse import mybir

B, S, D = 16, 128, 256
HEADS, HD = 16, 16
P = 128
KT = D // P
BLK = 4
NBLK = B // BLK
TOK = B * S
N = BLK * S
GRP = 4
NG = HEADS // GRP
VW = 50
RING, RINGT = 6, 3
E0, E1 = 8, 16
TOP0, TOP1 = 2, 4
UNITS = 18
EPS = 1e-5
LOGIT_SCALE = 1.0 / 16.0
ROUTE_SCALE = 2.5
TILE = 256
TILES = (TOK * TOP0 + E0 * (TILE - 1)) // TILE
XW = D + 2
SHARED = UNITS - 2
BIG = 3.3895313892515355e38


def program(nc, x, ctxT, maskrow, tab_in, ident_in, aw, ab, arow, rw, rrow, fw, sort_in, empty_in, sorted_x, summed, out):
    F32, F32R = mybir.dt.float32, mybir.dt.float32r
    F16, BF16, I32 = mybir.dt.float16, mybir.dt.bfloat16, mybir.dt.int32
    ALU, ACT = mybir.AluOpType, mybir.ActivationFunctionType
    AX = mybir.AxisListType
    ds = bass.ds

    ctx = ExitStack()
    with ctx:
        def sb(stack, name, shape, dt):
            return stack.enter_context(nc.sbuf_tensor(name, shape, dt))

        def sem(name):
            return ctx.enter_context(nc.semaphore(name))

        xres = sb(ctx, "xres", [P, B, D], F32)
        xT_hi = sb(ctx, "xT_hi", [P, KT, TOK], F32R)
        xT_lo = sb(ctx, "xT_lo", [P, KT, TOK], F32R)
        ident = sb(ctx, "ident", [P, P], F32)
        stats = sb(ctx, "stats", [P, 2, BLK, 6], F32)
        meanvar = sb(ctx, "meanvar", [P, NBLK, BLK, 2], F32)
        std = sb(ctx, "std", [P, NBLK, BLK], F32)
        rstd = sb(ctx, "rstd", [P, NBLK, BLK], F32)
        shift = sb(ctx, "shift", [P, NBLK, BLK], F32)
        eps_col = sb(ctx, "eps_col", [P, 1], F32)
        zero_col = sb(ctx, "zero_col", [P, 1], F32)
        rope_tab = sb(ctx, "rope_tab", [P, 2, 2, S], F32)
        empty_row = sb(ctx, "empty_row", [P, 2, XW], F32)
        first_row = sb(ctx, "first_row", [P, P], BF16)
        mask_b = sb(ctx, "mask_b", [P, B * S], BF16)
        bias_col = [sb(ctx, f"bias_col{l}", [P, 8], F32) for l in range(2)]
        bv_row = [sb(ctx, f"bv_row{l}", [P, D], F32) for l in range(2)]
        bo_row = [sb(ctx, f"bo_row{l}", [P, D], F32) for l in range(2)]
        NE, TOPS = [E0, E1], [TOP0, TOP1]
        route_w = [sb(ctx, f"route_w{l}", [P, KT, NE[l]], F32) for l in range(2)]
        route_wr = [sb(ctx, f"route_wr{l}", [P, KT, 2, NE[l]], F32R) for l in range(2)]
        route_b = [sb(ctx, f"route_b{l}", [P, NE[l]], F32) for l in range(2)]
        EW = E1 + 8
        logit = sb(ctx, "logit", [P, B, E1], F32)
        score = sb(ctx, "score", [P, B, EW], F32)
        taken = sb(ctx, "taken", [P, B, EW], F32)
        top8 = sb(ctx, "top8", [P, B, 8], F32)
        rt = [sb(ctx, f"rt{i}", [P, B, E1], F32) for i in range(2)]
        r1 = [sb(ctx, f"r1_{i}", [P, B, 4], F32) for i in range(4)]
        gate = sb(ctx, "gate", [P, UNITS, B], F32)

        tile_to = sb(ctx, "tile_to", [P, TILES, 2], I32)

        at = ExitStack()
        ctx_raw = sb(at, "ctx_raw", [P, KT, N], F32)
        ctx_hi = sb(at, "ctx_hi", [P, KT, N], F32R)
        ctx_lo = sb(at, "ctx_lo", [P, KT, N], F32R)
        aw_hi = sb(at, "aw_hi", [P, 6, KT, D], F32R)
        aw_lo = sb(at, "aw_lo", [P, 6, KT, D], F32R)
        rope_b = sb(at, "rope_b", [P, 2, N], F32)
        qk = sb(at, "qk", [P, 2, N], F32)
        k_parts = sb(at, "k_parts", [P, 2, KT, N], F32R)
        kexp = [sb(at, f"kexp{i}", [P, 2, NG, GRP, S], F32R) for i in range(2)]
        v32 = sb(at, "v32", [P, 2, 2, D], F32)
        v_parts = sb(at, "v_parts", [P, BLK, HEADS, VW], BF16)
        q_parts = sb(at, "q_parts", [P, 2, KT, N], F32R)
        probT_hi = sb(at, "probT_hi", [P, RINGT, N], F16)
        probT_lo = sb(at, "probT_lo", [P, RINGT, N], F16)
        nmax = sb(at, "nmax", [P, 2, HEADS], F32)
        rden = sb(at, "rden", [P, 2, HEADS // 2], F32)
        o_raw = sb(at, "o_raw", [P, 2, HEADS // 2, VW], F32)
        o_sb = sb(at, "o_sb", [P, BLK, HEADS, HD], F32)
        oT_hi = sb(at, "oT_hi", [P, KT, N], F32R)
        oT_lo = sb(at, "oT_lo", [P, KT, N], F32R)
        st = ExitStack()
        prob = sb(st, "prob", [P, RING, N], F32)
        st.close()
        xn = sb(at, "xn", [P, 2, BLK, D], F32)
        mask_f = xn[0:1].rearrange("p a b d -> p (a b d)")
        aw_raw = sb(at, "aw_raw", [P, 2, KT * D], F32)
        at.close()
        ft = ExitStack()
        w_raw = sb(ft, "w_raw", [P, 4, 1536], F32)
        w_hi = [sb(ft, f"w_hi{i}", [P, 1536], F32R) for i in range(2)]
        y_sb = sb(ft, "y_sb", [P, 2, 2, D], F32)
        w_lo = [sb(ft, f"w_lo{i}", [P, 1536], F32R) for i in range(2)]
        w_hi4 = [sb(ft, f"w_hi{i}", [P, 1536], F32R) for i in (2, 3)] + w_hi
        w_lo4 = [sb(ft, f"w_lo{i}", [P, 1536], F32R) for i in (2, 3)] + w_lo
        w_raw4 = [w_raw[:, i, :] for i in (2, 3, 0, 1)]
        xs = sb(ft, "xs", [P, 2, 2, XW], F32)
        xsT_hi = sb(ft, "xsT_hi", [P, 2, KT, TILE], F32R)
        xsT_lo = sb(ft, "xsT_lo", [P, 2, KT, TILE], F32R)
        act_sb = sb(ft, "act_sb", [P, 2, N], F32)
        hid = sb(ft, "hid", [P, 2, N], F32)
        xn_all = sb(ft, "xn_all", [P, B, XW], F32)
        hid_hi = sb(ft, "hid_hi", [P, 2, 2, N], F32R)
        hid_lo = sb(ft, "hid_lo", [P, 2, 2, N], F32R)
        sort_c = sb(ft, "sort_c", [P, P + E0 + E0 * E0 + TILES + 1 + B], F32)
        before_bf = sb(ft, "before_bf", [P, P], BF16)
        ones_bf = sb(ft, "ones_bf", [P, P], BF16)
        pick_bf = sb(ft, "pick_bf", [P, B + 1, E0], BF16)
        rank_sb = sb(ft, "rank_sb", [P, (B + 1) * E0], F32)
        pos = sb(ft, "pos", [P, B, E0], F32)
        pos1 = sb(ft, "pos1", [P, B, E0], F32)
        hit = sb(ft, "hit", [P, B, E0], F32)
        pair_pos = sb(ft, "pair_pos", [P, 2, B], F32)
        cmp_e = sb(ft, "cmp_e", [P, E0, E0], F32)
        ntile = sb(ft, "ntile", [P, 3, E0], F32)
        cmp_t = sb(ft, "cmp_t", [P, TILES, E0], F32)
        of_tile = sb(ft, "of_tile", [P, TILES], F32)
        place = sb(ft, "place", [P, 2, B], I32)
        place_w = sb(ft, "place_w", [P, 2, B], F32)
        tile_w = sb(ft, "tile_w", [P, TILES, 2], F32)
        w_row = sb(ft, "w_row", [P, 2, TILES], F32)
        w_idx = sb(ft, "w_idx", [P, 2, TILES], I32)
        ft.close()

        bank = [ctx.enter_context(nc.psum_tensor(f"bank{i}", [P, 512], F32)) for i in range(8)]

        s_in = sem("s_in")
        s_ident = sem("s_ident")
        s_first = sem("s_first")
        s_x = [sem(f"s_x{n}") for n in range(NBLK)]
        s_store = sem("s_store")
        s_set = sem("s_set")
        s_vset = sem("s_vset")
        s_rope = sem("s_rope")
        s_wsplit = [sem(f"s_route_split{l}") for l in range(2)]

        def stage_sems(names, l):
            return {n: sem(f"{n}_{l}") for n in names}

        LN = {n: sem(n) for n in ("ln_stat", "ln_var", "ln_std", "ln_rstd", "ln_xn", "ln_T", "ln_hi", "ln_lo")}
        AT = [stage_sems(["aw_in0", "aw_in1", "kdma0", "kdma1", "aw_hi", "aw_lo", "ctx_in", "ctx_hi", "ctx_lo",
                          "proj", "qk", "qkhi", "qklo", "vps", "v32", "vhi", "vones", "vres", "vmid", "vlo",
                          "kzero", "score", "max", "sub", "exp", "pT", "phi", "plo", "pv", "ocopy", "oadd", "rden", "olast",
                          "o", "oT", "ohi", "olo", "wo", "xadd", "xbo"], l)
              for l in range(2)]
        FF = [stage_sems(["w_in0", "w_in1", "w_hi", "w_lo", "up", "act", "hid", "hhi", "hlo", "y", "acc",
                          "route"], l) for l in range(2)]
        RT = {n: sem(n) for n in ("rprod", "rT", "rturn", "rcopy", "rfun_in", "rfun")}

        TS = stage_sems(["const_in", "const", "pick", "rank", "idx", "scatter", "tlabel", "w_in0", "w_in1", "w_hi", "w_lo",
                         "x_in0", "x_in1", "xT", "xhi", "xlo", "up", "act", "hid", "hhi", "hlo", "down", "ycopy",
                         "y_out0", "y_out1", "add"], "tile")
        def ln_bank(m, n, k):
            return (4 if m == 2 else 0) + 2 * (n % 2) + k

        NSORT = P + E0 + E0 * E0 + TILES + 1
        PAIRS = TILES // 2

        NW = [6, 4]
        JT = [2, 1]
        V_W, O_W = [4, 2], [5, 3]
        W_ORDER = [[2, 3, 0, 1, 4, 5], [1, 2, 0, 3]]
        KV_WEIGHTS = 2
        UNIT_W = [[(2, 3), (2, 3), (0, 1), (0, 1)], [(1,), (1,), (0,), (0,)]]
        GROUPS = BLK * NG
        HALF = UNITS // 2
        STEPS = 2 * NBLK

        def step_no(it, ls):
            return it * STEPS + ls

        def tile_no(it, ls, j, J):
            return it * (STEPS * J) + (ls * J + j)

        block = ctx.enter_context(nc.Block())

        @block.sync
        def _(sp):
            for n in range(NBLK):
                sp.dma_start(xres[:, BLK * n:BLK * (n + 1), :],
                             x[BLK * n:BLK * (n + 1)].rearrange("b s d -> s b d")).then_inc(s_x[n], 16)
                if n == 0:
                    sp.dma_start(ident[:], ident_in).then_inc(s_ident, 16)
            sp.dma_start(ctx_raw[:], ctxT[:, :, 0:N]).then_inc(AT[0]["ctx_in"], 16)
            sp.dma_start(aw_raw[:, 0, :], aw[0][:, W_ORDER[0][0], :]).then_inc(AT[0]["aw_in0"], 16)
            sp.dma_start(aw_raw[:, 1, :], aw[0][:, W_ORDER[0][1], :]).then_inc(AT[0]["aw_in1"], 16)
            sp.dma_start(rope_tab[:], tab_in).then_inc(s_first, 16)
            sp.dma_start(bias_col[0][:], ab[0]).then_inc(s_first, 16)
            sp.dma_start(bv_row[0][:], arow[0][0:1, :].to_broadcast([P, D])).then_inc(s_first, 16)

            def later_constants():
                sp.wait_ge(LN["ln_lo"], 2 * NBLK)
                sp.dma_start(mask_f, maskrow).then_inc(s_in, 16)
                sp.dma_start(bo_row[0][:], arow[0][1:2, :].to_broadcast([P, D])).then_inc(s_in, 16)
                sp.dma_start(bias_col[1][:], ab[1]).then_inc(s_in, 16)
                sp.dma_start(bv_row[1][:], arow[1][0:1, :].to_broadcast([P, D])).then_inc(s_in, 16)
                sp.dma_start(bo_row[1][:], arow[1][1:2, :].to_broadcast([P, D])).then_inc(s_in, 16)
                for l in range(2):
                    sp.dma_start(route_w[l][:], rw[l]).then_inc(s_in, 16)
                    sp.dma_start(route_b[l][:], rrow[l].to_broadcast([P, NE[l]])).then_inc(s_in, 16)

            for l in range(2):
                a, f, J = AT[l], FF[l], JT[l]
                if l > 0:
                    sp.wait_ge(TS["w_lo"], 2 * TILES - 2)
                    sp.dma_start(ctx_raw[:], ctxT[:, :, 0:N]).then_inc(a["ctx_in"], 16)
                    sp.wait_ge(TS["ycopy"], TILES)
                for i, w in enumerate(W_ORDER[l]):
                    if l == 0 and i < 2:
                        continue
                    if i >= 2:
                        sp.wait_ge(a["aw_lo"], i - 1)
                    sp.dma_start(aw_raw[:, i % 2, :], aw[l][:, w, :]).then_inc(a[f"aw_in{i % 2}"], 16)
                    if l == 1 and i == 1:
                        for q in range(2):
                            sp.wait_ge(TS[f"y_out{q}"], 32 * ((TILES + 1 - q) // 2))
                        for n in range(NBLK):
                            src = summed[1 + N * n:1 + N * (n + 1), :].rearrange("(b s) d -> s b d", s=S)
                            sp.dma_start(xn_all[:, BLK * n:BLK * (n + 1), 0:D], src).then_inc(s_x[n], 16)
                if l == 0:
                    later_constants()

                def keys(n):
                    sp.wait_ge(a["qklo"], n * 4 + 2)
                    for b in range(BLK):
                        if b >= 2:
                            sp.wait_ge(a["score"], n * GROUPS + (b - 1) * NG)
                        for g2 in range(2):
                            for j in range(GRP):
                                rows = slice(64 * g2 + HD * j, 64 * g2 + HD * (j + 1))
                                src = k_parts[rows, :, :, b * S:(b + 1) * S]
                                dst = kexp[b % 2][rows, :, g2::2, j, :]
                                sp.dma_start(dst.bitcast(F32), src.bitcast(F32)).then_inc(a[f"kdma{b % 2}"], 16)

                sp.wait_ge(a["kzero"], 2)
                with sp.Fori(0, NBLK - 1) as n:
                    sp.wait_ge(a["ctx_lo"], n + 1)
                    sp.dma_start(ctx_raw[:], ctxT[:, :, ds(n * N + N, N)]).then_inc(a["ctx_in"], 16)
                    keys(n)
                keys(NBLK - 1)
                if l == 0:
                    sp.dma_start(empty_row[:], empty_in).then_inc(TS["const_in"], 16)
                    sp.wait_ge(TS["const_in"], 16)
                    for c in range(2):
                        dst = sorted_x.rearrange("(t c p) d -> c p t d", c=2, p=P)[c]
                        src = empty_row[:, c, :].unsqueeze(1).to_broadcast([P, TILES, XW])
                        sp.dma_start(dst, src).then_inc(TS["const_in"], 16)
                    dst = summed[1:1 + TOK + TILE, :].rearrange("(p r) d -> p r d", p=P)
                    src = empty_row[:, 0, 0:D].unsqueeze(1).to_broadcast([P, (TOK + TILE) // P, D])
                    sp.dma_start(dst, src).then_inc(TS["const_in"], 16)
                sp.wait_ge(a["xadd"], 2 * NBLK)
                for par in range(2):
                    sp.dma_start(w_raw[:, par, 0:768 * J], fw[l][par + (0 if l else SHARED), :, :]).then_inc(f[f"w_in{par}"], 16)
                if l == 0:
                    sp.dma_start(sort_c[:], sort_in).then_inc(TS["const_in"], 16)

                    def tile_x(it, q):
                        j = it * 2 + q
                        if not (isinstance(it, int) and it == 0):
                            sp.wait_ge(TS["xT"], j - 1)
                        rows = sorted_x[ds(j * TILE, TILE), :] if not isinstance(it, int) else \
                            sorted_x[j * TILE:(j + 1) * TILE, :]
                        sp.dma_start(xs[:, q], rows.rearrange("(c p) d -> p c d", p=P)).then_inc(TS[f"x_in{q}"], 16)

                    sp.wait_ge(TS["scatter"], 16 * 2 * B)
                    tile_x(0, 0)
                    tile_x(0, 1)
                    with sp.Fori(0, PAIRS - 1) as pair:
                        tile_x(pair + 1, 0)
                        tile_x(pair + 1, 1)
                    if TILES % 2:
                        tile_x(PAIRS, 0)
                    continue
                with sp.Fori(1, HALF) as it:
                    for par in range(2):
                        sp.wait_ge(f["w_lo"], it * 2 + par - 1)
                        src = fw[l][ds(it * 2 + par, 1), :, :].rearrange("u p c -> p (u c)")
                        sp.dma_start(w_raw[:, par, 0:768 * J], src).then_inc(f[f"w_in{par}"], 16)
            sp.wait_ge(FF[1]["acc"], UNITS * NBLK * BLK)
            sp.dma_start(out.rearrange("b s d -> s b d"), xres[:]).then_inc(s_store, 16)
            sp.wait_ge(s_store, 16)

        @block.gpsimd
        def _(pool):
            def add_bias(m, bo, a):
                for n in range(NBLK):
                    pool.wait_ge(LN["ln_xn"], 4 * (NBLK * m + n) + 4)
                    rows = xres[:, BLK * n:BLK * (n + 1), :]
                    nc.gpsimd.tensor_tensor(rows, rows, bo[:].unsqueeze(1).to_broadcast([P, BLK, D]),
                                            ALU.add).then_inc(a["xbo"], 1)

            def split_unit(f, it, par, W):
                pool.wait_ge(f[f"w_in{par}"], it * 16 + 16)
                raw = w_raw[:, par, 0:W]
                nc.gpsimd.tensor_tensor(w_hi[par][:, 0:W], raw, zero_col[:].to_broadcast([P, W]),
                                        ALU.subtract).then_inc(f["w_hi"], 1)
                pool.wait_ge(f["w_hi"], it * 2 + par + 1)
                nc.gpsimd.tensor_tensor(w_lo[par][:, 0:W], w_raw[:, par, 0:W],
                                        w_hi[par][:, 0:W].bitcast(F32), ALU.subtract).then_inc(f["w_lo"], 1)

            def context_low(a, m):
                pool.wait_ge(a["ctx_hi"], m + 1)
                nc.gpsimd.tensor_tensor(ctx_lo[:], ctx_raw[:], ctx_hi[:].bitcast(F32),
                                        ALU.subtract).then_inc(a["ctx_lo"], 1)

            def sorting():
                pool.wait_ge(TS["const_in"], 16 * 5)
                nc.gpsimd.tensor_copy(before_bf[:], sort_c[:, 0:P]).then_inc(TS["const"], 1)
                nc.gpsimd.memset(ones_bf[:], 1.0).then_inc(TS["const"], 1)
                pool.wait_ge(TS["idx"], 1)

                def tile_weights(j, h):
                    if j == 1:
                        pool.wait_ge(FF[0]["w_lo"], 2)
                    elif j > 1:
                        pool.wait_ge(TS["w_lo"], 2 * j + h - 3)
                    if j:
                        pool.wait_ge(TS["w_hi"], 2 * j + h - 1)
                    nc.gpsimd.indirect_dma_start(
                        out=w_raw4[2 * (j % 2) + h], out_offset=None, in_=fw[0].rearrange("u p c -> (u p) c"),
                        in_offset=bass.IndirectOffsetOnAxis(ap=w_idx[:, h, j:j + 1], axis=0),
                        bounds_check=2 * E0 * P - 1, oob_is_err=True).then_inc(TS[f"w_in{h}"], 16)

                for h in range(2):
                    tile_weights(0, h)
                pool.wait_ge(LN["ln_xn"], 2 * B)
                nc.gpsimd.tensor_copy(xn_all[:, :, D], sort_c[:, NSORT:NSORT + B]).then_inc(TS["tlabel"], 1)
                for r in range(2):
                    if r:
                        pool.wait_ge(TS["scatter"], 16 * B)
                    nc.gpsimd.tensor_copy(xn_all[:, :, D + 1], place_w[:, r, :]).then_inc(TS["tlabel"], 1)
                    pool.wait_ge(TS["tlabel"], r + 2)
                    for b in range(B):
                        nc.gpsimd.indirect_dma_start(
                            out=sorted_x, out_offset=bass.IndirectOffsetOnAxis(ap=place[:, r, b:b + 1], axis=0),
                            in_=xn_all[:, b, :], in_offset=None,
                            bounds_check=TILES * TILE - 1, oob_is_err=True).then_inc(TS["scatter"], 16)

                def tile_labels(j):
                    number = xs[:, j % 2, :, D]
                    pool.wait_ge(TS[f"x_in{j % 2}"], 16 * (j // 2 + 1))
                    nc.gpsimd.tensor_copy(tile_w[:, j, :], xs[:, j % 2, :, D + 1]).then_inc(TS["tlabel"], 1)
                    nc.gpsimd.tensor_copy(tile_to[:, j, :], number).then_inc(TS["tlabel"], 1)

                def tile_sum(j):
                    pool.wait_ge(TS["ycopy"], j + 1)
                    pool.wait_ge(TS["tlabel"], 3 + 2 * j + 2)
                    if j:
                        pool.wait_ge(TS[f"y_out{(j - 1) % 2}"], 32 * ((j - 1) // 2 + 1))
                    for c in range(2):
                        nc.gpsimd.indirect_dma_start(
                            out=summed, out_offset=bass.IndirectOffsetOnAxis(ap=tile_to[:, j, c:c + 1], axis=0),
                            in_=y_sb[:, j % 2, c, :], in_offset=None, bounds_check=TOK + TILE, oob_is_err=True,
                            compute_op=ALU.add).then_inc(TS[f"y_out{j % 2}"], 16)

                tile_labels(0)
                for j in range(1, TILES + 3):
                    if j < TILES:
                        for h in range(2):
                            tile_weights(j, h)
                        tile_labels(j)
                    if j >= 3:
                        tile_sum(j - 3)

            nc.gpsimd.memset(first_row[:], 0.0).then_inc(s_set, 1)
            nc.gpsimd.memset(mask_b[:], 0.0).then_inc(s_set, 1)
            nc.gpsimd.memset(eps_col[:], EPS).then_inc(s_set, 1)
            nc.gpsimd.memset(zero_col[:], 0.0).then_inc(s_set, 1)
            pool.wait_ge(s_set, 4)
            nc.gpsimd.memset(first_row[0:1, :], 1.0).then_inc(s_set, 1)
            def split_routers():
                for l in range(2):
                    nc.gpsimd.tensor_copy(route_wr[l][:, :, 0, :], route_w[l][:]).then_inc(s_wsplit[l], 1)
                    pool.wait_ge(s_wsplit[l], 1)
                    nc.gpsimd.tensor_tensor(route_wr[l][:, :, 1, :], route_w[l][:],
                                            route_wr[l][:, :, 0, :].bitcast(F32), ALU.subtract).then_inc(s_wsplit[l], 1)

            for l in range(2):
                a, f = AT[l], FF[l]

                def value_parts(m):
                    for h in range(2):
                        parts = v_parts[:, 2 * h:2 * h + 2].rearrange("p b h w -> p (b h) w")
                        rest = v32[:, h].rearrange("p b (h d) -> p (b h) d", h=HEADS)
                        pool.wait_ge(a["vhi"], m * 2 + (h + 1))
                        nc.gpsimd.tensor_tensor(rest, rest, parts[:, :, 0:16], ALU.subtract).then_inc(a["vres"], 1)
                        pool.wait_ge(a["vres"], m * 2 + (h + 1))
                        nc.gpsimd.tensor_tensor(parts[:, :, 18:34], rest,
                                                zero_col[:].unsqueeze(2).to_broadcast([P, 2 * HEADS, HD]),
                                                ALU.subtract).then_inc(a["vmid"], 1)
                        pool.wait_ge(a["vmid"], m * 2 + (h + 1))
                        nc.gpsimd.tensor_tensor(parts[:, :, 34:50], rest, parts[:, :, 18:34],
                                                ALU.subtract).then_inc(a["vlo"], 1)

                def rotate(m, i):
                    pool.wait_ge(s_rope, m * 8 + 2 * (i + 1))
                    nc.gpsimd.tensor_tensor(qk[:, i % 2, :], qk[:, i % 2, :], rope_b[:, i % 2, :], ALU.add).then_inc(a["qk"], 1)

                def outputs(n, build):
                    for c in range(2 * BLK - 1):
                        if build and l == 0:
                            for i in {4: (0,), 5: (1, 2), 6: (3,)}.get(c, ()):
                                rotate(n + 1, i)
                        raw, dst = o_raw[:, c % 2], o_sb[:, c // 2, 8 * (c % 2):8 * (c % 2) + 8, :]
                        pool.wait_ge(a["ocopy"], n * 8 + (c + 1))
                        nc.gpsimd.tensor_tensor(dst, raw[:, :, 0:16], raw[:, :, 18:34], ALU.add).then_inc(a["oadd"], 1)
                        pool.wait_ge(a["oadd"], n * 14 + (2 * c + 1))
                        nc.gpsimd.tensor_tensor(dst, dst, raw[:, :, 34:50], ALU.add).then_inc(a["oadd"], 1)
                        pool.wait_ge(a["oadd"], n * 14 + (2 * c + 2))
                        pool.wait_ge(a["rden"], n * 8 + (c + 1))
                        nc.gpsimd.tensor_tensor(dst, dst, rden[:, c % 2].unsqueeze(2).to_broadcast([P, 8, HD]),
                                                ALU.mult).then_inc(a["o"], 1)

                nc.gpsimd.memset(v_parts[:, :, :, HD:HD + 2], 1.0).then_inc(a["vones"], 1)
                for i in range(2):
                    nc.gpsimd.memset(kexp[i][:].bitcast(F32), 0.0).then_inc(a["kzero"], 1)
                if l == 0:
                    context_low(a, 0)
                    for i in range(4):
                        rotate(0, i)
                value_parts(0)
                if l == 0:
                    pool.wait_ge(s_in, 16 * 9)
                    split_routers()
                add_bias(2 * l, bo_row[l], a)
                with pool.Fori(0, NBLK - 1) as n:
                    context_low(a, n + 1)
                    outputs(n, True)
                    value_parts(n + 1)
                outputs(NBLK - 1, False)
                pool.wait_ge(a["xadd"], 2 * NBLK)
                for par in range(2):
                    split_unit(f, 0, par, 768 * JT[l])
                if l == 0:
                    sorting()
                    continue
                with pool.Fori(1, HALF) as it:
                    for par in range(2):
                        pool.wait_ge(f["y"], (it * 2 + par - 1) * (2 * NBLK))
                        split_unit(f, it, par, 768 * JT[l])

        @block.scalar
        def _(act):
            def ln_act(m, xn_of=lambda n, t: xn[:, n % 2, t, :]):
                def deviation(n):
                    act.wait_ge(LN["ln_var"], 4 * (NBLK * m + n) + 4)
                    nc.scalar.activation(std[:, n, :], meanvar[:, n, :, 1], ACT.Sqrt,
                                         bias=eps_col[:]).then_inc(LN["ln_std"], 1)

                def router_copy(n):
                    rows = slice(0, 2 * NE[m // 2])
                    act.wait_ge(RT["rprod"], NBLK * (m // 2) + n + 1)
                    if n >= 2:
                        act.wait_ge(RT["rturn"], NBLK * (m // 2) + n - 1)
                    nc.scalar.activation(act_sb[rows, n % 2, :], bank[4 + n % 2][rows, :], ACT.Copy).then_inc(RT["rT"], 1)

                deviation(0)
                for n in range(NBLK + 1):
                    if n < NBLK:
                        act.wait_ge(LN["ln_rstd"], 2 * (NBLK * m + n) + 2)
                        for t in range(BLK):
                            nc.scalar.activation(xn_of(n, t), xres[:, BLK * n + t, :], ACT.Identity,
                                                 bias=shift[:, n, t:t + 1],
                                                 scale=rstd[:, n, t:t + 1]).then_inc(LN["ln_xn"], 1)
                    for k in range(KT if n else 0):
                        act.wait_ge(LN["ln_T"], 2 * (NBLK * m + n) + k - 1)
                        nc.scalar.activation(xT_hi[:, k, N * (n - 1):N * n], bank[ln_bank(m, n - 1, k)][:],
                                             ACT.Copy).then_inc(LN["ln_hi"], 1)
                    if n + 1 < NBLK:
                        deviation(n + 1)
                    if m % 2 and n >= 2:
                        router_copy(n - 2)
                if m % 2:
                    router_copy(NBLK - 1)

            def tile_weights_high(it, s):
                act.wait_ge(TS[f"w_in{s % 2}"], (it * 2 + (s // 2 + 1)) * 16)
                if s == 2 and isinstance(it, int) and it == 0:
                    act.wait_ge(FF[0]["y"], STEPS * 2)
                elif not (isinstance(it, int) and it == 0):
                    act.wait_ge(TS["down"], it * 4 + s - 3)
                nc.scalar.activation(w_hi4[s][:], w_raw4[s], ACT.Copy).then_inc(TS["w_hi"], 1)

            def tile_rows_high(it, q):
                act.wait_ge(TS["xT"], it * 2 + (q + 1))
                if not (isinstance(it, int) and it == 0):
                    act.wait_ge(TS["up"], it * 4 + (2 * q - 2))
                nc.scalar.activation(xsT_hi[:, q].rearrange("p k t -> p (k t)"), bank[4][:], ACT.Copy).then_inc(TS["xhi"], 1)

            def tile_out(it, q):
                act.wait_ge(TS["down"], it * 4 + (2 * q + 2))
                if not (isinstance(it, int) and it == 0):
                    act.wait_ge(TS[f"y_out{q}"], it * 32)
                j = it * 2 + q
                for c in range(2):
                    w = tile_w[:, j, c:c + 1] if isinstance(it, int) else tile_w[:, ds(j, 1), c]
                    last = nc.scalar.activation(y_sb[:, q, c, :], bank[5 + q][:, D * c:D * (c + 1)], ACT.Copy, scale=w)
                last.then_inc(TS["ycopy"], 1)

            def tile_step(it, s, ahead, more, first):
                act.wait_ge(TS["up"], it * 4 + (s + 1))
                nc.scalar.activation(act_sb[:, s % 2, :], bank[2 * (s % 2) + 1][:], ACT.Silu).then_inc(TS["act"], 1)
                if s % 2 == 0 and more:
                    tile_rows_high(it + s // 2, 1 - s // 2)
                act.wait_ge(TS["hid"], it * 4 + (s + 1))
                if not (first and s < 2):
                    act.wait_ge(TS["down"], it * 4 + (s - 1))
                nc.scalar.activation(hid_hi[:, s % 2, 0, :], hid[:, s % 2, :],
                                     ACT.Copy).then_inc(TS["hhi"], 1)
                if ahead:
                    if first and s == 0:
                        tile_weights_high(0, 2)
                    tile_weights_high(it + (s + 3) // 4, (s + 3) % 4)
                if s % 2 == 0 and not (first and s == 0):
                    if s == 0:
                        tile_out(it - 1, 1)
                    else:
                        tile_out(it, 0)

            def experts(f, J, it, first, between=None):
                for ls in range(STEPS):
                    if between:
                        between(ls)
                    for j in range(J):
                        t = tile_no(it, ls, j, J)
                        act.wait_ge(f["up"], t + 1)
                        nc.scalar.activation(act_sb[:, (ls * J + j) % 2, :], bank[2 * ((ls * J + j) % 2) + 1][:],
                                             ACT.Silu).then_inc(f["act"], 1)
                        act.wait_ge(f["hid"], t + 1)
                        if not (first and ls < 2):
                            act.wait_ge(f["y"], (step_no(it, ls) - 1) * 2)
                        nc.scalar.activation(hid_hi[:, ls % 2, j, :], hid[:, (ls * J + j) % 2, :],
                                             ACT.Copy).then_inc(f["hhi"], 1)

            act.wait_ge(s_set, 5)
            for l in range(2):
                a, f, J = AT[l], FF[l], JT[l]

                def weights_high(steps):
                    for i in steps:
                        act.wait_ge(a[f"aw_in{i % 2}"], 16 * (i // 2 + 1))
                        nc.scalar.activation(aw_hi[:, W_ORDER[l][i]].rearrange("p k d -> p (k d)"), aw_raw[:, i % 2, :],
                                             ACT.Copy).then_inc(a["aw_hi"], 1)

                def context_high(m):
                    act.wait_ge(a["ctx_in"], m * 16 + 16)
                    nc.scalar.activation(ctx_hi[:], ctx_raw[:], ACT.Copy).then_inc(a["ctx_hi"], 1)

                def unit_high(m, i):
                    if l == 1:
                        act.wait_ge(a["proj"], m * 4 + (i + 1))
                        if i >= 2:
                            act.wait_ge(a["qklo"], m * 4 + (i - 1))
                        nc.scalar.activation(qk[:, i % 2, :], bank[2 * (i % 2)][:], ACT.Identity,
                                             bias=bias_col[l][:, i:i + 1],
                                             scale=0.25 if i >= 2 else 1.0).then_inc(a["qk"], 1)
                    act.wait_ge(a["qk"], m * 4 + (i + 1))
                    dst = k_parts if i < 2 else q_parts
                    nc.scalar.activation(dst[:, 0, i % 2, :], qk[:, i % 2, :], ACT.Copy).then_inc(a["qkhi"], 1)

                def values_high(m):
                    for h in range(2):
                        act.wait_ge(a["v32"], m * 2 + (h + 1))
                        nc.scalar.activation(
                            v_parts[:, 2 * h:2 * h + 2].rearrange("p b h w -> p (b h) w")[:, :, 0:16],
                            v32[:, h].rearrange("p b (h d) -> p (b h) d", h=HEADS), ACT.Copy).then_inc(a["vhi"], 1)

                def exps(n, i):
                    b, g = divmod(i, NG)
                    dst = prob[:, i % RING, :]
                    if g % 2 == 0:
                        act.wait_ge(a["sub"], n * 8 + (i // 2 + 1))
                        nc.scalar.activation(dst, dst, ACT.Exp).then_inc(a["exp"], 1)
                    else:
                        act.wait_ge(a["max"], n * GROUPS + (i + 1))
                        for h in range(GRP):
                            last = nc.scalar.activation(dst[:, S * h:S * (h + 1)], bank[g][:, S * h:S * (h + 1)], ACT.Exp,
                                                        bias=nmax[:, b % 2, GRP * g + h:GRP * g + h + 1])
                        last.then_inc(a["exp"], 1)

                def output_copy(n, c):
                    act.wait_ge(a["pv"], n * GROUPS + (2 * c + 2))
                    if c >= 2:
                        act.wait_ge(a["o"], n * 8 + (c - 1))
                    nc.scalar.activation(o_raw[:, c % 2].rearrange("p h w -> p (h w)"),
                                         bank[6 + c % 2][:, 0:8 * VW], ACT.Copy).then_inc(a["ocopy"], 1)

                def attend(n, build):
                    for i in range(GROUPS):
                        if i == 4 and build:
                            context_high(n + 1)
                        act.wait_ge(a["pT"], n * GROUPS + (i + 1))
                        if i >= RINGT:
                            act.wait_ge(a["pv"], n * GROUPS + (i - RINGT + 1))
                        nc.scalar.activation(probT_hi[:, i % RINGT, :], bank[4 + i % 2][:],
                                             ACT.Copy).then_inc(a["phi"], 1)
                        if i + NG < GROUPS:
                            exps(n, i + NG)
                        elif build:
                            unit_high(n + 1, i % NG)
                        if i >= 4 and i % 2 == 0:
                            output_copy(n, i // 2 - 2)
                    output_copy(n, 6)
                    output_copy(n, 7)
                    if build:
                        values_high(n + 1)
                    for k in range(KT):
                        act.wait_ge(a["oT"], n * 2 + (k + 1))
                        nc.scalar.activation(oT_hi[:, k, :], bank[4 + k][:], ACT.Copy).then_inc(a["ohi"], 1)
                    if build:
                        for g in range(NG):
                            exps(n + 1, g)

                if l == 0:
                    ln_act(0)
                    context_high(0)
                    weights_high(range(4))
                    unit_high(0, 0)
                    weights_high(range(4, NW[0]))
                    for i in range(1, 4):
                        unit_high(0, i)
                    values_high(0)
                else:
                    context_high(0)
                    weights_high(range(KV_WEIGHTS))
                    ln_act(2)
                    weights_high(range(KV_WEIGHTS, NW[1]))
                    act.wait_ge(s_vset, 2)
                    for i in range(4):
                        unit_high(0, i)
                    values_high(0)
                for g in range(NG):
                    exps(0, g)
                with act.Fori(0, NBLK - 1) as n:
                    attend(n, True)
                attend(NBLK - 1, False)
                ln_act(2 * l + 1, (lambda n, t: xn[:, n % 2, t, :]) if l else (lambda n, t: xn_all[:, BLK * n + t, 0:D]))
                act.wait_ge(RT["rturn"], NBLK * (l + 1))
                E = NE[l]
                prods = bank[7][:, 0:B * 2 * E].rearrange("p (b c e) -> p b c e", b=B, c=2)
                nc.scalar.activation(logit[:, :, 0:E], prods[:, :, 0, :], ACT.Copy,
                                     scale=LOGIT_SCALE if l == 0 else 1.0).then_inc(RT["rcopy"], 1)

                def router_function():
                    act.wait_ge(RT["rfun_in"], l + 1)
                    nc.scalar.activation(rt[1][:, :, 0:E], rt[1][:, :, 0:E],
                                         ACT.Exp if l == 0 else ACT.Sigmoid).then_inc(RT["rfun"], 1)

                def between(ls):
                    if l == 0 and ls == 1:
                        router_function()
                    if ls >= STEPS - 2:
                        tile_weights_high(0, ls - (STEPS - 2))

                if l == 0:
                    experts(f, J, 0, True, between)
                    tile_rows_high(0, 0)
                    for s in range(4):
                        tile_step(0, s, True, True, True)
                    with act.Fori(0, PAIRS - 2) as pair:
                        for s in range(4):
                            tile_step(pair + 1, s, True, True, False)
                    left = TILES % 2
                    for s in range(4):
                        tile_step(PAIRS - 1, s, s < 1 + 2 * left, s == 0 or left, False)
                    if left:
                        for s in range(2):
                            tile_step(PAIRS, s, False, False, False)
                    tile_out(*divmod(TILES - 1, 2))
                    continue
                router_function()
                experts(f, J, 0, True)
                with act.Fori(1, HALF) as it:
                    experts(f, J, it, False)

        @block.vector
        def _(dve):
            def ln_dve(m, ready):
                def statistics(n):
                    ready(n)
                    for t in range(BLK):
                        nc.vector.bn_stats(stats[:, n % 2, t, :], xres[:, BLK * n + t, :]).then_inc(LN["ln_stat"], 1)
                    for t in range(BLK):
                        dve.wait_ge(LN["ln_stat"], 4 * (NBLK * m + n) + t + 1)
                        nc.vector.bn_aggr(meanvar[:, n, t, :], stats[:, n % 2, t, :]).then_inc(LN["ln_var"], 1)

                def low(n):
                    for k in range(KT):
                        dve.wait_ge(LN["ln_hi"], 2 * (NBLK * m + n) + k + 1)
                        cols = slice(N * n, N * (n + 1))
                        nc.vector.tensor_tensor(xT_lo[:, k, cols], bank[ln_bank(m, n, k)][:],
                                                xT_hi[:, k, cols].bitcast(F32), ALU.subtract).then_inc(LN["ln_lo"], 1)

                def scales(n):
                    dve.wait_ge(LN["ln_std"], (NBLK * m + n) + 1)
                    nc.vector.reciprocal(rstd[:, n, :], std[:, n, :]).then_inc(LN["ln_rstd"], 1)
                    dve.wait_ge(LN["ln_rstd"], 2 * (NBLK * m + n) + 1)
                    nc.vector.scalar_tensor_tensor(out=shift[:, n, :], in0=meanvar[:, n, :, 0], scalar=-1.0,
                                                   in1=rstd[:, n, :], op0=ALU.mult, op1=ALU.mult).then_inc(LN["ln_rstd"], 1)

                statistics(0)
                scales(0)
                for n in range(NBLK):
                    if n + 1 < NBLK:
                        statistics(n + 1)
                        scales(n + 1)
                    if n >= 1:
                        low(n - 1)
                low(NBLK - 1)

            def route(l, f):
                E, K = NE[l], TOPS[l]
                W = E + 8 - K
                done = [0]

                def link(ins):
                    done[0] += 1
                    ins.then_inc(f["route"], 1)
                    dve.wait_ge(f["route"], done[0])

                V = nc.vector
                lg, a0, a1 = logit[:, :, 0:E], rt[0][:, :, 0:E], rt[1][:, :, 0:E]
                sc, tk = score[:, :, 0:E], taken[:, :, 0:E]
                prods = bank[7][:, 0:B * 2 * E].rearrange("p (b c e) -> p b c e", b=B, c=2)
                bias = route_b[l][:].unsqueeze(1).to_broadcast([P, B, E])
                link(V.memset(gate[:, 0:2, :], 1.0))
                link(V.memset(score[:, :, E:W], -3e38))
                dve.wait_ge(RT["rcopy"], l + 1)
                if l == 0:
                    link(V.scalar_tensor_tensor(out=lg, in0=prods[:, :, 1, :], scalar=LOGIT_SCALE, in1=lg,
                                                op0=ALU.mult, op1=ALU.add))
                    link(V.tensor_tensor(sc, lg, bias, ALU.add))
                else:
                    V.tensor_tensor(a1, prods[:, :, 1, :], lg, ALU.add).then_inc(RT["rfun_in"], 1)
                    yield
                    dve.wait_ge(RT["rfun"], l + 1)
                    link(V.tensor_tensor(lg, a1, bias, ALU.add))
                    quad = logit[:].rearrange("p b (g e) -> p b g e", g=4)
                    best, pair = r1[0][:], r1[1][:]
                    link(V.tensor_tensor(best, quad[:, :, :, 0], quad[:, :, :, 1], ALU.add))
                    for i, j in ((0, 2), (0, 3), (1, 2), (1, 3), (2, 3)):
                        if (i, j) == (1, 2):
                            yield
                        link(V.tensor_tensor(pair, quad[:, :, :, i], quad[:, :, :, j], ALU.add))
                        link(V.tensor_tensor(best, best, pair, ALU.max))
                    beats = rt[0][:].rearrange("p b (g o) -> p b g o", g=4)
                    link(V.tensor_tensor(beats, best.unsqueeze(2).to_broadcast([P, B, 4, 4]),
                                         best.unsqueeze(3).to_broadcast([P, B, 4, 4]), ALU.is_gt))
                    yield
                    for g in range(1, 4):
                        link(V.tensor_tensor(beats[:, :, g, 0:g], best[:, :, 0:g],
                                             best[:, :, g:g + 1].to_broadcast([P, B, g]), ALU.is_ge))
                    rank, keep = r1[2][:], r1[3][:]
                    link(V.tensor_reduce(rank, beats, AX.X, ALU.add))
                    link(V.tensor_scalar(keep, rank, 2.0, None, ALU.is_lt))
                    link(V.tensor_tensor(score[:, :, 0:E].rearrange("p b (g e) -> p b g e", g=4), quad,
                                         keep.unsqueeze(3).to_broadcast([P, B, 4, 4]), ALU.mult))
                    link(V.tensor_scalar(sc, sc, 0.0, None, ALU.add))
                    yield
                for t in range(B):
                    ins = V.max(top8[:, t, :], score[:, t, 0:W])
                    ins.then_inc(f["route"], 1)
                    done[0] += 1
                dve.wait_ge(f["route"], done[0])
                link(V.memset(top8[:, :, K:8], -3e38))
                if l == 1:
                    yield
                for t in range(B):
                    V.match_replace(taken[:, t, 0:W], top8[:, t, :], score[:, t, 0:W], 3e38).then_inc(f["route"], 1)
                    done[0] += 1
                dve.wait_ge(f["route"], done[0])
                link(V.tensor_tensor(a0, tk, sc, ALU.not_equal))
                total, inv = r1[0][:, :, 0:1], r1[1][:, :, 0:1]
                if l == 0:
                    V.memset(pick_bf[:, B, :], 0.0).then_inc(TS["pick"], 1)
                    V.tensor_copy(pick_bf[:, 0:B, :], a0).then_inc(TS["pick"], 1)
                    dve.wait_ge(TS["rank"], 1)
                    V.tensor_copy(rank_sb[:], bank[7][:, 256:256 + (B + 1) * E]).then_inc(TS["pick"], 1)
                    link(V.tensor_scalar(a1, a0, -1.0, 1e30, ALU.add, ALU.mult))
                    link(V.tensor_tensor(a1, a1, lg, ALU.add))
                    link(V.reduce_max(r1[2][:, :, 0:1], a1, AX.X))
                    V.tensor_tensor(a1, a1, r1[2][:, :, 0:1].to_broadcast([P, B, E]),
                                    ALU.subtract).then_inc(RT["rfun_in"], 1)
                    dve.wait_ge(TS["pick"], 3)
                    yield
                    sort_tokens(V, link, a0)
                    tiles_experts(V, link)
                    yield
                    dve.wait_ge(RT["rfun"], l + 1)
                else:
                    yield
                link(V.tensor_tensor(a1, a1, a0, ALU.mult))
                link(V.tensor_reduce(total, a1, AX.X, ALU.add))
                if l == 1:
                    link(V.tensor_scalar(total, total, 1e-20, None, ALU.add))
                link(V.reciprocal(inv, total))
                link(V.tensor_tensor(a1, a1, inv.to_broadcast([P, B, E]), ALU.mult))
                if l == 0:
                    for r in range(2):
                        link(V.tensor_tensor(hit[:], pos1[:], pair_pos[:, r].unsqueeze(2).to_broadcast([P, B, E]),
                                             ALU.is_equal))
                        link(V.tensor_tensor(hit[:], hit[:], a1, ALU.mult))
                        link(V.tensor_reduce(place_w[:, r], hit[:], AX.X, ALU.add))
                    V.tensor_copy(w_idx[:], w_row[:]).then_inc(TS["idx"], 1)
                else:
                    link(V.tensor_scalar(gate[:, 2:E + 2, :], a1.rearrange("p b e -> p e b"), ROUTE_SCALE, None, ALU.mult))

            def sort_tokens(V, link, picked):
                E = E0
                step, ahead = sort_c[:, P:P + E], sort_c[:, P + E:P + E + E * E].rearrange("p (e f) -> p e f", e=E)
                ranks, total = rank_sb[:, 0:B * E].rearrange("p (b e) -> p b e", e=E), rank_sb[:, B * E:(B + 1) * E]
                count, base, end = ntile[:, 0], ntile[:, 1], ntile[:, 2]
                link(V.tensor_tensor(cmp_e[:], total.unsqueeze(2).to_broadcast([P, E, E]),
                                     step.unsqueeze(1).to_broadcast([P, E, E]), ALU.is_gt))
                link(V.tensor_reduce(count, cmp_e[:], AX.X, ALU.add))
                link(V.tensor_tensor(cmp_e[:], count.unsqueeze(1).to_broadcast([P, E, E]), ahead, ALU.mult))
                link(V.tensor_reduce(base, cmp_e[:], AX.X, ALU.add))
                link(V.tensor_tensor(end, base, count, ALU.add))
                link(V.scalar_tensor_tensor(out=pos[:], in0=base.unsqueeze(1).to_broadcast([P, B, E]),
                                            scalar=float(TILE), in1=ranks, op0=ALU.mult, op1=ALU.add))
                link(V.scalar_tensor_tensor(out=pos1[:], in0=pos[:], scalar=1.0, in1=picked, op0=ALU.add, op1=ALU.mult))
                link(V.reduce_max(pair_pos[:, 0], pos1[:], AX.X))
                link(V.tensor_reduce(pair_pos[:, 1], pos1[:], AX.X, ALU.add))
                link(V.tensor_tensor(pair_pos[:, 1], pair_pos[:, 1], pair_pos[:, 0], ALU.subtract))
                link(V.tensor_scalar(place[:], pair_pos[:], -1.0, None, ALU.add))

            def tiles_experts(V, link):
                E, end = E0, ntile[:, 2]
                tile_c = sort_c[:, P + E + E * E:P + E + E * E + TILES]
                lane = sort_c[:, P + E + E * E + TILES:P + E + E * E + TILES + 1]
                link(V.tensor_tensor(cmp_t[:], end.unsqueeze(1).to_broadcast([P, TILES, E]),
                                     tile_c.unsqueeze(2).to_broadcast([P, TILES, E]), ALU.is_le))
                link(V.tensor_reduce(of_tile[:], cmp_t[:], AX.X, ALU.add))
                link(V.tensor_scalar(of_tile[:], of_tile[:], float(E - 1), float(2 * P), ALU.min, ALU.mult))
                link(V.tensor_scalar(w_row[:, 0], of_tile[:], lane, None, ALU.add))
                link(V.tensor_scalar(w_row[:, 1], w_row[:, 0], float(P), None, ALU.add))

            def tile_weights_low(it, s):
                dve.wait_ge(TS["w_hi"], it * 4 + (s + 1))
                nc.vector.tensor_tensor(w_lo4[s][:], w_raw4[s], w_hi4[s][:].bitcast(F32),
                                        ALU.subtract).then_inc(TS["w_lo"], 1)

            def tile_rows_low(it, q):
                dve.wait_ge(TS["xhi"], it * 2 + (q + 1))
                nc.vector.tensor_tensor(xsT_lo[:, q].rearrange("p k t -> p (k t)"), bank[4][:],
                                        xsT_hi[:, q].rearrange("p k t -> p (k t)").bitcast(F32),
                                        ALU.subtract).then_inc(TS["xlo"], 1)

            def tile_step(it, s, ahead, more):
                dve.wait_ge(TS["act"], it * 4 + (s + 1))
                nc.vector.tensor_tensor(hid[:, s % 2, :], bank[2 * (s % 2)][:], act_sb[:, s % 2, :],
                                        ALU.mult).then_inc(TS["hid"], 1)
                if s % 2 == 0 and more:
                    tile_rows_low(it + s // 2, 1 - s // 2)
                dve.wait_ge(TS["hhi"], it * 4 + (s + 1))
                nc.vector.tensor_tensor(hid_lo[:, s % 2, 0, :], hid[:, s % 2, :],
                                        hid_hi[:, s % 2, 0, :].bitcast(F32),
                                        ALU.subtract).then_inc(TS["hlo"], 1)
                if ahead:
                    tile_weights_low(it + s // 2, (s + 2) % 4)

            def tiles_back(n):
                dve.wait_ge(s_x[n], 32)
                rows = xres[:, BLK * n:BLK * (n + 1), :]
                nc.vector.tensor_tensor(rows, xn_all[:, BLK * n:BLK * (n + 1), 0:D], rows, ALU.add).then_inc(TS["add"], 1)
                dve.wait_ge(TS["add"], n + 1)

            def acc(f, it, ls, subs, first):
                par, n = divmod(ls, NBLK)
                for sub in subs:
                    dve.wait_ge(f["y"], step_no(it, ls) * 2 + (sub // 2 + 1))
                    if not (first and ls < NBLK):
                        dve.wait_ge(f["acc"], (step_no(it, ls) - NBLK) * 4 + (sub + 1))
                    rows = xres[:, BLK * n + sub, :]
                    nc.vector.scalar_tensor_tensor(
                        out=rows, in0=bank[4 + 2 * (ls % 2) + sub // 2][:, D * (sub % 2):D * (sub % 2 + 1)],
                        scalar=gate[:, ds(it * 2 + par, 1), BLK * n + sub] if not isinstance(it, int)
                        else gate[:, it * 2 + par, BLK * n + sub:BLK * n + sub + 1],
                        in1=rows, op0=ALU.mult, op1=ALU.add).then_inc(f["acc"], 1)

            def experts(f, J, it, first, between=None):
                for ls in range(STEPS):
                    if between:
                        between(ls)
                    for j in range(J):
                        t, r = tile_no(it, ls, j, J), (ls * J + j) % 2
                        dve.wait_ge(f["act"], t + 1)
                        nc.vector.tensor_tensor(hid[:, r, :], bank[2 * r][:], act_sb[:, r, :],
                                                ALU.mult).then_inc(f["hid"], 1)
                        subs = range(2 * j, 2 * j + 2) if J == 2 else range(BLK)
                        if ls >= 2:
                            acc(f, it, ls - 2, subs, first)
                        elif not first:
                            acc(f, it - 1, ls - 2 + STEPS, subs, False)
                        dve.wait_ge(f["hhi"], t + 1)
                        nc.vector.tensor_tensor(hid_lo[:, ls % 2, j, :], hid[:, r, :],
                                                hid_hi[:, ls % 2, j, :].bitcast(F32),
                                                ALU.subtract).then_inc(f["hlo"], 1)

            def first_constants():
                dve.wait_ge(s_in, 16 * 9)
                dve.wait_ge(s_set, 4)
                nc.vector.tensor_scalar(mask_b[0:1, :], mask_f, 1.0, -BIG, ALU.not_equal, ALU.mult).then_inc(s_vset, 1)
                nc.vector.tensor_scalar(bias_col[1][:, 2:4], bias_col[1][:, 2:4], 0.25, None, ALU.mult).then_inc(s_vset, 1)

            for l in range(2):
                a, f, J = AT[l], FF[l], JT[l]

                def weights_low(steps):
                    for i in steps:
                        w = W_ORDER[l][i]
                        dve.wait_ge(a["aw_hi"], i + 1)
                        nc.vector.tensor_tensor(aw_lo[:, w].rearrange("p k d -> p (k d)"), aw_raw[:, i % 2, :],
                                                aw_hi[:, w].rearrange("p k d -> p (k d)").bitcast(F32),
                                                ALU.subtract).then_inc(a["aw_lo"], 1)

                def unit_build(m, i):
                    r = i % 2
                    if l == 0:
                        dve.wait_ge(a["proj"], m * 4 + (i + 1))
                        if i >= 2:
                            dve.wait_ge(a["qklo"], m * 4 + (i - 1))
                        for c, dst in enumerate((qk, rope_b)):
                            nc.vector.scalar_tensor_tensor(
                                out=dst[:, r].rearrange("p (b s) -> p b s", b=BLK),
                                in0=bank[2 * r + c][:].rearrange("p (b s) -> p b s", b=BLK),
                                scalar=bias_col[l][:, 4 * c + i:4 * c + i + 1],
                                in1=rope_tab[:, i // 2, c].unsqueeze(1).to_broadcast([P, BLK, S]),
                                op0=ALU.add, op1=ALU.mult).then_inc(s_rope, 1)

                def unit_low(m, i):
                    r, dst = i % 2, k_parts if i < 2 else q_parts
                    dve.wait_ge(a["qkhi"], m * 4 + (i + 1))
                    nc.vector.tensor_tensor(dst[:, 1, r, :], qk[:, r, :], dst[:, 0, r, :].bitcast(F32),
                                            ALU.subtract).then_inc(a["qklo"], 1)

                def values(m):
                    for h in range(2):
                        dve.wait_ge(a["vps"], m * 2 + (h + 1))
                        nc.vector.tensor_tensor(v32[:, h], bank[h][:].rearrange("p (b d) -> p b d", b=2),
                                                bv_row[l][:].unsqueeze(1).to_broadcast([P, 2, D]),
                                                ALU.add).then_inc(a["v32"], 1)

                def shifted(n, i):
                    b, g = divmod(i, NG)
                    dve.wait_ge(a["score"], n * GROUPS + (i + 1))
                    grp = bank[g][:].rearrange("p (h t) -> p h t", h=GRP)
                    mx = nmax[:, b % 2, GRP * g:GRP * (g + 1)]
                    nc.vector.tensor_reduce(mx, grp, AX.X, ALU.max, negate=True).then_inc(a["max"], 1)
                    if g % 2 == 0:
                        dve.wait_ge(a["max"], n * GROUPS + (i + 1))
                        nc.vector.tensor_tensor(prob[:, i % RING, :].rearrange("p (h t) -> p h t", h=GRP), grp,
                                                mx.unsqueeze(2).to_broadcast([P, GRP, S]),
                                                ALU.add).then_inc(a["sub"], 1)

                def denominators(n, c):
                    dve.wait_ge(a["ocopy"], n * 8 + (c + 1))
                    nc.vector.reciprocal(rden[:, c % 2, :], o_raw[:, c % 2, :, HD]).then_inc(a["rden"], 1)

                def last_outputs(n):
                    raw, dst = o_raw[:, 1], o_sb[:, BLK - 1, 8:16, :]
                    nc.vector.tensor_tensor(dst, raw[:, :, 0:16], raw[:, :, 18:34], ALU.add).then_inc(a["olast"], 1)
                    dve.wait_ge(a["olast"], n * 2 + 1)
                    nc.vector.tensor_tensor(dst, dst, raw[:, :, 34:50], ALU.add).then_inc(a["olast"], 1)
                    dve.wait_ge(a["olast"], n * 2 + 2)
                    dve.wait_ge(a["rden"], n * 8 + 8)
                    nc.vector.tensor_tensor(dst, dst, rden[:, 1].unsqueeze(2).to_broadcast([P, 8, HD]),
                                            ALU.mult).then_inc(a["o"], 1)

                def attend(n, build):
                    for i in range(GROUPS):
                        if i + NG < GROUPS:
                            shifted(n, i + NG)
                        elif build:
                            unit_build(n + 1, i % NG)
                        dve.wait_ge(a["phi"], n * GROUPS + (i + 1))
                        nc.vector.tensor_tensor(probT_lo[:, i % RINGT, :], bank[4 + i % 2][:],
                                                probT_hi[:, i % RINGT, :], ALU.subtract).then_inc(a["plo"], 1)
                        if i >= 5 and i % 2 == 1:
                            denominators(n, (i - 5) // 2)
                        if i + NG >= GROUPS and build:
                            unit_low(n + 1, i % NG)
                    denominators(n, 6)
                    denominators(n, 7)
                    last_outputs(n)
                    if build:
                        values(n + 1)
                    for k in range(KT):
                        dve.wait_ge(a["ohi"], n * 2 + (k + 1))
                        nc.vector.tensor_tensor(oT_lo[:, k, :], bank[4 + k][:], oT_hi[:, k, :].bitcast(F32),
                                                ALU.subtract).then_inc(a["olo"], 1)
                    if build:
                        for g in range(NG):
                            shifted(n + 1, g)
                    dve.wait_ge(a["xbo"], n + 1)
                    for h in range(2):
                        dve.wait_ge(a["wo"], n * 2 + (h + 1))
                        rows = xres[:, ds(n * BLK + 2 * h, 2), :] if not isinstance(n, int) else \
                            xres[:, n * BLK + 2 * h:n * BLK + 2 * h + 2, :]
                        nc.vector.tensor_tensor(rows, bank[6 + h][:].rearrange("p (b d) -> p b d", b=2), rows,
                                                ALU.add).then_inc(a["xadd"], 1)

                if l == 0:
                    ln_dve(0, lambda n: dve.wait_ge(s_x[n], 16))
                    weights_low(range(4))
                    dve.wait_ge(s_first, 16 * 3)
                    for i in range(4):
                        unit_build(0, i)
                        unit_low(0, i)
                        if i == 0:
                            weights_low(range(4, NW[0]))
                    values(0)
                    first_constants()
                else:
                    dve.wait_ge(a["ctx_hi"], 1)
                    nc.vector.tensor_tensor(ctx_lo[:], ctx_raw[:], ctx_hi[:].bitcast(F32),
                                            ALU.subtract).then_inc(a["ctx_lo"], 1)
                    weights_low(range(KV_WEIGHTS))
                    ln_dve(2, tiles_back)
                    weights_low(range(KV_WEIGHTS, NW[1]))
                    for i in range(4):
                        unit_build(0, i)
                        unit_low(0, i)
                    values(0)
                for g in range(NG):
                    shifted(0, g)
                with dve.Fori(0, NBLK - 1) as n:
                    attend(n, True)
                attend(NBLK - 1, False)
                ln_dve(2 * l + 1, lambda n: dve.wait_ge(a["xadd"], 2 * n + 2))
                dve.wait_ge(RT["rturn"], NBLK * (l + 1))
                parts = route(l, f)
                next(parts)

                def between(ls):
                    if ls >= 1:
                        next(parts, None)
                    if l == 0 and ls >= STEPS - 2:
                        tile_weights_low(0, ls - (STEPS - 2))

                if l == 0:
                    experts(f, J, 0, True, between)
                    for ls in range(STEPS - 2, STEPS):
                        acc(f, 0, ls, range(BLK), False)
                    dve.wait_ge(f["acc"], STEPS * BLK)
                    tile_rows_low(0, 0)
                    for s in range(4):
                        tile_step(0, s, True, True)
                    with dve.Fori(0, PAIRS - 2) as pair:
                        for s in range(4):
                            tile_step(pair + 1, s, True, True)
                    left = TILES % 2
                    for s in range(4):
                        tile_step(PAIRS - 1, s, s < 2 or left, s == 0 or left)
                    if left:
                        for s in range(2):
                            tile_step(PAIRS, s, False, False)
                    continue
                experts(f, J, 0, True, between)
                with dve.Fori(1, HALF) as it:
                    experts(f, J, it, False)
                for ls in range(STEPS - 2, STEPS):
                    acc(f, HALF - 1, ls, range(BLK), False)

        @block.tensor
        def _(pe):
            def ln_pe(m, xn_of=lambda n, t: xn[:, n % 2, t, :], then=lambda n: None):
                for n in range(NBLK):
                    pe.wait_ge(LN["ln_xn"], 4 * (NBLK * m + n) + 4)
                    if n >= 2:
                        pe.wait_ge(LN["ln_lo"], 2 * (NBLK * m + n) - 2)
                    for k in range(KT):
                        for t in range(BLK):
                            last = nc.tensor.transpose(bank[ln_bank(m, n, k)][:, P * t:P * (t + 1)],
                                                       xn_of(n, t)[:, P * k:P * (k + 1)], ident[:])
                        last.then_inc(LN["ln_T"], 1)
                    if n >= 1:
                        then(n - 1)
                then(NBLK - 1)

            def products(dst, left, right, finish=True):
                pairs = [(lh, rh) for k in range(KT)
                         for lh, rh in ((left[0](k), right[0](k)), (left[1](k), right[0](k)),
                                        (left[0](k), right[1](k)))]
                for i, (lh, rh) in enumerate(pairs):
                    last = nc.tensor.matmul(dst, lh, rh, start=(i == 0), stop=(i == len(pairs) - 1))
                return last

            def up(l, f, J, it, ls, first):
                par, n = divmod(ls, NBLK)
                if n == 0:
                    pe.wait_ge(f["w_lo"], it * 2 + (par + 1))
                for j in range(J):
                    r = (ls * J + j) % 2
                    if not (first and ls * J + j < 2):
                        pe.wait_ge(f["hid"], tile_no(it, ls, j, J) - 1)
                    for c in range(2):
                        def w(part):
                            return lambda k: part[par][:, (c * KT + k) * P * J + P * j:(c * KT + k) * P * J + P * (j + 1)]
                        cols = slice(N * n, N * (n + 1))
                        last = products(bank[2 * r + c][:], (w(w_hi), w(w_lo)),
                                        (lambda k: xT_hi[:, k, cols], lambda k: xT_lo[:, k, cols]))
                    last.then_inc(f["up"], 1)

            def down(f, J, it, ls, first):
                par = ls // NBLK
                pe.wait_ge(f["hlo"], tile_no(it, ls, J, J))
                if not (first and ls < 2):
                    pe.wait_ge(f["acc"], (step_no(it, ls) - 1) * 4)
                for sub in range(BLK):
                    rows = slice(P * sub, P * (sub + 1))
                    pairs = []
                    for j in range(J):
                        cols = slice(4 * P * J + D * j, 4 * P * J + D * (j + 1))
                        hh, hl = hid_hi[:, ls % 2, j, rows], hid_lo[:, ls % 2, j, rows]
                        wh, wl = w_hi[par][:, cols], w_lo[par][:, cols]
                        pairs += [(hh, wh), (hl, wh), (hh, wl)]
                    dst = bank[4 + 2 * (ls % 2) + sub // 2][:, D * (sub % 2):D * (sub % 2 + 1)]
                    for i, (h, w) in enumerate(pairs):
                        last = nc.tensor.matmul(dst, h, w, start=(i == 0), stop=(i == len(pairs) - 1))
                    if sub % 2:
                        last.then_inc(f["y"], 1)

            def ranks():
                pe.wait_ge(TS["const"], 2)
                pe.wait_ge(TS["pick"], 2)
                dst = bank[7][:, 256:256 + (B + 1) * E0]
                nc.tensor.matmul(dst, before_bf[:], pick_bf[:].rearrange("p b e -> p (b e)"), start=True, stop=False)
                for b in range(B):
                    last = nc.tensor.matmul(dst.rearrange("p (b e) -> p b e", e=E0)[:, b + 1:B + 1, :], ones_bf[:],
                                            pick_bf[:, b, :].unsqueeze(1).to_broadcast([P, B - b, E0]),
                                            start=False, stop=(b == B - 1))
                last.then_inc(TS["rank"], 1)

            def tile_turn(it, q):
                pe.wait_ge(TS[f"x_in{q}"], it * 16 + 16)
                pe.wait_ge(TS["tlabel"], it * 4 + (3 + 2 * q + 2))
                if not (isinstance(it, int) and it == 0 and q == 0):
                    pe.wait_ge(TS["xlo"], it * 2 + q)
                for k in range(KT):
                    for c in range(2):
                        last = nc.tensor.transpose(bank[4][:, TILE * k + P * c:TILE * k + P * (c + 1)],
                                                   xs[:, q, c, P * k:P * (k + 1)], ident[:])
                last.then_inc(TS["xT"], 1)

            def tile_up(it, s, first):
                q = s // 2
                if s % 2 == 0:
                    pe.wait_ge(TS["xlo"], it * 2 + (q + 1))
                pe.wait_ge(TS["w_lo"], it * 4 + (s + 1))
                if not (first and s < 2):
                    pe.wait_ge(TS["hid"], it * 4 + (s - 1))
                for c in range(2):
                    for j in range(2):
                        def w(part):
                            return lambda k: part[s][:, (c * KT + k) * 2 * P + P * j:(c * KT + k) * 2 * P + P * (j + 1)]
                        last = products(bank[2 * (s % 2) + c][:, TILE * j:TILE * (j + 1)], (w(w_hi4), w(w_lo4)),
                                        (lambda k: xsT_hi[:, q, k, :], lambda k: xsT_lo[:, q, k, :]))
                last.then_inc(TS["up"], 1)

            def tile_down(it, s, first):
                q, h = divmod(s, 2)
                pe.wait_ge(TS["hlo"], it * 4 + (s + 1))
                if h == 0 and not first:
                    pe.wait_ge(TS["ycopy"], it * 2 + (q - 1))
                todo = []
                for c in range(2):
                    for j in range(2):
                        hh, hl = (p[:, s % 2, 0, TILE * j + P * c:TILE * j + P * (c + 1)] for p in (hid_hi, hid_lo))
                        wh, wl = (p[s][:, 4 * 2 * P + D * j:4 * 2 * P + D * (j + 1)] for p in (w_hi4, w_lo4))
                        todo += [(c, hh, wh), (c, hl, wh), (c, hh, wl)]
                for i, (c, left, right) in enumerate(todo):
                    last = nc.tensor.matmul(bank[5 + q][:, D * c:D * (c + 1)], left, right,
                                            start=(h == 0 and i == 0), stop=(h == 1 and i == len(todo) - 1))
                last.then_inc(TS["down"], 1)

            def tile_step(it, s, turn, ahead, first):
                if s % 2 == 0 and turn:
                    tile_turn(it + s // 2, 1 - s // 2)
                if ahead:
                    tile_up(it + (s + 1) // 4, (s + 1) % 4, first and s < 3)
                tile_down(it, s, first)

            def experts(l, f, J, it, first, final):
                for ls in range(STEPS):
                    if ls + 1 < STEPS:
                        up(l, f, J, it, ls + 1, first)
                    elif not final:
                        up(l, f, J, it + 1, 0, False)
                    down(f, J, it, ls, first)

            for l in range(2):
                a, f, J = AT[l], FF[l], JT[l]

                def block_cols(n):
                    return slice(n * N, n * N + N) if isinstance(n, int) else ds(n * N, N)

                def unit(m, i, first):
                    if i == 0:
                        pe.wait_ge(a["ctx_lo"], m + 1)
                    if i >= 2:
                        pe.wait_ge(a["qk"], m * 4 + (i - 1))
                    elif not first:
                        pe.wait_ge(a["exp"], (m - 1) * GROUPS + (14 + 2 * i))
                    for c, w in enumerate(UNIT_W[l][i]):
                        def wt(part):
                            return lambda k: part[:, w, k, P * (i % 2):P * (i % 2 + 1)]
                        if i < 2:
                            right = (lambda k: ctx_hi[:, k, :], lambda k: ctx_lo[:, k, :])
                        else:
                            right = (lambda k: xT_hi[:, k, block_cols(m)], lambda k: xT_lo[:, k, block_cols(m)])
                        last = products(bank[2 * (i % 2) + c][:], (wt(aw_hi), wt(aw_lo)), right)
                    last.then_inc(a["proj"], 1)

                def values(m):
                    pe.wait_ge(a["qk"], m * 4 + 3)
                    for b in range(BLK):
                        rows = slice(P * b, P * (b + 1))
                        last = products(bank[b // 2][:, D * (b % 2):D * (b % 2 + 1)],
                                        (lambda k: ctx_hi[:, k, rows], lambda k: ctx_lo[:, k, rows]),
                                        (lambda k: aw_hi[:, V_W[l], k, :], lambda k: aw_lo[:, V_W[l], k, :]))
                        if b % 2:
                            last.then_inc(a["vps"], 1)

                def scores(n, i):
                    b, g = divmod(i, NG)
                    if i == 0:
                        pe.wait_ge(a["qklo"], n * 4 + 4)
                        pe.wait_ge(a["v32"], n * 2 + 2)
                    if b >= 1 and g % 2 == 0:
                        pe.wait_ge(a["sub"], n * 8 + (i - NG) // 2 + 1)
                    elif b >= 1:
                        pe.wait_ge(a["exp"], n * GROUPS + (i - NG + 1))
                    if g == 0:
                        pe.wait_ge(a[f"kdma{b % 2}"], n * 256 + (b // 2 + 1) * 128)
                    q = [q_parts[:, part, g // 2, S * b:S * (b + 1)] for part in range(2)]
                    k = [kexp[b % 2][:, part, g].rearrange("p h t -> p (h t)") for part in range(2)]
                    nc.tensor.matmul(bank[g][:], q[0], k[0], start=True, stop=False)
                    nc.tensor.matmul(bank[g][:], q[1], k[0], start=False, stop=False)
                    last = nc.tensor.matmul(bank[g][:], q[0], k[1], start=False, stop=(l == 0))
                    if l == 1:
                        cols = ds((n * BLK + b) * S, S) if not isinstance(n, int) else \
                            slice((n * BLK + b) * S, (n * BLK + b + 1) * S)
                        row = mask_b[:, cols].unsqueeze(1).to_broadcast([P, GRP, S])
                        last = nc.tensor.matmul(bank[g][:].rearrange("p (h t) -> p h t", h=GRP), first_row[:], row,
                                                start=False, stop=True)
                    last.then_inc(a["score"], 1)

                def turned(n, i):
                    pe.wait_ge(a["exp"], n * GROUPS + (i + 1))
                    if i >= 2:
                        pe.wait_ge(a["plo"], n * GROUPS + (i - 1))
                    for h in range(GRP):
                        last = nc.tensor.transpose(bank[4 + i % 2][:, S * h:S * (h + 1)],
                                                   prob[:, i % RING, S * h:S * (h + 1)], ident[:])
                    last.then_inc(a["pT"], 1)

                def weighed(n, i):
                    b, g = divmod(i, NG)
                    pe.wait_ge(a["plo"], n * GROUPS + (i + 1))
                    if i == 0:
                        pe.wait_ge(a["vlo"], n * 2 + 2)
                    if b >= 1 and g % 2 == 0:
                        pe.wait_ge(a["ocopy"], n * 8 + (2 * b - 2 + g // 2 + 1))
                    for h in range(GRP):
                        at_col = VW * (GRP * (g % 2) + h)
                        for part, p in enumerate((probT_hi, probT_lo)):
                            last = nc.tensor.matmul(bank[6 + g // 2][:, at_col:at_col + VW],
                                                    p[:, i % RINGT, S * h:S * (h + 1)],
                                                    v_parts[:, b, GRP * g + h, :], start=(part == 0), stop=(part == 1))
                    last.then_inc(a["pv"], 1)

                def attend(n, build):
                    for i in range(GROUPS):
                        if i + NG < GROUPS:
                            scores(n, i + NG)
                        elif build:
                            unit(n + 1, i % NG, False)
                        turned(n, i)
                        if i >= 2:
                            weighed(n, i - 2)
                    weighed(n, GROUPS - 2)
                    weighed(n, GROUPS - 1)
                    if build:
                        values(n + 1)
                    pe.wait_ge(a["plo"], n * GROUPS + GROUPS)
                    pe.wait_ge(a["o"], n * 8 + 8)
                    for k in range(KT):
                        for b in range(BLK):
                            src = o_sb[:, b, 8 * k:8 * (k + 1), :].rearrange("p h d -> p (h d)")
                            last = nc.tensor.transpose(bank[4 + k][:, P * b:P * (b + 1)], src, ident[:])
                        last.then_inc(a["oT"], 1)
                    if build:
                        for g in range(NG):
                            scores(n + 1, g)
                    pe.wait_ge(a["olo"], n * 2 + 2)
                    for b in range(BLK):
                        rows = slice(P * b, P * (b + 1))
                        last = products(bank[6 + b // 2][:, D * (b % 2):D * (b % 2 + 1)],
                                        (lambda k: oT_hi[:, k, rows], lambda k: oT_lo[:, k, rows]),
                                        (lambda k: aw_hi[:, O_W[l], k, :], lambda k: aw_lo[:, O_W[l], k, :]))
                        if b % 2:
                            last.then_inc(a["wo"], 1)

                if l == 0:
                    pe.wait_ge(s_ident, 16)
                    ln_pe(0)
                    pe.wait_ge(LN["ln_lo"], 2 * NBLK)
                    for i in range(4):
                        pe.wait_ge(a["aw_lo"], 4 if i >= 2 else 2)
                        unit(0, i, True)
                    pe.wait_ge(a["aw_lo"], NW[0])
                    values(0)
                else:
                    pe.wait_ge(a["aw_lo"], KV_WEIGHTS)
                    unit(0, 0, True)
                    unit(0, 1, True)
                    ln_pe(2)
                    pe.wait_ge(LN["ln_lo"], 2 * NBLK * 3)
                    pe.wait_ge(a["aw_lo"], NW[1])
                    unit(0, 2, True)
                    unit(0, 3, True)
                    values(0)
                if l == 1:
                    pe.wait_ge(s_vset, 2)
                pe.wait_ge(s_set, 5)
                for g in range(NG):
                    scores(0, g)
                with pe.Fori(0, NBLK - 1) as n:
                    attend(n, True)
                attend(NBLK - 1, False)
                E = NE[l]

                def router_products(n):
                    pe.wait_ge(LN["ln_lo"], 2 * (NBLK * (2 * l + 1) + n + 1))
                    if n == 0:
                        pe.wait_ge(s_wsplit[l], 2)
                    if n >= 2:
                        pe.wait_ge(RT["rT"], NBLK * l + n - 1)
                    pairs = [(p[:, k, N * n:N * (n + 1)], k) for k in range(KT) for p in (xT_hi, xT_lo)]
                    for i, (p, k) in enumerate(pairs):
                        last = nc.tensor.matmul(bank[4 + n % 2][0:2 * E, :], route_wr[l][:, k].rearrange("p c e -> p (c e)"),
                                                p, start=(i == 0), stop=(i == len(pairs) - 1))
                    last.then_inc(RT["rprod"], 1)

                def router_turn(n):
                    pe.wait_ge(RT["rT"], NBLK * l + n + 1)
                    for t in range(BLK):
                        at_col = 2 * E * (BLK * n + t)
                        last = nc.tensor.transpose(bank[7][:, at_col:at_col + 2 * E],
                                                   act_sb[0:2 * E, n % 2, P * t:P * (t + 1)], ident[0:2 * E, 0:2 * E])
                    last.then_inc(RT["rturn"], 1)

                def router(n):
                    router_products(n)
                    if n >= 1:
                        router_turn(n - 1)
                    if n == NBLK - 1:
                        router_turn(n)

                ln_pe(2 * l + 1, (lambda n, t: xn[:, n % 2, t, :]) if l else (lambda n, t: xn_all[:, BLK * n + t, 0:D]),
                      router)
                up(l, f, J, 0, 0, True)
                if l == 0:
                    ranks()
                    pe.wait_ge(TS["pick"], 3)
                    experts(l, f, J, 0, True, True)
                    pe.wait_ge(f["acc"], STEPS * BLK)
                    tile_turn(0, 0)
                    tile_up(0, 0, True)
                    for s in range(4):
                        tile_step(0, s, True, True, True)
                    with pe.Fori(0, PAIRS - 2) as pair:
                        for s in range(4):
                            tile_step(pair + 1, s, True, True, False)
                    left = TILES % 2
                    for s in range(4):
                        tile_step(PAIRS - 1, s, s == 0 or left, s < 3 or left, False)
                    if left:
                        tile_step(PAIRS, 0, False, True, False)
                        tile_step(PAIRS, 1, False, False, False)
                    continue
                pe.wait_ge(RT["rfun"], 2)
                experts(l, f, J, 0, True, False)
                with pe.Fori(1, HALF - 1) as it:
                    experts(l, f, J, it, False, False)
                experts(l, f, J, HALF - 1, False, True)



def kernel(**inputs):
    import concourse.bacc as bacc
    from concourse import mybir as _mybir
    from concourse.bass_utils import run_bass_kernel_spmd

    a = {k: np.asarray(v) for k, v in inputs.items()}

    def tiles(w):
        return w.reshape(w.shape[0] // P, P, w.shape[1]).transpose(1, 0, 2)

    def flat(w):
        t = tiles(w)
        return t.reshape(P, -1)

    partner = np.arange(D) ^ 1
    arrays = {"x": a["x"]}
    arrays["ctxT"] = tiles(a["ctx_1024"].reshape(TOK, D).T)
    arrays["maskrow"] = a["mask_BxS2_ff1"].reshape(1, TOK)
    freq = 1.0 / 10000.0 ** (np.arange(0, HD, 2, dtype=np.float32) / HD)
    angle = (np.arange(S, dtype=np.float32)[:, None] * freq[None, :].astype(np.float32)).astype(np.float32)
    row = np.arange(P) % HD
    sign = np.where(row % 2 == 0, -1.0, 1.0).astype(np.float32)
    cos, sin = np.cos(angle).T[row // 2], np.sin(angle).T[row // 2] * sign[:, None]
    arrays["tab"] = np.stack([cos, sin, cos * np.float32(0.25), sin * np.float32(0.25)],
                             axis=1).reshape(P, 2, 2, S)
    arrays["ident"] = np.eye(P, dtype=np.float32)
    for l in range(2):
        w = {n: a[f"L{l}_xattn_W{n}"].T for n in "qkvo"}
        b = {n: a[f"L{l}_xattn_b{n}"] for n in "qkvo"}
        ws = [w["q"], w["q"][:, partner], w["k"], w["k"][:, partner], w["v"], w["o"]] if l == 0 else \
            [w[n] for n in "qkvo"]
        arrays[f"aw{l}"] = np.stack([flat(v) for v in ws], axis=1)
        cols = [b["k"], b["q"], b["k"][partner], b["q"][partner]]
        arrays[f"ab{l}"] = np.concatenate([c.reshape(KT, P).T for c in cols], axis=1)
        arrays[f"arow{l}"] = np.stack([b["v"], b["o"]])
    ahead = np.triu(np.ones((P, P), np.float32), 1)
    rows = [np.arange(E0) * TILE, (np.arange(E0)[None, :] < np.arange(E0)[:, None]).reshape(-1), np.arange(TILES)]
    arrays["sort"] = np.concatenate([ahead, np.tile(np.concatenate(rows).astype(np.float32), (P, 1)),
                                     np.arange(P, dtype=np.float32)[:, None],
                                     1 + np.arange(TOK, dtype=np.float32).reshape(B, P).T], axis=1)
    arrays["empty"] = np.zeros((P, 2, XW), np.float32)
    arrays["empty"][:, :, D] = 1 + TOK + np.arange(TILE).reshape(2, P).T
    arrays["rw0"] = tiles(a["L0_ffn_Wr"])
    arrays["rw1"] = tiles(a["L1_ffn_router_weight"].T)
    arrays["rrow0"] = a["L0_ffn_rb"].reshape(1, E0)
    arrays["rrow1"] = a["L1_ffn_e_bias"].reshape(1, E1)

    def unit(linear, gated, out):
        return np.concatenate([flat(linear), flat(gated), flat(out)], axis=1)

    W1 = list(a["L0_ffn_W1"]) + [a["L0_ffn_Ws1"]]
    W2 = list(a["L0_ffn_W2"]) + [a["L0_ffn_Ws2"]]
    W3 = list(a["L0_ffn_W3"]) + [a["L0_ffn_Ws3"]]
    arrays["fw0"] = np.stack([unit(W1[u // 2][:, h], W3[u // 2][:, h], W2[u // 2][h, :])
                              for u in range(UNITS) for h in (slice(256 * (u % 2), 256 * (u % 2) + 256),)])
    parts = []
    for h in (slice(0, P), slice(P, 2 * P)):
        parts.append((a["L1_ffn_sh_up_w"][h], a["L1_ffn_sh_gate_w"][h], a["L1_ffn_sh_down_w"][:, h]))
    parts += [(a["L1_ffn_up_w"][e], a["L1_ffn_gate_w"][e], a["L1_ffn_down_w"][e]) for e in range(E1)]
    arrays["fw1"] = np.stack([unit(u.T, g.T, d.T) for u, g, d in parts])

    nc = bacc.Bacc("TRN2", target_bir_lowering=False, num_devices=1)
    arrays = {f"in_{k}": np.ascontiguousarray(v) for k, v in arrays.items()}
    ap = {k[3:]: nc.dram_tensor(k, v.shape, _mybir.dt.from_np(v.dtype), kind="ExternalInput").ap()
          for k, v in arrays.items()}
    out = nc.dram_tensor("out_x", (B, S, D), _mybir.dt.float32, kind="ExternalOutput").ap()
    sorted_x = nc.dram_tensor("sorted_x", (TILES * TILE, XW), _mybir.dt.float32, kind="Internal").ap()
    summed = nc.dram_tensor("summed", (1 + TOK + TILE, D), _mybir.dt.float32, kind="Internal").ap()
    program(nc, ap["x"], ap["ctxT"], ap["maskrow"], ap["tab"], ap["ident"],
            [ap["aw0"], ap["aw1"]], [ap["ab0"], ap["ab1"]], [ap["arow0"], ap["arow1"]],
            [ap["rw0"], ap["rw1"]], [ap["rrow0"], ap["rrow1"]], [ap["fw0"], ap["fw1"]], ap["sort"], ap["empty"], sorted_x, summed, out)
    r = run_bass_kernel_spmd(nc, [arrays], core_ids=[0])
    return r.results[0]["out_x"]
```
